# Optimizing a Trainium2 kernel written in Bass

```python
import numpy as np
import jax
import jax.numpy as jnp

def _softmax(x, axis=-1):
    return jax.nn.softmax(x, axis=axis)

def _gelu(x):
    return jax.nn.gelu(x, approximate=True)

def _silu(x):
    return jax.nn.silu(x)

def _sigmoid(x):
    return jax.nn.sigmoid(x)

def _layernorm(x, axis=-1, eps=1e-05):
    m = jnp.mean(x, axis=axis, keepdims=True)
    v = jnp.var(x, axis=axis, keepdims=True)
    return (x - m) / jnp.sqrt(v + eps)

def _scatter_add(tgt, idx, src, axis=0):
    return tgt.at[idx].add(src)

def _segment_sum(src, seg, n):
    return jax.ops.segment_sum(src, seg, n)
kernel_name = 'mk_lm_tower_d1_tok_ids256_r4_a0cb89'

def setup_inputs(seed: int=0):
    np.random.seed(seed)
    _w = jnp.asarray

    def _rec_inputs():
        import jax
        import jax.numpy as jnp
        _rk = jax.random.key(seed)
        x = jax.random.randint(jax.random.fold_in(_rk, 1), (8, 512), 0, 64, jnp.int32)
        return x
    x = _rec_inputs()

    def _L0_tok_setup():
        import jax, jax.numpy as jnp
        import numpy as np
        D_MODEL = 128
        N_LAYERS = 4
        VOCAB = 64
        SEQ = 512
        BATCH = 8
        EPS = 1e-05

        def _ln(x, g, b):
            mu = jnp.mean(x, axis=-1, keepdims=True)
            var = jnp.mean(jnp.square(x - mu), axis=-1, keepdims=True)
            return (x - mu) * jax.lax.rsqrt(var + EPS) * g + b

        def _fast_memory(x, mask, W_upd, b_upd, W_f, b_f, decay_param):
            decay = jax.nn.sigmoid(decay_param[0])
            u = jnp.einsum('bsd,de->bse', x, W_upd) + b_upd
            u_t = jnp.swapaxes(u, 0, 1)
            m_t = jnp.swapaxes(mask, 0, 1)[..., None]

            def step(mem, inp):
                u_i, msk = inp
                new = decay * mem + u_i
                mem = msk * new + (1.0 - msk) * mem
                return (mem, mem)
            mem0 = jnp.zeros((x.shape[0], x.shape[2]), x.dtype)
            _, mems = jax.lax.scan(step, mem0, (u_t, m_t))
            mems = jnp.swapaxes(mems, 0, 1)
            return jnp.einsum('bsd,de->bse', mems, W_f) + b_f
        key = jax.random.key(seed)
        ks = jax.random.split(key, 16)
        d, dff = (D_MODEL, 4 * D_MODEL)
        s = 0.02
        inp = {'tokens': jax.random.randint(ks[0], (BATCH, SEQ), 0, VOCAB, dtype=jnp.int64), 'emb': jax.random.normal(ks[1], (VOCAB, d), jnp.float32) * s, 'W_upd': jax.random.normal(ks[2], (d, d), jnp.float32) * s, 'b_upd': jnp.zeros((d,), jnp.float32), 'W_f': jax.random.normal(ks[3], (d, d), jnp.float32) * s, 'b_f': jnp.zeros((d,), jnp.float32), 'decay_param': jnp.zeros((1,), jnp.float32), 'norm_g': jnp.ones((d,), jnp.float32), 'norm_b': jnp.zeros((d,), jnp.float32), 'cms_ln_g': jnp.ones((N_LAYERS, d), jnp.float32), 'cms_ln_b': jnp.zeros((N_LAYERS, d), jnp.float32), 'cms_W1': jax.random.normal(ks[4], (N_LAYERS, d, dff), jnp.float32) * s, 'cms_b1': jnp.zeros((N_LAYERS, dff), jnp.float32), 'cms_W2': jax.random.normal(ks[5], (N_LAYERS, dff, d), jnp.float32) * s, 'cms_b2': jnp.zeros((N_LAYERS, d), jnp.float32), 'head_W': jax.random.normal(ks[6], (d, VOCAB), jnp.float32) * s, 'head_b': jnp.zeros((VOCAB,), jnp.float32)}
        return inp
    _L0_tok_all = _L0_tok_setup()
    _L0_tok_in = {k: v for k, v in _L0_tok_all.items() if k in ('emb', 'W_upd', 'b_upd', 'W_f', 'b_f', 'decay_param', 'norm_g', 'norm_b', 'cms_ln_g', 'cms_ln_b', 'cms_W1', 'cms_b1', 'cms_W2', 'cms_b2', 'head_W', 'head_b')}
    del _L0_tok_all

    def _L0_attn_setup():
        import jax, jax.numpy as jnp
        import numpy as np
        DIM = 64
        HEADS = 4
        DIM_HEAD = 32
        NUM_MEM = 4
        HIDDEN = HEADS * DIM_HEAD
        SCALE = DIM_HEAD ** (-0.5)

        def rmsnorm(x, g):
            n = jnp.linalg.norm(x, axis=-1, keepdims=True)
            return x / jnp.maximum(n, 1e-12) * g * x.shape[-1] ** 0.5
        key = jax.random.key(seed)
        ks = jax.random.split(key, 8)
        B, N = (4, 4096)
        return {'x': jax.random.normal(ks[0], (B, N, DIM), jnp.float32), 't': jax.random.normal(ks[1], (B,), jnp.float32), 'w_qkv': jax.random.normal(ks[2], (DIM, 3 * HIDDEN), jnp.float32) * 0.02, 'mem_kv': jax.random.normal(ks[3], (2, HEADS, DIM_HEAD, NUM_MEM), jnp.float32), 'w_out': jax.random.normal(ks[4], (HIDDEN, DIM), jnp.float32) * 0.02, 'b_out': jnp.zeros((DIM,), jnp.float32), 'g_out': jnp.ones((DIM,), jnp.float32), 'g_pre': jnp.ones((DIM,), jnp.float32)}
    _L0_attn_all = _L0_attn_setup()
    _L0_attn_in = {k: v for k, v in _L0_attn_all.items() if k in ('t', 'w_qkv', 'mem_kv', 'w_out', 'b_out', 'g_out', 'g_pre')}
    del _L0_attn_all

    def _L0_ffn_setup():
        import jax, jax.numpy as jnp
        import numpy as np
        E = 8
        K = 2
        D = 64
        H = 128
        DOUT = 64
        EPS = 1e-05
        key = jax.random.key(seed)
        ks = jax.random.split(key, 9)
        s = 0.02
        return {'x': jax.random.normal(ks[0], (4, 2048, D), jnp.float32), 'gamma': 1.0 + 0.05 * jax.random.normal(ks[1], (D,), jnp.float32), 'beta': 0.05 * jax.random.normal(ks[2], (D,), jnp.float32), 'Wr': 0.01 * jax.random.normal(ks[3], (D, E), jnp.float32), 'br': jnp.zeros((E,), jnp.float32), 'W1': s * jax.random.normal(ks[4], (E, D, H), jnp.float32), 'b1': s * jax.random.normal(ks[5], (E, H), jnp.float32), 'W2': s * jax.random.normal(ks[6], (E, H, DOUT), jnp.float32), 'b2': s * jax.random.normal(ks[7], (E, DOUT), jnp.float32)}
    _L0_ffn_all = _L0_ffn_setup()
    _L0_ffn_in = {k: v for k, v in _L0_ffn_all.items() if k in ('gamma', 'beta', 'Wr', 'br', 'W1', 'b1', 'W2', 'b2')}
    del _L0_ffn_all
    return {'x': x, 'L0_tok_emb': _L0_tok_in['emb'], 'L0_tok_W_upd': _L0_tok_in['W_upd'], 'L0_tok_b_upd': _L0_tok_in['b_upd'], 'L0_tok_W_f': _L0_tok_in['W_f'], 'L0_tok_b_f': _L0_tok_in['b_f'], 'L0_tok_decay_param': _L0_tok_in['decay_param'], 'L0_tok_norm_g': _L0_tok_in['norm_g'], 'L0_tok_norm_b': _L0_tok_in['norm_b'], 'L0_tok_cms_ln_g': _L0_tok_in['cms_ln_g'], 'L0_tok_cms_ln_b': _L0_tok_in['cms_ln_b'], 'L0_tok_cms_W1': _L0_tok_in['cms_W1'], 'L0_tok_cms_b1': _L0_tok_in['cms_b1'], 'L0_tok_cms_W2': _L0_tok_in['cms_W2'], 'L0_tok_cms_b2': _L0_tok_in['cms_b2'], 'L0_tok_head_W': _L0_tok_in['head_W'], 'L0_tok_head_b': _L0_tok_in['head_b'], 'L0_attn_t': _L0_attn_in['t'], 'L0_attn_w_qkv': _L0_attn_in['w_qkv'], 'L0_attn_mem_kv': _L0_attn_in['mem_kv'], 'L0_attn_w_out': _L0_attn_in['w_out'], 'L0_attn_b_out': _L0_attn_in['b_out'], 'L0_attn_g_out': _L0_attn_in['g_out'], 'L0_attn_g_pre': _L0_attn_in['g_pre'], 'L0_ffn_gamma': _L0_ffn_in['gamma'], 'L0_ffn_beta': _L0_ffn_in['beta'], 'L0_ffn_Wr': _L0_ffn_in['Wr'], 'L0_ffn_br': _L0_ffn_in['br'], 'L0_ffn_W1': _L0_ffn_in['W1'], 'L0_ffn_b1': _L0_ffn_in['b1'], 'L0_ffn_W2': _L0_ffn_in['W2'], 'L0_ffn_b2': _L0_ffn_in['b2']}

def reference(x, L0_tok_emb, L0_tok_W_upd, L0_tok_b_upd, L0_tok_W_f, L0_tok_b_f, L0_tok_decay_param, L0_tok_norm_g, L0_tok_norm_b, L0_tok_cms_ln_g, L0_tok_cms_ln_b, L0_tok_cms_W1, L0_tok_cms_b1, L0_tok_cms_W2, L0_tok_cms_b2, L0_tok_head_W, L0_tok_head_b, L0_attn_t, L0_attn_w_qkv, L0_attn_mem_kv, L0_attn_w_out, L0_attn_b_out, L0_attn_g_out, L0_attn_g_pre, L0_ffn_gamma, L0_ffn_beta, L0_ffn_Wr, L0_ffn_br, L0_ffn_W1, L0_ffn_b1, L0_ffn_W2, L0_ffn_b2):
    import jax
    import jax.numpy as jnp

    def _L0_tok_ref(tokens, emb, W_upd, b_upd, W_f, b_f, decay_param, norm_g, norm_b, cms_ln_g, cms_ln_b, cms_W1, cms_b1, cms_W2, cms_b2, head_W, head_b):
        import jax, jax.numpy as jnp
        import numpy as np
        D_MODEL = 128
        N_LAYERS = 4
        VOCAB = 64
        SEQ = 512
        BATCH = 8
        EPS = 1e-05

        def _ln(x, g, b):
            mu = jnp.mean(x, axis=-1, keepdims=True)
            var = jnp.mean(jnp.square(x - mu), axis=-1, keepdims=True)
            return (x - mu) * jax.lax.rsqrt(var + EPS) * g + b

        def _fast_memory(x, mask, W_upd, b_upd, W_f, b_f, decay_param):
            decay = jax.nn.sigmoid(decay_param[0])
            u = jnp.einsum('bsd,de->bse', x, W_upd) + b_upd
            u_t = jnp.swapaxes(u, 0, 1)
            m_t = jnp.swapaxes(mask, 0, 1)[..., None]

            def step(mem, inp):
                u_i, msk = inp
                new = decay * mem + u_i
                mem = msk * new + (1.0 - msk) * mem
                return (mem, mem)
            mem0 = jnp.zeros((x.shape[0], x.shape[2]), x.dtype)
            _, mems = jax.lax.scan(step, mem0, (u_t, m_t))
            mems = jnp.swapaxes(mems, 0, 1)
            return jnp.einsum('bsd,de->bse', mems, W_f) + b_f
        mask = (tokens != 0).astype(emb.dtype)
        x = emb[tokens]
        x = x + _fast_memory(x, mask, W_upd, b_upd, W_f, b_f, decay_param)
        x = _ln(x, norm_g, norm_b)
        for i in range(N_LAYERS):
            h = _ln(x, cms_ln_g[i], cms_ln_b[i])
            h = jax.nn.gelu(jnp.einsum('bsd,df->bsf', h, cms_W1[i]) + cms_b1[i], approximate=False)
            h = jnp.einsum('bsf,fd->bsd', h, cms_W2[i]) + cms_b2[i]
            x = x + h
        return jnp.einsum('bsd,dv->bsv', x, head_W) + head_b

    def _L0_attn_ref(x, t, w_qkv, mem_kv, w_out, b_out, g_out, g_pre):
        import jax, jax.numpy as jnp
        import numpy as np
        DIM = 64
        HEADS = 4
        DIM_HEAD = 32
        NUM_MEM = 4
        HIDDEN = HEADS * DIM_HEAD
        SCALE = DIM_HEAD ** (-0.5)

        def rmsnorm(x, g):
            n = jnp.linalg.norm(x, axis=-1, keepdims=True)
            return x / jnp.maximum(n, 1e-12) * g * x.shape[-1] ** 0.5
        b, n, c = x.shape
        xn = rmsnorm(x, g_pre)
        qkv = xn @ w_qkv
        q, k, v = jnp.split(qkv, 3, axis=-1)

        def to_heads(z):
            return z.reshape(b, n, HEADS, DIM_HEAD).transpose(0, 2, 3, 1)
        q, k, v = map(to_heads, (q, k, v))
        mk = jnp.broadcast_to(mem_kv[0], (b, HEADS, DIM_HEAD, NUM_MEM))
        mv = jnp.broadcast_to(mem_kv[1], (b, HEADS, DIM_HEAD, NUM_MEM))
        k = jnp.concatenate([mk, k], axis=-1)
        v = jnp.concatenate([mv, v], axis=-1)
        q = jax.nn.softmax(q, axis=-2) * SCALE
        k = jax.nn.softmax(k, axis=-1)
        context = jnp.einsum('bhdn,bhen->bhde', k, v)
        out = jnp.einsum('bhde,bhdn->bhen', context, q)
        out = out.transpose(0, 3, 1, 2).reshape(b, n, HIDDEN)
        out = rmsnorm(out @ w_out + b_out, g_out)
        return out + x

    def _L0_ffn_ref(x, gamma, beta, Wr, br, W1, b1, W2, b2):
        import jax, jax.numpy as jnp
        import numpy as np
        E = 8
        K = 2
        D = 64
        H = 128
        DOUT = 64
        EPS = 1e-05
        mu = jnp.mean(x, axis=-1, keepdims=True)
        var = jnp.mean(jnp.square(x - mu), axis=-1, keepdims=True)
        xn = (x - mu) * jax.lax.rsqrt(var + EPS) * gamma + beta
        logits = jnp.einsum('bsd,de->bse', xn, Wr) + br
        top_vals, top_idx = jax.lax.top_k(logits, K)
        w = jax.nn.softmax(top_vals, axis=-1)
        w_full = jnp.einsum('bsk,bske->bse', w, jax.nn.one_hot(top_idx, E, dtype=w.dtype))
        y = jnp.zeros(x.shape[:-1] + (DOUT,), x.dtype)
        for e in range(E):
            h = jax.nn.gelu(jnp.einsum('bsd,dh->bsh', xn, W1[e]) + b1[e], approximate=False)
            y_e = jnp.einsum('bsh,hd->bsd', h, W2[e]) + b2[e]
            y = y + y_e * w_full[..., e, None]
        return y
    h = _L0_tok_ref(x, L0_tok_emb, L0_tok_W_upd, L0_tok_b_upd, L0_tok_W_f, L0_tok_b_f, L0_tok_decay_param, L0_tok_norm_g, L0_tok_norm_b, L0_tok_cms_ln_g, L0_tok_cms_ln_b, L0_tok_cms_W1, L0_tok_cms_b1, L0_tok_cms_W2, L0_tok_cms_b2, L0_tok_head_W, L0_tok_head_b)
    h = h + _L0_attn_ref(_layernorm(h, axis=-1), L0_attn_t, L0_attn_w_qkv, L0_attn_mem_kv, L0_attn_w_out, L0_attn_b_out, L0_attn_g_out, L0_attn_g_pre)
    h = h + _L0_ffn_ref(_layernorm(h, axis=-1), L0_ffn_gamma, L0_ffn_beta, L0_ffn_Wr, L0_ffn_br, L0_ffn_W1, L0_ffn_b1, L0_ffn_W2, L0_ffn_b2)
    return h

_drawn_inputs = setup_inputs


def setup_inputs(seed=0):
    import zlib

    import numpy as np

    out = dict(_drawn_inputs(seed))
    spreads = {'L0_tok_b_upd': (0.0, 0.1),
     'L0_tok_b_f': (0.0, 0.1),
     'L0_tok_norm_g': (1.0, 0.2),
     'L0_tok_norm_b': (0.0, 0.1),
     'L0_tok_cms_ln_g': (1.0, 0.6),
     'L0_tok_cms_ln_b': (0.0, 0.8),
     'L0_tok_cms_b1': (0.0, 0.1),
     'L0_tok_cms_b2': (0.0, 0.1),
     'L0_tok_head_b': (0.0, 0.1),
     'L0_attn_b_out': (0.0, 0.1),
     'L0_attn_g_out': (1.0, 0.2),
     'L0_attn_g_pre': (1.0, 0.6),
     'L0_ffn_br': (0.0, 1.331)}
    factors = {'L0_tok_W_upd': 6.573,
     'L0_attn_mem_kv': 8.0,
     'L0_ffn_gamma': 8.0,
     'L0_ffn_beta': 8.0,
     'L0_ffn_Wr': 4.211,
     'L0_ffn_W1': 5.876,
     'L0_ffn_b1': 8.0,
     'L0_ffn_W2': 5.302,
     'L0_ffn_b2': 20.973}
    for name, (base, spread) in spreads.items():
        noise = np.random.default_rng([zlib.crc32(name.encode()), seed]).standard_normal(out[name].shape)
        drawn = base * np.exp(spread * noise) if base else spread * noise
        out[name] = jnp.asarray(drawn.astype(out[name].dtype))
    for name, factor in factors.items():
        out[name] = (out[name] * factor).astype(out[name].dtype)
    return out
```

```python
import concourse.bass as bass
from concourse import mybir
from contextlib import ExitStack

fp32 = mybir.dt.float32
fp32r = mybir.dt.float32r
i32 = mybir.dt.int32
u32 = mybir.dt.uint32
ALU = mybir.AluOpType
ACT = mybir.ActivationFunctionType
AX = mybir.AxisListType

P = 128
B, S, V = 8, 512, 64
NT = S // P
D, L = 128, 4
F = 4 * D // P
D2 = 64
HEADS, DH, NMEM = 4, 32, 4
E = 8
EPS = 1e-5
FREE = 1
ROUTER_OWN = 20 + 4 * NT
TOKC = 4

C_BUPD, C_BF, C_NG, C_NB = 0, 1, 2, 3
C_LNG, C_LNB, C_B2 = 4, 8, 12
C_B1 = 16
C_GPRE, C_GAMMA, C_BETA = 32, 33, 34
C_EB1 = 35
C_MK = 43
NCOL = 47
R_HEADB, R_BOUT, R_GOUT, R_BR, R_DECAY = 0, 64, 128, 192, 200
NROW = 201
K_ID, K_CEN, K_BLK, K_II, K_IOTA8, K_VOC, K_SEL, K_HALF = 0, 128, 256, 384, 448, 456, 457, 465
NCON = 466


class Own:

    def __init__(self, engine, semaphore):
        self.engine, self.semaphore, self.base, self.n = engine, semaphore, 0, 0

    def inc(self, instruction):
        instruction.then_inc(self.semaphore, 1)
        self.n += 1
        return self.base + self.n

    def wait(self, value):
        self.engine.wait_ge(self.semaphore, value)

    def enter(self, i, per_turn):
        self.start, self.per_turn = self.base + self.n, per_turn
        self.base, self.n = i * per_turn + self.start, 0

    def leave(self, turns):
        assert self.n == self.per_turn, (self.n, self.per_turn)
        self.base, self.n = self.start + turns * self.per_turn, 0


def build(nc, tok_in, emb_in, wupd_in, wf_in, w1_in, w2_in, headw_in, cols_in, rows_in, cons_in,
          wqkv_in, wout_in, memv_in, wr_in, ew1_in, ew2_in, eb2_in, out_hbm):
    ctx = ExitStack()
    with ctx:
        def sb(name, shape, dt=fp32):
            return ctx.enter_context(nc.sbuf_tensor(name, shape, dt))

        def sem(name):
            return ctx.enter_context(nc.semaphore(name))

        x = sb("x", [P, B, S])
        w_all = sb("w_all", [P, L, 2, F, 2, P])
        w_cur = sb("w_cur", [P, 2, F, 2, P], fp32r)
        hid = sb("hid", [P, 2, F, S])
        hid_hi = sb("hid_hi", [P, 2, F, S], fp32r)
        hid_lo = sb("hid_lo", [P, 2, F, S], fp32r)
        xn = sb("xn", [P, 2, S])
        xn_hi = sb("xn_hi", [P, 2, S], fp32r)
        xn_lo = sb("xn_lo", [P, 2, S], fp32r)
        hh = sb("hh", [P, 2, B, NT * D2])
        cols = sb("cols", [P, NCOL])
        rows = sb("rows", [P, NROW])
        cons = sb("cons", [P, NCON])
        headw = sb("headw", [P, D2])
        b1_fold = sb("b1_fold", [P, L * F])
        stats6 = sb("stats6", [P, 4, NT, 6])
        var_in = sb("var_in", [P, 4, 3, NT])
        rstd = sb("rstd", [P, 4, NT])
        mhalf = sb("mhalf", [P, 8])
        two = sb("two", [P, NT])
        small = sb("small", [P, 16])
        scratch = sb("scratch", [P, 8, S])
        tab_full = sb("tab_full", [P, 3, P])
        tab_hi = sb("tab_hi", [P, 3, P], fp32r)
        tab = sb("tab", [P, 3, P], fp32r)

        ident = cons[:, K_ID:K_ID + P]
        centre = cons[:, K_CEN:K_CEN + P]
        blkmask = cons[:, K_BLK:K_BLK + P]
        stack2 = cons[:, K_II:K_II + D2]
        iota8 = cons[:, K_IOTA8:K_IOTA8 + E]
        vocab_id = cons[:, K_VOC:K_VOC + 1]

        w1_raw = hid[:, 0, :, :]
        w2_raw = hid[:, 1, :, :]
        onehot = hid_lo[:, :, :, :].rearrange("p a f s -> p (a f s)")
        emb2, embT, uT = xn[:, 0, 0:P], xn[:, 0, P:2 * P], xn[:, 0, 2 * P:3 * P]
        wupd, wf = xn[:, 1, 0:P], xn[:, 1, P:2 * P]
        toks = hh[:, :, :, :].rearrange("p a b n -> p (a b n)").bitcast(i32)

        h0 = hh[:, 0, :, :]
        h1 = hh[:, 1, :, :]

        wqkv_raw = sb("wqkv_raw", [P, 3 * P])
        wqkv_g = sb("wqkv_g", [P, 3 * P])
        wqkv = sb("wqkv", [P, 2, 3 * P], fp32r)
        wout = sb("wout", [P, D2])
        memv = sb("memv", [NMEM, P])
        mk_max = sb("mk_max", [P, 1])
        ew1_raw = sb("ew1_raw", [P, E * P])
        ew1 = sb("ew1", [P, 2, E * P], fp32r)
        ew2_raw = sb("ew2_raw", [P, E, D2])
        ew2 = sb("ew2", [P, E, 2, D2], fp32r)
        wr_raw = sb("wr_raw", [P, E])
        wr_g = sb("wr_g", [P, E])
        wr = sb("wr", [P, 2, E], fp32r)
        eb2_raw = sb("eb2_raw", [4 * E, D2])
        eb2_hi = sb("eb2_hi", [4 * E, D2], fp32r)
        eb2_lo = sb("eb2_lo", [4 * E, D2])
        eb2_mix = sb("eb2_mix", [4 * E, D2])
        eb2 = sb("eb2", [4 * E, P], fp32r)
        sel = sb("sel", [4 * E, E], fp32r)
        br_fold = sb("br_fold", [P, E])
        eb1_fold = sb("eb1_fold", [P, E])

        st0 = sb("st0", [P, B, NT, 6])
        mv0 = sb("mv0", [P, B, NT, 2])
        pin0 = sb("pin0", [P, B, 2 * NT])
        r0 = sb("r0", [P, B, 2 * NT])
        s0 = sb("s0", [P, B, NT])
        sto = sb("sto", [P, 2, NT, 6])
        mvo = sb("mvo", [P, 2, NT, 2])
        e2o = sb("e2o", [P, 2, 2, NT])
        r2 = sb("r2", [P, B, NT])
        st1 = sb("st1", [P, 2, NT, 6])
        mv1 = sb("mv1", [P, 2, NT, 2])
        t1s = sb("t1s", [P, 2, 4, NT])
        s1 = sb("s1", [P, B, NT])
        mean1 = sb("mean1", [P, B, NT])

        att = w_all[:, :, :, :, :, :].rearrange("p l w f h n -> p (l w f h n)")

        def att_buf(first, width):
            return att[:, first:first + 2 * width].rearrange("p (k n) -> p k n", k=2)
        KEXP = S + NMEM
        xc = att_buf(0, NT * D2)
        zf = att_buf(512, NT * D2)
        zst = att_buf(1024, NT * 2 * D2)
        kexp = att_buf(2048, KEXP)
        v_sb = att_buf(3080, S)
        q_sb = att_buf(4104, S)
        kT = att_buf(5128, S)
        qT = att_buf(6152, S)
        ctm = att_buf(7176, P)
        mx_sb = att_buf(7432, D2)
        memT = att_buf(7560, P)
        zt = xn_hi
        qmax = sb("qmax", [P, 2, NT * HEADS])
        qsum = sb("qsum", [P, 2, NT * HEADS])
        qrec = sb("qrec", [P, 2, NT * HEADS])
        kstat = sb("kstat", [P, 2, 6])

        lg = sb("lg", [P, 2, NT, E])
        mx = sb("mx", [P, 2, NT, 8])
        ix = sb("ix", [P, 2, NT, 8], u32)
        wt = sb("wt", [P, 2, 4, NT])
        oh = sb("oh", [P, 2, 2, NT, E])
        wgt = sb("wgt", [P, 2, NT, E])
        w32 = sb("w32", [P, 2, NT, 4 * E])
        z_all = hid_hi[:, :, :, :].rearrange("p a f s -> p (a f s)")
        wT_all = hid_lo[0:4 * E, :, :, :].rearrange("p a f s -> p (a f s)")
        NSLOT = 4
        hg = hid[:, 0, :, :]
        hw = hid[:, 1, :, :]
        hw_hi = w_cur[:, :, :, :, :].rearrange("p w f h n -> p (w f h n)")
        y_sb = scratch[:, 0:2, :]
        t_sb = scratch[:, 4:6, 0:NT * D2]

        def hw_lo(s):
            return (xn_hi, xn_lo)[s // 2][:, s % 2, :]

        ps = ctx.enter_context(nc.psum_tensor("ps", [P, 8, 512], fp32))
        bank = [ps[:, n, :] for n in range(8)]
        YB, TB, BB = 4, 6, 7

        ld = {n: sem("ld_" + n) for n in
              ("cons", "cols", "rows", "emb", "wupd", "wf", "w1", "w2", "headw", "wqkv", "wout",
               "memv", "wr", "ew1", "ew2", "eb2")}
        ld_tok = [sem(f"ld_tok{c}") for c in range(TOKC)]
        own_dve, own_pool = sem("own_dve"), sem("own_pool")
        mhalf_set = sem("mhalf_set")

        passed = {n: sem("passed_" + n) for n in ("act", "dve", "pool", "pe")}

        def alone(engine, name):
            engine.sem_inc(passed[name], 1)
        embt_done, embt_copied = sem("embt_done"), sem("embt_copied")
        u_done, u_ready = sem("u_done"), sem("u_ready")
        tmem_done = sem("tmem_done")
        tanh_done = sem("tanh_done")
        tables_ready = sem("tables_ready")
        w1_scaled, w1_centred = sem("w1_scaled"), sem("w1_centred")
        w1_hi_ready, w1_lo_ready = sem("w1_hi_ready"), sem("w1_lo_ready")
        w2_hi_ready, w2_lo_ready = sem("w2_hi_ready"), sem("w2_lo_ready")
        folds_done, folds_ready = sem("folds_done"), sem("folds_ready")
        late_weights = sem("late_weights")
        onehot_ready, decay_done, looked_up = sem("onehot_ready"), sem("decay_done"), sem("looked_up")
        decay_copied, scanned, pre_ready = sem("decay_copied"), sem("scanned"), sem("pre_ready")
        x_t, stats_ready, rstd_ready = sem("x_transposed"), sem("stats_ready"), sem("rstd_ready")
        rstd_bc, normed, x_ready = sem("rstd_broadcast"), sem("normed"), sem("x_ready")
        xhi_ready, xlo_ready = sem("xhi_ready"), sem("xlo_ready")
        mm1_done, gelu_done = sem("mm1_done"), sem("gelu_done")
        hhi_ready, hlo_ready, mm2_done = sem("hhi_ready"), sem("hlo_ready"), sem("mm2_done")
        w1_loaded = [sem(f"w1_loaded{f}") for f in range(F)]
        w2_loaded = sem("w2_loaded")
        head_done, h0_ready, mv0_ready = sem("head_done"), sem("h0_ready"), sem("mv0_ready")
        r0_ready, s0_ready = sem("r0_ready"), sem("s0_ready")
        xc_ready, z_ready, zhi_ready, zlo_ready = (sem("xc_ready"), sem("z_ready"), sem("zhi_ready"),
                                                   sem("zlo_ready"))
        res_ready = sem("residual_ready")
        z_t, zt_ready = sem("z_transposed"), sem("zt_ready")
        k_done, qv_done = sem("k_done"), sem("qv_done")
        kmax_ready, kexp_ready, v_ready = sem("kmax_ready"), sem("kexp_ready"), sem("v_ready")
        qsub_ready, qexp_ready, qn_ready = sem("qsub_ready"), sem("qexp_ready"), sem("qn_ready")
        k_t, kt_ready, q_t, qt_ready = sem("k_t"), sem("kt_ready"), sem("q_t"), sem("qt_ready")
        ctx_done, ctm_ready, m_done, m_ready = (sem("ctx_done"), sem("ctm_ready"), sem("m_done"),
                                                sem("m_ready"))
        o_done, o_ready, mvo_ready, r2_ready = (sem("o_done"), sem("o_ready"), sem("mvo_ready"),
                                                sem("r2_ready"))
        mean1_ready = sem("mean1_ready")
        h1_ready, mv1_ready, s1_ready = sem("h1_ready"), sem("mv1_ready"), sem("s1_ready")
        ez_ready, ezhi_ready, ezlo_ready = sem("ez_ready"), sem("ezhi_ready"), sem("ezlo_ready")
        ez_t, ezt_ready, eza_ready = sem("ez_t"), sem("ezt_ready"), sem("eza_ready")
        router_done, gap_ready, gate_tanh = sem("router_done"), sem("gap_ready"), sem("gate_tanh")
        gates_ready, gates_t, gates_copied = sem("gates_ready"), sem("gates_t"), sem("gates_copied")
        e1_done, wb_done, eg_done = sem("e1_done"), sem("wb_done"), sem("eg_done")
        hw_ready, hwhi_ready, hwlo_ready = sem("hw_ready"), sem("hwhi_ready"), sem("hwlo_ready")
        e2_done, y_done, y_copied = sem("e2_done"), sem("y_done"), sem("y_copied")
        yt_done, out_ready = sem("yt_done"), sem("out_ready")
        stored = [sem("stored0"), sem("stored1")]

        def per_tile(ap, width):
            return ap.unsqueeze(2).broadcast_to([P, NT, width])

        def tiles(ap, width=D2):
            return ap.rearrange("p (t c) -> p t c", c=width)

        def row64(first):
            return rows[:, first:first + D2].unsqueeze(1).broadcast_to([P, NT, D2])

        def qv_view(k):
            both = ps[:, 4 * k + 2:4 * k + 4, :].rearrange("p a n -> p (a n)")
            return both.rearrange("p (t w c) -> p t w c", t=NT, w=2)

        block = ctx.enter_context(nc.Block())

        @block.sync
        def _(sp):
            def load(name, dst, src):
                sp.dma_start(dst, src).then_inc(ld[name], 16)

            load("cons", cons[:, :], cons_in)
            load("emb", emb2, emb_in)
            load("wupd", wupd, wupd_in)
            load("wf", wf, wf_in)
            load("cols", cols[:, :], cols_in)
            load("rows", rows[:, :], rows_in.partition_broadcast(P))
            for c in range(TOKC):
                piece = slice(c * (B * S // TOKC), (c + 1) * (B * S // TOKC))
                sp.dma_start(toks[:, piece], tok_in[piece].partition_broadcast(P)).then_inc(ld_tok[c], 16)
            load("w1", w1_raw.rearrange("p l n -> p (l n)"), w1_in)
            load("w2", w2_raw.rearrange("p l n -> p (l n)"), w2_in)
            load("headw", headw[:, :], headw_in)
            load("wqkv", wqkv_raw[:, :], wqkv_in)
            load("wout", wout[:, :], wout_in)
            load("memv", memv[:, :], memv_in)
            load("wr", wr_raw[:, :], wr_in)
            load("ew1", ew1_raw[:, :], ew1_in)
            load("ew2", ew2_raw[:, :, :].rearrange("p e n -> p (e n)"), ew2_in)
            load("eb2", eb2_raw[:, :], eb2_in)

            sp.wait_ge(w1_hi_ready, L)
            sp.wait_ge(w1_lo_ready, L)
            sp.wait_ge(w2_hi_ready, L)
            sp.wait_ge(w2_lo_ready, L)
            for f in range(F):
                sp.dma_start(w_cur[:, 0, f, :, :].bitcast(fp32), w_all[:, 0, 0, f, :, :]).then_inc(w1_loaded[f], 16)
            sp.dma_start(w_cur[:, 1, :, :, :].bitcast(fp32), w_all[:, 0, 1, :, :, :]).then_inc(w2_loaded, 16)
            with sp.Fori(1, L) as l:
                for f in range(F):
                    sp.wait_ge(mm1_done, l * (B * F) + (f + 1 - F))
                    sp.dma_start(w_cur[:, 0, f, :, :].bitcast(fp32),
                                 w_all[:, bass.ds(l, 1), 0, f, :, :]).then_inc(w1_loaded[f], 16)
                sp.wait_ge(mm2_done, l * B)
                sp.dma_start(w_cur[:, 1, :, :, :].bitcast(fp32),
                             w_all[:, bass.ds(l, 1), 1, :, :, :]).then_inc(w2_loaded, 16)

            with sp.Fori(0, B // 2) as g:
                for k in range(2):
                    sp.wait_ge(out_ready, g * 2 + (k + 1) + FREE)
                    dst = out_hbm[bass.ds(g * 2 + k, 1), :, :].rearrange("o (t p) c -> p (o t) c", p=P)
                    src = h1[:, bass.ds(g * 2 + k, 1), :].rearrange("p o n -> p (o n)")
                    sp.dma_start(dst, tiles(src)).then_inc(stored[k], 16)
            sp.wait_ge(stored[0], 16 * (B // 2))
            sp.wait_ge(stored[1], 16 * (B // 2))

        @block.gpsimd
        def _(pool):
            own = Own(pool, own_pool)
            for free in (r2_ready, s1_ready, res_ready):
                pool.sem_inc(free, FREE)
            pool.memset(two[:, :], 2.0)
            pool.memset(mhalf[:, :], -0.5).then_inc(mhalf_set, 1)
            pool.wait_ge(ld["w2"], 16)
            for l in range(L):
                pool.wait_ge(w2_hi_ready, l + 1)
                pool.tensor_tensor(w_all[:, l, 1, :, 1, :].bitcast(fp32r),
                                   w2_raw[:, l, :].rearrange("p (f n) -> p f n", f=F),
                                   w_all[:, l, 1, :, 0, :], ALU.subtract).then_inc(w2_lo_ready, 1)

            def inverse_root_of_row(n, slot):
                pool.wait_ge(stats_ready, n + 1 + FREE)
                st, vi = stats6[:, slot, :, :], var_in[:, slot, :, :]
                own.inc(pool.tensor_tensor(vi[:, 0, :], st[:, :, 1], st[:, :, 4], ALU.subtract))
                v = own.inc(pool.tensor_tensor(vi[:, 1, :], st[:, :, 2], st[:, :, 5], ALU.add))
                own.wait(v)
                alone(pool, "pool")
                v = own.inc(pool.tensor_scalar(vi[:, 1, :], vi[:, 1, :], 4.0 / D, 4.0 * EPS, ALU.mult, ALU.add))
                own.inc(pool.tensor_tensor(vi[:, 0, :], vi[:, 0, :], vi[:, 0, :], ALU.mult))
                own.wait(v + 1)
                v = own.inc(pool.tensor_tensor(vi[:, 2, :], vi[:, 0, :], vi[:, 1, :], ALU.add))
                own.wait(v)
                v = own.inc(pool.tensor_tensor(vi[:, 0, :], vi[:, 2, :], mhalf[:, 0:NT], ALU.pow))
                own.wait(v)
                pool.tensor_tensor(rstd[:, slot, :], vi[:, 0, :], two[:, 0:NT], ALU.mult).then_inc(rstd_ready, 1)

            pool.wait_ge(mhalf_set, 1)
            with pool.Fori(0, B // 4) as g:
                own.enter(g, 4 * 6)
                for k in range(4):
                    inverse_root_of_row(g * 4 + k, k)
                own.leave(B // 4)
            for n in range(2):
                inverse_root_of_row(B + n, n % 4)
            with pool.Fori(0, L) as l:
                own.enter(l, B * 6)
                for i in range(B):
                    inverse_root_of_row(l * B + (B + i + 2), (i + 2) % 4)
                own.leave(L)

            for b in range(B):
                pool.wait_ge(mv0_ready, b + 1)
                own.inc(pool.tensor_scalar(pin0[:, b, 0:NT], mv0[:, b, :, 1], EPS, None, ALU.add))
                v = own.inc(pool.tensor_scalar(pin0[:, b, NT:2 * NT], mv0[:, b, :, 1], 1e-37, None, ALU.max))
                own.wait(v)
                pool.tensor_tensor(r0[:, b, :], pin0[:, b, :], mhalf[:, 0:2 * NT], ALU.pow).then_inc(r0_ready, 1)

            with pool.Fori(0, B // 2) as g:
                own.enter(g, 2 * 4)
                for k in range(2):
                    b = g * 2 + k
                    pool.wait_ge(zlo_ready, b + 1)
                    alone(pool, "pool")
                    v = own.inc(pool.tensor_tensor(tiles(xc[:, k, :]), tiles(xc[:, k, :]),
                                                   per_tile(r0[:, bass.ds(b, 1), 0:NT].rearrange("p o t -> p (o t)"), D2),
                                                   ALU.mult))
                    own.wait(v)
                    alone(pool, "pool")
                    h = h0[:, bass.ds(b, 1), :].rearrange("p o n -> p (o n)")
                    pool.tensor_tensor(h, h, xc[:, k, :], ALU.add).then_inc(res_ready, 1)
                for k in range(2):
                    b = g * 2 + k
                    pool.wait_ge(mvo_ready, b + 1)
                    v = own.inc(pool.tensor_tensor(e2o[:, k, 0, :], mvo[:, k, :, 0], mvo[:, k, :, 0], ALU.mult))
                    own.wait(v)
                    v = own.inc(pool.tensor_tensor(e2o[:, k, 1, :], e2o[:, k, 0, :], mvo[:, k, :, 1], ALU.add))
                    own.wait(v)
                    alone(pool, "pool")
                    v = own.inc(pool.tensor_scalar(e2o[:, k, 0, :], e2o[:, k, 1, :], 1e-24 / D2, None, ALU.max))
                    own.wait(v)
                    alone(pool, "pool")
                    pool.tensor_tensor(r2[:, bass.ds(b, 1), :].rearrange("p o t -> p (o t)"), e2o[:, k, 0, :],
                                       mhalf[:, 0:NT], ALU.pow).then_inc(r2_ready, 1)
                own.leave(B // 2)

            with pool.Fori(0, B // 2) as g:
                own.enter(g, 2 * 6)
                for k in range(2):
                    b = g * 2 + k
                    pool.wait_ge(mv1_ready, b + 1)
                    alone(pool, "pool")
                    var, t = mv1[:, k, :, 1], t1s[:, k, :, :]
                    v = own.inc(pool.tensor_scalar(t[:, 0, :], var, EPS, None, ALU.add))
                    own.wait(v)
                    v = own.inc(pool.tensor_tensor(t[:, 1, :], t[:, 0, :], mhalf[:, 0:NT], ALU.pow))
                    own.wait(v)
                    v = own.inc(pool.tensor_tensor(t[:, 2, :], t[:, 1, :], t[:, 1, :], ALU.mult))
                    own.wait(v)
                    v = own.inc(pool.tensor_tensor(t[:, 3, :], t[:, 2, :], var, ALU.mult))
                    own.wait(v)
                    alone(pool, "pool")
                    v = own.inc(pool.tensor_scalar(t[:, 0, :], t[:, 3, :], EPS, None, ALU.add))
                    own.wait(v)
                    v = own.inc(pool.tensor_tensor(t[:, 2, :], t[:, 0, :], mhalf[:, 0:NT], ALU.pow))
                    own.wait(v)
                    alone(pool, "pool")
                    pool.tensor_tensor(s1[:, bass.ds(b, 1), :].rearrange("p o t -> p (o t)"), t[:, 1, :], t[:, 2, :],
                                       ALU.mult).then_inc(s1_ready, 1)
                own.leave(B // 2)

        @block.scalar
        def _(act):
            for free in (kt_ready, eza_ready, gates_copied):
                act.sem_inc(free, FREE)
            act.preload_act_table(ACT.Gelu)
            act.wait_ge(ld["rows"], 16)
            act.activation(small[:, 0:1], rows[:, R_DECAY:R_DECAY + 1], ACT.Tanh, scale=0.5).then_inc(tanh_done, 1)
            act.wait_ge(ld["cols"], 16)
            act.wait_ge(ld["w1"], 16)
            act.wait_ge(ld["w2"], 16)
            for l in range(L):
                if l >= 2:
                    act.wait_ge(w1_centred, l - 1)
                act.activation(scratch[:, l % 2, :], w1_raw[:, l, :], ACT.Copy,
                               scale=cols[:, C_LNG + l:C_LNG + l + 1]).then_inc(w1_scaled, 1)
                act.activation(w_all[:, l, 1, :, 0, :].bitcast(fp32r),
                               w2_raw[:, l, :].rearrange("p (f n) -> p f n", f=F), ACT.Copy).then_inc(w2_hi_ready, 1)
            for l in range(L):
                act.wait_ge(w1_centred, l + 1)
                act.activation(w_all[:, l, 0, :, 0, :].bitcast(fp32r),
                               bank[l].rearrange("p (f n) -> p f n", f=F), ACT.Copy).then_inc(w1_hi_ready, 1)

            with act.Fori(0, B // 4) as g:
                for k in range(4):
                    act.wait_ge(decay_done, g * 4 + (k + 1))
                    if k >= 2:
                        act.wait_ge(scanned, g * 4 + (k - 1) + FREE)
                    else:
                        act.wait_ge(scanned, g * 4 + FREE)
                    act.activation(scratch[:, 2 + k % 2, :], bank[3 * (k % 2)], ACT.Copy).then_inc(decay_copied, 1)

            def xhi(j, i):
                act.wait_ge(normed, j + (B + 1) + FREE)
                act.activation(xn_hi[:, i % 2, :], xn[:, i % 2, :], ACT.Copy).then_inc(xhi_ready, 1)

            xhi(0, 0)
            with act.Fori(0, L) as l:
                for i in range(B):
                    j = l * B + i
                    for f in range(F):
                        act.wait_ge(mm1_done, j * F + (f + 1))
                        alone(act, "act")
                        act.activation(hid[:, i % 2, f, :], bank[f], ACT.Gelu,
                                       bias=b1_fold[:, bass.ds(l * F + f, 1)]).then_inc(gelu_done, 1)
                        if f % 2:
                            act.wait_ge(gelu_done, j * F + (f + 1))
                            act.activation(hid_hi[:, i % 2, f - 1:f + 1, :], hid[:, i % 2, f - 1:f + 1, :],
                                           ACT.Copy).then_inc(hhi_ready, 1)
                        if f == 1 and i < B - 1:
                            xhi(j + 1, i + 1)
                xhi(l * B + B, 0)

            act.preload_act_table(ACT.Exp)
            with act.Fori(0, B // 2) as g:
                for k in range(2):
                    act.wait_ge(z_ready, g * 2 + (k + 1))
                    act.activation(tiles(zst[:, k, :], 2 * D2)[:, :, 0:D2].bitcast(fp32r), tiles(zf[:, k, :]),
                                   ACT.Copy).then_inc(zhi_ready, 1)
                for k in range(2):
                    act.wait_ge(z_t, g * 2 + (k + 1))
                    act.activation(zt[:, k, :], bank[4 * k], ACT.Copy).then_inc(zt_ready, 1)
                for k in range(2):
                    b = g * 2 + k
                    act.wait_ge(kmax_ready, b + 1)
                    act.activation(kexp[:, k, 0:S], bank[4 * k + 1], ACT.Exp, bias=kstat[:, k, 1:2],
                                   accum_out=kstat[:, k, 2:3])
                    act.activation(kexp[:, k, S:S + NMEM], cols[:, C_MK:C_MK + NMEM], ACT.Exp,
                                   bias=kstat[:, k, 1:2], accum_out=kstat[:, k, 3:4]).then_inc(kexp_ready, 1)
                    act.wait_ge(qsub_ready, b + 1)
                    act.activation(tiles(v_sb[:, k, :], P), qv_view(k)[:, :, 1, :], ACT.Copy).then_inc(v_ready, 1)
                    act.activation(q_sb[:, k, :], q_sb[:, k, :], ACT.Exp).then_inc(qexp_ready, 1)
                for k in range(2):
                    b = g * 2 + k
                    act.wait_ge(k_t, b + 1)
                    act.activation(kT[:, k, :], bank[4 * k], ACT.Copy)
                    act.activation(memT[0:NMEM, k, :], bank[4 * k + 1][0:NMEM, 0:P], ACT.Copy).then_inc(kt_ready, 1)
                for k in range(2):
                    act.wait_ge(q_t, g * 2 + (k + 1))
                    act.activation(qT[:, k, :], bank[4 * k + 2], ACT.Copy).then_inc(qt_ready, 1)

            act.preload_act_table(ACT.Gelu)
            with act.Fori(0, B // 2) as g:
                for k in range(2):
                    act.wait_ge(ez_ready, g * 2 + (k + 1))
                    act.activation(tiles(zst[:, k, :], 2 * D2)[:, :, 0:D2].bitcast(fp32r), tiles(zf[:, k, :]),
                                   ACT.Copy).then_inc(ezhi_ready, 1)
                for k in range(2):
                    b = g * 2 + k
                    act.wait_ge(ez_t, b + 1)
                    act.activation(zt[:, k, :], bank[k], ACT.Copy).then_inc(ezt_ready, 1)
                    alone(act, "act")
                    act.activation(z_all[:, bass.ds(b * S, S)], bank[k], ACT.Copy).then_inc(eza_ready, 1)
                for k in range(2):
                    act.wait_ge(gap_ready, g * 2 + (k + 1))
                    act.activation(wt[:, k, 1, :], wt[:, k, 0, :], ACT.Tanh, scale=0.5).then_inc(gate_tanh, 1)
                for k in range(2):
                    b = g * 2 + k
                    act.wait_ge(gates_t, b + 1)
                    alone(act, "act")
                    act.activation(wT_all[:, bass.ds(b * S, S)], bank[4 + k][0:4 * E, :],
                                   ACT.Copy).then_inc(gates_copied, 1)

            def copy_sum(g, k):
                act.wait_ge(y_done, g * 2 + (k + 1))
                act.activation(y_sb[:, k, :], bank[6 + k], ACT.Copy).then_inc(y_copied, 1)

            with act.Fori(0, B // 2) as g:
                for m in range(2 * E + 1):
                    n = g * (2 * E) + m
                    if m < 2 * E:
                        act.wait_ge(e1_done, n + 1)
                        act.activation(hg[:, m % NSLOT, :], bank[m % 3], ACT.Gelu,
                                       bias=eb1_fold[:, m % E:m % E + 1]).then_inc(eg_done, 1)
                    if m >= 1:
                        act.wait_ge(hw_ready, n)
                        act.activation(hw_hi[:, (m - 1) % NSLOT * S:((m - 1) % NSLOT + 1) * S],
                                       hw[:, (m - 1) % NSLOT, :], ACT.Copy).then_inc(hwhi_ready, 1)
                    if m == E + 4:
                        copy_sum(g, 0)
                copy_sum(g, 1)

        @block.vector
        def _(dve):
            own = Own(dve, own_dve)
            for free in (stats_ready, normed, scanned, m_ready, o_ready, out_ready):
                dve.sem_inc(free, FREE)
            dve.wait_ge(embt_done, 1)
            dve.tensor_copy(embT, bank[6][:, 0:P]).then_inc(embt_copied, 1)
            dve.wait_ge(ld["cols"], 16)
            dve.wait_ge(u_done, 1)
            v = own.inc(dve.tensor_scalar(uT, bank[7][:, 0:P], cols[:, C_BUPD:C_BUPD + 1], None, ALU.add))
            own.wait(v)
            dve.memset(xn[:, 0, 2 * P:2 * P + 1], 0.0).then_inc(u_ready, 1)
            dve.memset(xn[:, 0, 2 * P + V:2 * P + V + 1], 0.0).then_inc(u_ready, 1)
            dve.wait_ge(tanh_done, 1)
            dve.wait_ge(ld["cons"], 16)
            own.inc(dve.tensor_scalar(small[:, 1:2], small[:, 0:1], 0.5, 0.5, ALU.mult, ALU.add))
            own.inc(dve.tensor_scalar(small[:, 2:3], small[:, 0:1], -0.5, 0.5, ALU.mult, ALU.add))
            v = own.inc(dve.tensor_scalar(small[:, 3:4], vocab_id, 0.0, None, ALU.is_equal))
            own.wait(v)
            v = own.inc(dve.scalar_tensor_tensor(small[:, 4:5], small[:, 2:3], small[:, 3:4], small[:, 1:2],
                                                 ALU.mult, ALU.add))
            own.wait(v)
            own.inc(dve.tensor_copy(tab_full[:, 0, :], small[:, 4:5].broadcast_to([P, P])))
            dve.wait_ge(ld["emb"], 16)
            own.inc(dve.reduce_sum(small[:, 5:6], emb2, AX.X))
            dve.wait_ge(tmem_done, 1)
            v = own.inc(dve.reduce_sum(small[:, 6:7], bank[5][:, 0:P], AX.X))
            own.wait(v)
            v = own.inc(dve.tensor_scalar(small[:, 7:9], small[:, 5:7], -1.0 / D, None, ALU.mult))
            own.wait(v)
            own.inc(dve.tensor_scalar(tab_full[:, 2, :], emb2, small[:, 7:8], None, ALU.add))
            v = own.inc(dve.tensor_scalar(tab_full[:, 1, :], bank[5][:, 0:P], small[:, 8:9], None, ALU.add))
            own.wait(v)
            own.inc(dve.tensor_copy(tab[0:V], tab_full[0:V]))
            v = own.inc(dve.tensor_copy(tab_hi[V:P], tab_full[V:P]))
            own.wait(v)
            dve.tensor_tensor(tab[V:P], tab_full[V:P], tab_hi[V:P].bitcast(fp32), ALU.subtract).then_inc(tables_ready, 1)
            for l in range(L):
                dve.wait_ge(w1_hi_ready, l + 1)
                dve.tensor_tensor(w_all[:, l, 0, :, 1, :].bitcast(fp32r),
                                  bank[l].rearrange("p (f n) -> p f n", f=F),
                                  w_all[:, l, 0, :, 0, :], ALU.subtract).then_inc(w1_lo_ready, 1)
            dve.wait_ge(folds_done, 1)
            own.inc(dve.tensor_copy(small[:, 9:10], bank[4][:, 40:41]))
            own.inc(dve.tensor_tensor(b1_fold[:, :], bank[4][:, 0:16], cols[:, C_B1:C_B1 + 16], ALU.add))
            own.inc(dve.tensor_tensor(eb1_fold[:, :], bank[4][:, 16:24], cols[:, C_EB1:C_EB1 + E], ALU.add))
            dve.tensor_tensor(br_fold[:, :], bank[4][:, 24:32], rows[:, R_BR:R_BR + E],
                              ALU.add).then_inc(folds_ready, 1)

            def row_stats(slot, waited):
                dve.wait_ge(x_t, waited)
                for t in range(NT):
                    last = dve.bn_stats(stats6[:, slot, t, :], bank[TB][:, t * P:(t + 1) * P])
                last.then_inc(stats_ready, 1)

            for c in range(TOKC):
                dve.wait_ge(ld_tok[c], 16)
                dve.tensor_scalar(onehot[:, c * (B * S // TOKC):(c + 1) * (B * S // TOKC)],
                                  toks[:, c * (B * S // TOKC):(c + 1) * (B * S // TOKC)], vocab_id, None,
                                  ALU.is_equal).then_inc(onehot_ready, 1)
            dve.wait_ge(folds_ready, 1)
            with dve.Fori(0, B // 4) as g:
                n = [g * 4 + k for k in range(4)]
                def scan(k):
                    dve.wait_ge(decay_copied, n[k] + 1)
                    dve.wait_ge(looked_up, n[k] + 1)
                    dve.tensor_tensor_scan(scratch[:, 4 + k, :], scratch[:, 2 + k % 2, :],
                                           bank[3 * (k % 2) + 1], 0.0, ALU.mult, ALU.add).then_inc(scanned, 1)

                def pre(k):
                    dve.wait_ge(scanned, n[k] + 1 + FREE)
                    dve.scalar_tensor_tensor(scratch[:, 4 + k, :], scratch[:, 4 + k, :], small[:, 9:10],
                                             bank[3 * (k % 2) + 2], ALU.add, ALU.add).then_inc(pre_ready, 1)

                def norm(k):
                    dve.wait_ge(rstd_bc, n[k] + 1)
                    dve.tensor_tensor(scratch[:, 4 + k, :], scratch[:, 4 + k, :], bank[BB], ALU.mult).then_inc(normed, 1)

                def affine(k):
                    dve.wait_ge(normed, n[k] + 1 + FREE)
                    dve.tensor_scalar(x[:, bass.ds(n[k], 1), :].rearrange("p o n -> p (o n)"),
                                      scratch[:, 4 + k, :], cols[:, C_NG:C_NG + 1], cols[:, C_NB:C_NB + 1],
                                      ALU.mult, ALU.add).then_inc(x_ready, 1)

                scan(0)
                scan(1)
                pre(0)
                pre(1)
                row_stats(0, n[0] + 1)
                scan(2)
                row_stats(1, n[1] + 1)
                scan(3)
                pre(2)
                pre(3)
                row_stats(2, n[2] + 1)
                row_stats(3, n[3] + 1)
                norm(0)
                norm(1)
                affine(0)
                norm(2)
                affine(1)
                norm(3)
                affine(2)
                affine(3)

            def norm_x(j, i):
                dve.wait_ge(rstd_bc, j + (B + 1))
                dve.tensor_tensor(xn[:, i % 2, :], x[:, i % B, :], bank[BB], ALU.mult).then_inc(normed, 1)

            def x_lo(j, i):
                dve.wait_ge(xhi_ready, j + 1)
                dve.tensor_tensor(xn_lo[:, i % 2, :], xn[:, i % 2, :], xn_hi[:, i % 2, :].bitcast(fp32),
                                  ALU.subtract).then_inc(xlo_ready, 1)

            def h_lo(j, i, p):
                dve.wait_ge(hhi_ready, j * 2 + (p + 1))
                dve.tensor_tensor(hid_lo[:, i % 2, 2 * p:2 * p + 2, :], hid[:, i % 2, 2 * p:2 * p + 2, :],
                                  hid_hi[:, i % 2, 2 * p:2 * p + 2, :].bitcast(fp32),
                                  ALU.subtract).then_inc(hlo_ready, 1)

            def residual(j, i, l):
                dve.wait_ge(mm2_done, j + 1)
                dve.scalar_tensor_tensor(x[:, i, :], bank[YB + i % 2], cols[:, bass.ds(l + C_B2, 1)],
                                         x[:, i, :], ALU.add, ALU.add).then_inc(x_ready, 1)

            row_stats(0, B + 1)
            row_stats(1, B + 2)
            norm_x(0, 0)
            x_lo(0, 0)
            with dve.Fori(0, L) as l:
                for i in range(B):
                    j = l * B + i
                    if i < B - 1:
                        row_stats((i + 2) % 4, j + (B + 3))
                        norm_x(j + 1, i + 1)
                    if i >= 2:
                        residual(j - 2, i - 2, l)
                    h_lo(j, i, 0)
                    if i < B - 1:
                        x_lo(j + 1, i + 1)
                    h_lo(j, i, 1)
                j = l * B + B
                row_stats(1, j + (B + 2))
                norm_x(j, B)
                residual(j - 2, B - 2, l)
                x_lo(j, B)
                residual(j - 1, B - 1, l)

            for n in ("wqkv", "wr", "ew1", "ew2", "eb2"):
                dve.wait_ge(ld[n], 16)
            own.inc(dve.tensor_scalar(wqkv_g[:, :], wqkv_raw[:, :], cols[:, C_GPRE:C_GPRE + 1], None, ALU.mult))
            own.inc(dve.tensor_scalar(wr_g[:, :], wr_raw[:, :], cols[:, C_GAMMA:C_GAMMA + 1], None, ALU.mult))
            own.inc(dve.tensor_scalar(ew1_raw[:, :], ew1_raw[:, :], cols[:, C_GAMMA:C_GAMMA + 1], None, ALU.mult))
            own.inc(dve.tensor_copy(ew2[:, :, 0, :], ew2_raw[:, :, :]))
            own.inc(dve.tensor_copy(eb2_hi[:, :], eb2_raw[:, :]))
            own.inc(dve.tensor_copy(sel[:, :], cons[0:4 * E, K_SEL:K_SEL + E]))
            own.inc(dve.reduce_max(mk_max[:, :], cols[:, C_MK:C_MK + NMEM], AX.X))
            v = own.inc(dve.memset(eb2[:, D2:P].bitcast(fp32), 0.0))
            own.wait(v)
            own.inc(dve.tensor_copy(wqkv[:, 0, :], wqkv_g[:, :]))
            own.inc(dve.tensor_copy(wr[:, 0, :], wr_g[:, :]))
            own.inc(dve.tensor_copy(ew1[:, 0, :], ew1_raw[:, :]))
            v = own.inc(dve.tensor_tensor(eb2_lo[:, :], eb2_raw[:, :], eb2_hi[:, :].bitcast(fp32), ALU.subtract))
            own.wait(v)
            own.inc(dve.tensor_tensor(wqkv[:, 1, :], wqkv_g[:, :], wqkv[:, 0, :].bitcast(fp32), ALU.subtract))
            own.inc(dve.tensor_tensor(wr[:, 1, :], wr_g[:, :], wr[:, 0, :].bitcast(fp32), ALU.subtract))
            own.inc(dve.tensor_tensor(ew1[:, 1, :], ew1_raw[:, :], ew1[:, 0, :].bitcast(fp32), ALU.subtract))
            own.inc(dve.tensor_tensor(ew2[:, :, 1, :], ew2_raw[:, :, :], ew2[:, :, 0, :].bitcast(fp32), ALU.subtract))
            half = cons[0:4 * E, K_HALF:K_HALF + 1]
            v = own.inc(dve.tensor_tensor(eb2_mix[:, :], eb2_lo[:, :], eb2_hi[:, :].bitcast(fp32), ALU.subtract))
            own.wait(v)
            v = own.inc(dve.tensor_scalar(eb2_mix[:, :], eb2_mix[:, :], half, None, ALU.mult))
            own.wait(v)
            dve.tensor_tensor(eb2[:, 0:D2], eb2_mix[:, :], eb2_hi[:, :].bitcast(fp32), ALU.add).then_inc(late_weights, 1)
            dve.wait_ge(late_weights, 1)

            def row_moments(src, st, out):
                for t in range(NT):
                    v = own.inc(dve.bn_stats(st[:, t, :], src[:, t, :]))
                own.wait(v)
                alone(dve, "dve")
                for t in range(NT):
                    last = dve.bn_aggr(out[:, t, :], st[:, t, :])
                return last

            def head_moments(b):
                dve.wait_ge(h0_ready, b + 1)
                row_moments(tiles(h0[:, b, :]), st0[:, b, :, :], mv0[:, b, :, :]).then_inc(mv0_ready, 1)

            for b in range(B):
                dve.wait_ge(head_done, b + 1)
                dve.tensor_tensor(tiles(h0[:, b, :]), tiles(bank[b % 4][:, 0:NT * D2]), row64(R_HEADB),
                                  ALU.add).then_inc(h0_ready, 1)
                if b:
                    head_moments(b - 1)
            head_moments(B - 1)
            for b in range(B):
                dve.wait_ge(r0_ready, b + 1)
                dve.scalar_tensor_tensor(s0[:, b, :], r0[:, b, 0:NT], 8e12, r0[:, b, NT:2 * NT],
                                         ALU.mult, ALU.min).then_inc(s0_ready, 1)

            def at(buf, b):
                return buf[:, bass.ds(b, 1), :].rearrange("p o n -> p (o n)")

            def at_stat(buf, b, c):
                return buf[:, bass.ds(b, 1), :, c].rearrange("p o t -> p (o t)")

            dve.wait_ge(s0_ready, B)
            with dve.Fori(0, B // 2) as g:
                own.enter(g, 12 + 2 * NT)
                n = [g * 2 + k for k in range(2)]
                for k in range(2):
                    dve.wait_ge(res_ready, g * 2 + FREE)
                    dve.tensor_tensor(tiles(xc[:, k, :]), tiles(at(h0, n[k])), per_tile(at_stat(mv0, n[k], 0), D2),
                                      ALU.subtract).then_inc(xc_ready, 1)
                for k in range(2):
                    dve.wait_ge(xc_ready, n[k] + 1)
                    dve.tensor_tensor(tiles(zf[:, k, :]), tiles(xc[:, k, :]), per_tile(at(s0, n[k]), D2),
                                      ALU.mult).then_inc(z_ready, 1)
                for k in range(2):
                    dve.wait_ge(zhi_ready, n[k] + 1)
                    st = tiles(zst[:, k, :], 2 * D2)
                    dve.tensor_tensor(st[:, :, D2:2 * D2].bitcast(fp32r), tiles(zf[:, k, :]), st[:, :, 0:D2],
                                      ALU.subtract).then_inc(zlo_ready, 1)
                for k in range(2):
                    dve.wait_ge(k_done, n[k] + 1)
                    v = own.inc(dve.reduce_max(kstat[:, k, 0:1], bank[4 * k + 1], AX.X))
                    own.wait(v)
                    dve.tensor_scalar(kstat[:, k, 1:2], kstat[:, k, 0:1], mk_max[:, 0:1], -1.0, ALU.max,
                                      ALU.mult).then_inc(kmax_ready, 1)
                    dve.wait_ge(qv_done, n[k] + 1)
                    q4 = qv_view(k)[:, :, 0, :].rearrange("p t (h d) -> p t h d", h=HEADS)
                    v = own.inc(dve.reduce_max(qmax[:, k, :].rearrange("p (t h) -> p t h", h=HEADS), q4, AX.X))
                    own.wait(v)
                    dve.tensor_tensor(q_sb[:, k, :].rearrange("p (t h d) -> p t h d", t=NT, h=HEADS), q4,
                                      qmax[:, k, :].rearrange("p (t h) -> p t h", h=HEADS).unsqueeze(3)
                                      .broadcast_to([P, NT, HEADS, DH]), ALU.subtract).then_inc(qsub_ready, 1)
                for k in range(2):
                    dve.wait_ge(qexp_ready, n[k] + 1)
                    q3 = q_sb[:, k, :].rearrange("p (a d) -> p a d", d=DH)
                    v = own.inc(dve.reduce_sum(qsum[:, k, :], q3, AX.X))
                    own.wait(v)
                    v = own.inc(dve.reciprocal(qrec[:, k, :], qsum[:, k, :]))
                    own.wait(v)
                    dve.tensor_tensor(q3, q3, qrec[:, k, :].unsqueeze(2).broadcast_to([P, NT * HEADS, DH]),
                                      ALU.mult).then_inc(qn_ready, 1)
                for k in range(2):
                    dve.wait_ge(ctx_done, n[k] + 1)
                    dve.tensor_tensor(ctm[:, k, :], bank[4 * k + 1][:, P:2 * P], blkmask, ALU.mult).then_inc(ctm_ready, 1)
                    v = own.inc(dve.tensor_tensor(kstat[:, k, 4:5], kstat[:, k, 2:3], kstat[:, k, 3:4], ALU.add))
                    own.wait(v)
                    v = own.inc(dve.reciprocal(kstat[:, k, 5:6], kstat[:, k, 4:5]))
                for k in range(2):
                    if k == 0:
                        own.wait(v)
                    dve.wait_ge(m_done, n[k] + 1)
                    dve.tensor_scalar(mx_sb[:, k, :], bank[4 * k + 1][:, 2 * P:2 * P + D2], kstat[:, k, 5:6],
                                      float(DH) ** -0.5, ALU.mult, ALU.mult).then_inc(m_ready, 1)
                for k in range(2):
                    dve.wait_ge(o_done, n[k] + 1)
                    dve.tensor_tensor(tiles(at(h1, n[k])), tiles(bank[4 * k + 3][:, 0:NT * D2]), row64(R_BOUT),
                                      ALU.add).then_inc(o_ready, 1)
                for k in range(2):
                    dve.wait_ge(r2_ready, g * 2 + FREE)
                    dve.wait_ge(o_ready, n[k] + 1 + FREE)
                    alone(dve, "dve")
                    row_moments(tiles(at(h1, n[k])), sto[:, k, :, :], mvo[:, k, :, :]).then_inc(mvo_ready, 1)
                own.leave(B // 2)

            with dve.Fori(0, B // 2) as g:
                own.enter(g, 2 * (NT + 2))
                n = [g * 2 + k for k in range(2)]
                for k in range(2):
                    dve.wait_ge(r2_ready, n[k] + 1 + FREE)
                    own.inc(dve.tensor_tensor(tiles(t_sb[:, k, :]), tiles(at(h1, n[k])), per_tile(at(r2, n[k]), D2),
                                              ALU.mult))
                v = own.base + own.n
                for k in range(2):
                    own.wait(v - 1 + k)
                    own.inc(dve.tensor_tensor(tiles(t_sb[:, k, :]), tiles(t_sb[:, k, :]), row64(R_GOUT), ALU.mult))
                v = own.base + own.n
                for k in range(2):
                    own.wait(v - 1 + k)
                    dve.wait_ge(res_ready, n[k] + 1 + FREE)
                    dve.tensor_tensor(at(h1, n[k]), t_sb[:, k, :], at(h0, n[k]), ALU.add).then_inc(h1_ready, 1)
                for k in range(2):
                    dve.wait_ge(s1_ready, g * 2 + FREE)
                    dve.wait_ge(h1_ready, n[k] + 1)
                    alone(dve, "dve")
                    row_moments(tiles(at(h1, n[k])), st1[:, k, :, :], mv1[:, k, :, :]).then_inc(mv1_ready, 1)
                for k in range(2):
                    dve.wait_ge(mv1_ready, n[k] + 1)
                    dve.tensor_copy(at(mean1, n[k]), mv1[:, k, :, 0]).then_inc(mean1_ready, 1)
                own.leave(B // 2)

            with dve.Fori(0, B // 2) as g:
                own.enter(g, ROUTER_OWN)
                n = [g * 2 + k for k in range(2)]
                for k in range(2):
                    dve.wait_ge(mean1_ready, n[k] + 1)
                    dve.wait_ge(s1_ready, n[k] + 1 + FREE)
                    own.inc(dve.tensor_tensor(tiles(t_sb[:, k, :]), tiles(at(h1, n[k])), per_tile(at(mean1, n[k]), D2),
                                              ALU.subtract))
                v = own.base + own.n
                for k in range(2):
                    own.wait(v - 1 + k)
                    dve.tensor_tensor(tiles(zf[:, k, :]), tiles(t_sb[:, k, :]), per_tile(at(s1, n[k]), D2),
                                      ALU.mult).then_inc(ez_ready, 1)
                for k in range(2):
                    dve.wait_ge(ezhi_ready, n[k] + 1)
                    st = tiles(zst[:, k, :], 2 * D2)
                    dve.tensor_tensor(st[:, :, D2:2 * D2].bitcast(fp32r), tiles(zf[:, k, :]), st[:, :, 0:D2],
                                      ALU.subtract).then_inc(ezlo_ready, 1)
                for k in range(2):
                    dve.wait_ge(router_done, n[k] + 1)
                    own.inc(dve.tensor_tensor(lg[:, k, :, :], bank[2 + k][:, 0:NT * E].rearrange("p (t e) -> p t e", e=E),
                                              br_fold[:, :].unsqueeze(1).broadcast_to([P, NT, E]), ALU.add))
                v = own.base + own.n
                for k in range(2):
                    own.wait(v - 1 + k)
                    alone(dve, "dve")
                    for t in range(NT):
                        own.inc(dve.max(mx[:, k, t, :], lg[:, k, t, :]))
                v = own.base + own.n
                for k in range(2):
                    own.wait(v - NT * (1 - k))
                    alone(dve, "dve")
                    for t in range(NT):
                        own.inc(dve.max_index(ix[:, k, t, :], mx[:, k, t, :], lg[:, k, t, :]))
                    dve.tensor_tensor(wt[:, k, 0, :], mx[:, k, :, 0], mx[:, k, :, 1], ALU.subtract).then_inc(gap_ready, 1)
                v = own.base + own.n
                for k in range(2):
                    own.wait(v - NT * (1 - k))
                    for c in range(2):
                        own.inc(dve.tensor_tensor(oh[:, k, c, :, :], iota8.unsqueeze(1).broadcast_to([P, NT, E]),
                                                  per_tile(ix[:, k, :, c], E), ALU.is_equal))
                for k in range(2):
                    dve.wait_ge(gate_tanh, n[k] + 1)
                    for c, sign in ((0, 0.5), (1, -0.5)):
                        own.inc(dve.tensor_scalar(wt[:, k, 2 + c, :], wt[:, k, 1, :], sign, 0.5, ALU.mult, ALU.add))
                v = own.base + own.n
                for k in range(2):
                    own.wait(v - 2 * (1 - k))
                    for c in range(2):
                        own.inc(dve.tensor_tensor(oh[:, k, c, :, :], oh[:, k, c, :, :], per_tile(wt[:, k, 2 + c, :], E),
                                                  ALU.mult))
                v = own.base + own.n
                for k in range(2):
                    own.wait(v - 2 * (1 - k))
                    own.inc(dve.tensor_tensor(wgt[:, k, :, :], oh[:, k, 0, :, :], oh[:, k, 1, :, :], ALU.add))
                v = own.base + own.n
                w5 = [w32[:, k, :, :].rearrange("p t (r c e) -> p t r c e", r=2, c=2) for k in range(2)]
                wg = [wgt[:, k, :, :].unsqueeze(2).broadcast_to([P, NT, 2, E]) for k in range(2)]
                for k in range(2):
                    own.wait(v - 1 + k)
                    own.inc(dve.tensor_copy(w5[k][:, :, :, 0, :].bitcast(fp32r), wg[k]))
                v = own.base + own.n
                for k in range(2):
                    own.wait(v - 1 + k)
                    dve.tensor_tensor(w5[k][:, :, :, 1, :].bitcast(fp32r), wg[k], w5[k][:, :, :, 0, :],
                                      ALU.subtract).then_inc(gates_ready, 1)
                own.leave(B // 2)

            with dve.Fori(0, B // 2) as g:
                for m in range(2 * E + 1):
                    n = g * (2 * E) + m
                    if m < 2 * E:
                        dve.wait_ge(eg_done, n + 1)
                        dve.wait_ge(wb_done, n + 1)
                        dve.tensor_tensor(hw[:, m % NSLOT, :], hg[:, m % NSLOT, :], bank[3 + m % 3],
                                          ALU.mult).then_inc(hw_ready, 1)
                    if m >= 1:
                        slot = (m - 1) % NSLOT
                        dve.wait_ge(hwhi_ready, n)
                        dve.tensor_tensor(hw_lo(slot), hw[:, slot, :], hw_hi[:, slot * S:(slot + 1) * S].bitcast(fp32),
                                          ALU.subtract).then_inc(hwlo_ready, 1)
                for k in range(2):
                    b = g * 2 + k
                    dve.wait_ge(yt_done, b + 1)
                    dve.tensor_tensor(at(h1, b), bank[6 + k][:, 0:NT * D2], at(h1, b), ALU.add).then_inc(out_ready, 1)

        @block.tensor
        def _(pe):
            def mm(out, lhsT, rhs, start=True, stop=True):
                return pe.matmul(out, lhsT, rhs, start=start, stop=stop)

            pe.wait_ge(ld["cons"], 16)
            pe.wait_ge(ld["emb"], 16)
            pe.transpose(bank[6][:, 0:P], emb2, ident).then_inc(embt_done, 1)
            pe.wait_ge(ld["wupd"], 16)
            pe.wait_ge(embt_copied, 1)
            mm(bank[7][:, 0:P], wupd, embT).then_inc(u_done, 1)
            pe.wait_ge(ld["wf"], 16)
            pe.wait_ge(ld["cols"], 16)
            pe.wait_ge(u_ready, 2)
            mm(bank[5][:, 0:P], uT, wf).then_inc(tmem_done, 1)
            for l in range(L):
                pe.wait_ge(w1_scaled, l + 1)
                mm(bank[l], centre, scratch[:, l % 2, :]).then_inc(w1_centred, 1)
            for n in ("ew1", "wr"):
                pe.wait_ge(ld[n], 16)
            for l in range(L):
                for f in range(F):
                    mm(bank[4][:, l * F + f:l * F + f + 1], w1_raw[:, l, f * P:(f + 1) * P],
                       cols[:, C_LNB + l:C_LNB + l + 1])
            beta = cols[0:D2, C_BETA:C_BETA + 1]
            for e in range(E):
                mm(bank[4][:, 16 + e:17 + e], ew1_raw[0:D2, e * P:(e + 1) * P], beta)
            mm(bank[4][:, 40:41], centre, cols[:, C_BF:C_BF + 1])
            mm(bank[4][:, 24:32], beta.broadcast_to([D2, P]), wr_raw[0:D2, :]).then_inc(folds_done, 1)

            def turn(src, ready, count, n):
                pe.wait_ge(ready, count)
                pe.wait_ge(stats_ready, n + FREE)
                for t in range(NT):
                    last = pe.transpose(bank[TB][:, t * P:(t + 1) * P], src[:, t * P:(t + 1) * P], ident)
                last.then_inc(x_t, 1)

            def broadcast(slot, n):
                pe.wait_ge(rstd_ready, n + 1)
                pe.wait_ge(normed, n + FREE)
                for t in range(NT):
                    last = pe.transpose(bank[BB][:, t * P:(t + 1) * P], rstd[:, slot, t:t + 1].broadcast_to([P, P]), ident)
                last.then_inc(rstd_bc, 1)

            pe.wait_ge(tables_ready, 1)
            pe.wait_ge(w1_lo_ready, L)
            pe.wait_ge(folds_ready, 1)
            pe.wait_ge(onehot_ready, TOKC)
            with pe.Fori(0, B // 4) as g:
                n = [g * 4 + k for k in range(4)]

                def look_up(k):
                    oh_b = onehot[:, bass.ds(n[k] * S, S)]
                    if k >= 2:
                        pe.wait_ge(decay_copied, n[k] - 1)
                        pe.wait_ge(pre_ready, n[k] - 1)
                    mm(bank[3 * (k % 2)], tab[:, 0, :], oh_b).then_inc(decay_done, 1)
                    mm(bank[3 * (k % 2) + 1], tab[:, 1, :], oh_b)
                    mm(bank[3 * (k % 2) + 2], tab[:, 2, :], oh_b).then_inc(looked_up, 1)

                def turn_k(k):
                    turn(scratch[:, 4 + k, :], pre_ready, n[k] + 1, n[k])

                look_up(0)
                look_up(1)
                turn_k(0)
                look_up(2)
                turn_k(1)
                look_up(3)
                turn_k(2)
                turn_k(3)
                for k in range(4):
                    broadcast(k, n[k])

            def up(j, i):
                pe.wait_ge(xlo_ready, j + 1)
                for f in range(F):
                    if i == 0:
                        pe.wait_ge(w1_loaded[f], l * 16 + 16)
                    else:
                        pe.wait_ge(gelu_done, j * F + (f + 1 - F))
                    hi, lo = w_cur[:, 0, f, 0, :], w_cur[:, 0, f, 1, :]
                    mm(bank[f], hi, xn_hi[:, i % 2, :], stop=False)
                    mm(bank[f], hi, xn_lo[:, i % 2, :], start=False, stop=False)
                    mm(bank[f], lo, xn_hi[:, i % 2, :], start=False).then_inc(mm1_done, 1)

            def down(j, i):
                if i == 0:
                    pe.wait_ge(w2_loaded, l * 16 + 16)
                pe.wait_ge(x_ready, j + (B - 1))
                for f in range(F):
                    if f % 2 == 0:
                        pe.wait_ge(hlo_ready, j * 2 + (f // 2 + 1))
                    hi, lo = w_cur[:, 1, f, 0, :], w_cur[:, 1, f, 1, :]
                    mm(bank[YB + i % 2], hi, hid_hi[:, i % 2, f, :], start=f == 0, stop=False)
                    mm(bank[YB + i % 2], hi, hid_lo[:, i % 2, f, :], start=False, stop=False)
                    last = mm(bank[YB + i % 2], lo, hid_hi[:, i % 2, f, :], start=False, stop=f == F - 1)
                last.then_inc(mm2_done, 1)

            for n in range(2):
                turn(x[:, n, :], x_ready, n + 1, B + n)
            broadcast(0, B)
            with pe.Fori(0, L) as l:
                for i in range(B):
                    j = l * B + i
                    if i < B - 1:
                        turn(x[:, (i + 2) % B, :], x_ready, j + 3, j + (B + 2))
                        broadcast((i + 1) % 4, j + (B + 1))
                    up(j, i)
                    if i:
                        down(j - 1, i - 1)
                j = l * B + B
                turn(x[:, 1, :], x_ready, j + 2, j + (B + 1))
                broadcast(0, j + B)
                down(j - 1, B - 1)

            pe.wait_ge(ld["headw"], 16)
            pe.wait_ge(gelu_done, L * B * F)
            for b in range(B):
                pe.wait_ge(x_ready, B * L + b + 1)
                if b >= 4:
                    pe.wait_ge(h0_ready, b - 3)
                for t in range(NT):
                    last = mm(bank[b % 4][:, t * D2:(t + 1) * D2], x[:, b, t * P:(t + 1) * P], headw[:, :])
                last.then_inc(head_done, 1)

            for n in ("wout", "memv"):
                pe.wait_ge(ld[n], 16)
            pe.wait_ge(late_weights, 1)
            pe.wait_ge(h0_ready, B)
            pe.wait_ge(x_ready, B * (L + 1))
            pe.wait_ge(normed, B * (L + 1) + 1 + FREE)

            def turn_z(k, dst):
                for t in range(NT):
                    last = pe.transpose(dst[:, t * P:(t + 1) * P], zst[:, k, t * P:(t + 1) * P], ident)
                return last

            with pe.Fori(0, B // 2) as g:
                n = [g * 2 + k for k in range(2)]
                for k in range(2):
                    pe.wait_ge(kt_ready, g * 2 + FREE)
                    pe.wait_ge(zlo_ready, n[k] + 1)
                    turn_z(k, bank[4 * k]).then_inc(z_t, 1)
                for k in range(2):
                    kb = bank[4 * k + 1]
                    pe.wait_ge(zt_ready, n[k] + 1)
                    pe.wait_ge(m_ready, g * 2 + FREE)
                    mm(kb, wqkv[:, 0, P:2 * P], zt[:, k, :], stop=False)
                    mm(kb, wqkv[:, 1, P:2 * P], zt[:, k, :], start=False).then_inc(k_done, 1)
                    pe.wait_ge(o_ready, g * 2 + FREE)
                    qv = qv_view(k)
                    for t in range(NT):
                        for h in range(2):
                            w = wqkv[:, h, :].rearrange("p (c n) -> p c n", c=3)[:, 0:3:2, :]
                            last = mm(qv[:, t, :, :], zt[:, k, t * P:(t + 1) * P], w, start=h == 0, stop=h == 1)
                    last.then_inc(qv_done, 1)
                for k in range(2):
                    pe.wait_ge(kexp_ready, n[k] + 1)
                    for t in range(NT):
                        pe.transpose(bank[4 * k][:, t * P:(t + 1) * P], kexp[:, k, t * P:(t + 1) * P], ident)
                    pe.transpose(bank[4 * k + 1][0:NMEM, 0:P], kexp[:, k, S:S + NMEM], ident).then_inc(k_t, 1)
                for k in range(2):
                    pe.wait_ge(kt_ready, n[k] + 1 + FREE)
                    pe.wait_ge(v_ready, n[k] + 1)
                    cb = bank[4 * k + 1][:, P:2 * P]
                    for t in range(NT):
                        mm(cb, v_sb[:, k, t * P:(t + 1) * P], kT[:, k, t * P:(t + 1) * P], start=t == 0, stop=False)
                    mm(cb, memv[:, :], memT[0:NMEM, k, :], start=False).then_inc(ctx_done, 1)
                for k in range(2):
                    pe.wait_ge(qn_ready, n[k] + 1)
                    for t in range(NT):
                        last = pe.transpose(bank[4 * k + 2][:, t * P:(t + 1) * P], q_sb[:, k, t * P:(t + 1) * P], ident)
                    last.then_inc(q_t, 1)
                for k in range(2):
                    pe.wait_ge(ctm_ready, n[k] + 1)
                    mm(bank[4 * k + 1][:, 2 * P:2 * P + D2], ctm[:, k, :], wout[:, :]).then_inc(m_done, 1)
                for k in range(2):
                    pe.wait_ge(m_ready, n[k] + 1 + FREE)
                    pe.wait_ge(qt_ready, n[k] + 1)
                    for t in range(NT):
                        last = mm(bank[4 * k + 3][:, t * D2:(t + 1) * D2], qT[:, k, t * P:(t + 1) * P], mx_sb[:, k, :])
                    last.then_inc(o_done, 1)

            pe.wait_ge(o_ready, B + FREE)
            with pe.Fori(0, B // 2) as g:
                n = [g * 2 + k for k in range(2)]
                for k in range(2):
                    pe.wait_ge(eza_ready, g * 2 + FREE)
                    pe.wait_ge(ezlo_ready, n[k] + 1)
                    turn_z(k, bank[k]).then_inc(ez_t, 1)
                for k in range(2):
                    pe.wait_ge(ezt_ready, n[k] + 1)
                    for t in range(NT):
                        for h in range(2):
                            last = mm(bank[2 + k][:, t * E:(t + 1) * E], zt[:, k, t * P:(t + 1) * P], wr[:, h, :],
                                      start=h == 0, stop=h == 1)
                    last.then_inc(router_done, 1)
                for k in range(2):
                    pe.wait_ge(gates_copied, g * 2 + FREE)
                    pe.wait_ge(gates_ready, n[k] + 1)
                    for t in range(NT):
                        last = pe.transpose(bank[4 + k][0:4 * E, t * P:(t + 1) * P], w32[:, k, t, :], ident)
                    last.then_inc(gates_t, 1)

            SKEW = 3
            pe.wait_ge(eza_ready, B + FREE)
            pe.wait_ge(gates_copied, B + FREE)
            with pe.Fori(0, B // 2) as g:
                for m in range(2 * E + SKEW):
                    n = g * (2 * E) + m
                    if m < 2 * E:
                        k, e = m // E, m % E
                        z_b = z_all[:, bass.ds(g * (2 * S) + k * S, S)]
                        w_b = wT_all[:, bass.ds(g * (2 * S) + k * S, S)]
                        if m >= 3:
                            pe.wait_ge(eg_done, n - 2)
                        mm(bank[m % 3], ew1[:, 0, e * P:(e + 1) * P], z_b, stop=False)
                        mm(bank[m % 3], ew1[:, 1, e * P:(e + 1) * P], z_b, start=False).then_inc(e1_done, 1)
                        if m >= 3:
                            pe.wait_ge(hw_ready, n - 2)
                            alone(pe, "pe")
                        mm(bank[3 + m % 3], sel[:, e:e + 1].broadcast_to([4 * E, P]), w_b).then_inc(wb_done, 1)
                        if e == 0:
                            if k == 0:
                                pe.wait_ge(out_ready, g * 2 + FREE)
                                alone(pe, "pe")
                            mm(bank[6 + k], eb2[:, :], w_b, stop=False)
                    if m >= SKEW:
                        k, e, slot = (m - SKEW) // E, (m - SKEW) % E, (m - SKEW) % NSLOT
                        w = ew2[:, e, :, :].rearrange("p h n -> p (h n)")
                        pe.wait_ge(hwlo_ready, n - (SKEW - 1))
                        mm(bank[6 + k], w, hw_hi[:, slot * S:(slot + 1) * S], start=False, stop=False)
                        last = mm(bank[6 + k], w, hw_lo(slot), start=False, stop=e == E - 1)
                        if e == E - 1:
                            last.then_inc(y_done, 1)
                    if m >= 2 * E + SKEW - 2:
                        k = m - (2 * E + SKEW - 2)
                        pe.wait_ge(y_copied, g * 2 + (k + 1))
                        for t in range(NT):
                            last = mm(bank[6 + k][:, t * D2:(t + 1) * D2], y_sb[:, k, t * P:(t + 1) * P], stack2)
                        last.then_inc(yt_done, 1)


def kernel(**inputs):
    import numpy as np
    import concourse.bacc as bacc
    from concourse.bass_utils import run_bass_kernel_spmd

    a = {n: np.asarray(t) for n, t in inputs.items()}
    tok = {n[7:]: t for n, t in a.items() if n.startswith("L0_tok_")}
    att = {n[8:]: t for n, t in a.items() if n.startswith("L0_attn_")}
    ffn = {n[7:]: t for n, t in a.items() if n.startswith("L0_ffn_")}

    def twice(t):
        return np.concatenate([t, t], axis=0)

    cols = np.concatenate([
        tok["b_upd"][:, None], tok["b_f"][:, None], tok["norm_g"][:, None], tok["norm_b"][:, None],
        tok["cms_ln_g"].T, tok["cms_ln_b"].T, tok["cms_b2"].T,
        tok["cms_b1"].reshape(L * F, P).T,
        twice(att["g_pre"][:, None]), twice(ffn["gamma"][:, None]), twice(ffn["beta"][:, None]),
        ffn["b1"].T, att["mem_kv"][0].reshape(P, NMEM)], axis=1)
    rows = np.concatenate([tok["head_b"], att["b_out"], att["g_out"], ffn["br"], tok["decay_param"]])

    cons = np.zeros((P, NCON), np.float32)
    lane = np.arange(P)
    cons[:, K_ID:K_ID + P] = np.eye(P)
    cons[:, K_CEN:K_CEN + P] = np.eye(P) - 1.0 / P
    cons[:, K_BLK:K_BLK + P] = lane[:, None] // DH == lane[None, :] // DH
    cons[:, K_II:K_II + D2] = lane[:, None] % D2 == np.arange(D2)
    cons[:, K_IOTA8:K_IOTA8 + E] = np.arange(E)
    cons[:, K_VOC] = lane % V
    cons[:2 * E, K_SEL:K_SEL + E] = lane[:2 * E, None] % E == np.arange(E)
    cons[2 * E:4 * E, K_HALF] = 1.0

    arrays = {
        "tokens": a["x"].reshape(B * S),
        "emb": twice(tok["emb"]),
        "w_upd": tok["W_upd"],
        "w_f": tok["W_f"],
        "w1": tok["cms_W1"].transpose(1, 0, 2).reshape(P, L * F * P),
        "w2": tok["cms_W2"].reshape(L, F, P, D).transpose(2, 0, 1, 3).reshape(P, L * F * D),
        "head_w": tok["head_W"],
        "cols": cols,
        "rows": rows,
        "constants": cons,
        "w_qkv": twice(att["w_qkv"]),
        "w_out": att["w_out"],
        "mem_v": att["mem_kv"][1].reshape(P, NMEM).T,
        "w_r": twice(ffn["Wr"]),
        "expert_w1": twice(ffn["W1"].transpose(1, 0, 2).reshape(D2, E * P)),
        "expert_w2": ffn["W2"].transpose(1, 0, 2).reshape(P, E * D2),
        "expert_b2": np.concatenate([ffn["b2"]] * 4, axis=0),
    }
    arrays = {n: np.ascontiguousarray(t) for n, t in arrays.items()}
    nc = bacc.Bacc("TRN2", target_bir_lowering=False, num_devices=1)
    args = [nc.dram_tensor("in_" + n, t.shape, mybir.dt.from_np(t.dtype), kind="ExternalInput").ap()
            for n, t in arrays.items()]
    out = nc.dram_tensor("out", (B, S, D2), fp32, kind="ExternalOutput").ap()
    build(nc, *args, out)
    r = run_bass_kernel_spmd(nc, [{"in_" + n: t for n, t in arrays.items()}], core_ids=[0])
    return r.results[0]["out"]
```

```python
import concourse.bass as bass
from concourse import mybir
from contextlib import ExitStack

fp32 = mybir.dt.float32
fp32r = mybir.dt.float32r
i32 = mybir.dt.int32
u32 = mybir.dt.uint32
ALU = mybir.AluOpType
ACT = mybir.ActivationFunctionType
AX = mybir.AxisListType

P = 128
B, S, V = 8, 512, 64
NT = S // P
D, L = 128, 4
F = 4 * D // P
D2 = 64
HEADS, DH, NMEM = 4, 32, 4
E = 8
EPS = 1e-5
FREE = 1
TURN_OWN = 20 + 4 * NT
W1_STEP = 5
TOKC = B

C_BUPD, C_BF, C_NG, C_NB = 0, 1, 2, 3
C_LNG, C_LNB, C_B2 = 4, 8, 12
C_B1 = 16
C_GPRE, C_GAMMA, C_BETA = 32, 33, 34
C_EB1 = 35
C_MK = 43
NCOL = 47
R_HEADB, R_BOUT, R_GOUT, R_BR, R_DECAY = 0, 64, 128, 192, 200
NROW = 201
K_ID, K_CEN, K_BLK, K_II, K_BACK8, K_VOC, K_SEL, K_HALF = 0, 128, 256, 384, 448, 456, 457, 465
NCON = 466


class Own:

    def __init__(self, engine, semaphore):
        self.engine, self.semaphore, self.base, self.n = engine, semaphore, 0, 0

    def inc(self, instruction):
        instruction.then_inc(self.semaphore, 1)
        self.n += 1
        return self.base + self.n

    def wait(self, value):
        self.engine.wait_ge(self.semaphore, value)

    def enter(self, i, per_turn):
        self.start, self.per_turn = self.base + self.n, per_turn
        self.base, self.n = i * per_turn + self.start, 0

    def leave(self, turns):
        assert self.n == self.per_turn, (self.n, self.per_turn)
        self.base, self.n = self.start + turns * self.per_turn, 0


def build(nc, tok_in, emb_in, wupd_in, wf_in, w1_in, w2_in, headw_in, cols_in, rows_in, cons_in,
          wqkv_in, wout_in, memv_in, wr_in, ew1_in, ew2_in, eb2_in, out_hbm):
    ctx = ExitStack()
    with ctx:
        def sb(name, shape, dt=fp32):
            return ctx.enter_context(nc.sbuf_tensor(name, shape, dt))

        def sem(name):
            return ctx.enter_context(nc.semaphore(name))

        x = sb("x", [P, B, S])
        w_all = sb("w_all", [P, L, 2, F, 2, P])
        w_cur = sb("w_cur", [P, 2, F, 2, P], fp32r)
        hid = sb("hid", [P, 2, F, S])
        hid_hi = sb("hid_hi", [P, 2, F, S], fp32r)
        hid_lo = sb("hid_lo", [P, 2, F, S], fp32r)
        xn = sb("xn", [P, 2, S])
        xn_hi = sb("xn_hi", [P, 2, S], fp32r)
        xn_lo = sb("xn_lo", [P, 2, S], fp32r)
        hh = sb("hh", [P, 2, B, NT * D2])
        cols = sb("cols", [P, NCOL])
        rows = sb("rows", [P, NROW])
        cons = sb("cons", [P, NCON])
        headw = sb("headw", [P, D2])
        b1_fold = sb("b1_fold", [P, L * F])
        stats6 = sb("stats6", [P, 4, NT, 6])
        var_in = sb("var_in", [P, 4, 3, NT])
        rstd = sb("rstd", [P, 4, NT])
        mhalf = sb("mhalf", [P, 8])
        two = sb("two", [P, NT])
        eps_row = sb("eps_row", [P, NT])
        small = sb("small", [P, 16])
        scratch = sb("scratch", [P, 8, S])
        tab_full = sb("tab_full", [P, 3, P])
        tab_hi = sb("tab_hi", [P, 3, P], fp32r)
        tab = sb("tab", [P, 3, P], fp32r)

        ident = cons[:, K_ID:K_ID + P]
        centre = cons[:, K_CEN:K_CEN + P]
        blkmask = cons[:, K_BLK:K_BLK + P]
        stack2 = cons[:, K_II:K_II + D2]
        back8 = cons[:, K_BACK8:K_BACK8 + E]
        vocab_id = cons[:, K_VOC:K_VOC + 1]

        w1_raw = hid[:, 0, :, :]
        w2_raw = hid[:, 1, :, :]
        onehot = hid_lo[:, :, :, :].rearrange("p a f s -> p (a f s)")
        emb2, embT, uT = xn[:, 0, 0:P], xn[:, 0, P:2 * P], xn[:, 0, 2 * P:3 * P]
        wupd, wf = xn[:, 1, 0:P], xn[:, 1, P:2 * P]
        toks = hh[:, :, :, :].rearrange("p a b n -> p (a b n)").bitcast(i32)

        h0 = hh[:, 0, :, :]
        h1 = hh[:, 1, :, :]

        wqkv_raw = sb("wqkv_raw", [P, 3 * P])
        wqkv_g = sb("wqkv_g", [P, 3 * P])
        wqkv = sb("wqkv", [P, 2, 3 * P], fp32r)
        wout = sb("wout", [P, D2])
        memv = sb("memv", [NMEM, P])
        mk_max = sb("mk_max", [P, 1])
        ew1_raw = sb("ew1_raw", [P, E * P])
        ew1 = sb("ew1", [P, 2, E * P], fp32r)
        ew2_raw = sb("ew2_raw", [P, E, D2])
        ew2 = sb("ew2", [P, E, 2, D2], fp32r)
        wr_raw = sb("wr_raw", [P, E])
        wr_g = sb("wr_g", [P, E])
        wr = sb("wr", [P, 2, E], fp32r)
        eb2_raw = sb("eb2_raw", [4 * E, D2])
        eb2_hi = sb("eb2_hi", [4 * E, D2], fp32r)
        eb2_lo = sb("eb2_lo", [4 * E, D2])
        eb2_mix = sb("eb2_mix", [4 * E, D2])
        eb2 = sb("eb2", [4 * E, P], fp32r)
        sel = sb("sel", [4 * E, E], fp32r)
        br_fold = sb("br_fold", [P, E])
        eb1_fold = sb("eb1_fold", [P, E])
        tbuf = sb("tbuf", [P, 2, NT * D2])

        st0 = sb("st0", [P, B, NT, 6])
        mv0 = sb("mv0", [P, B, NT, 2])
        s0_in = sb("s0_in", [P, B, NT])
        r0_in = sb("r0_in", [P, 2, 2 * NT])
        s0 = sb("s0", [P, B, NT])
        sto = sb("sto", [P, 2, NT, 6])
        mvo = sb("mvo", [P, 2, NT, 2])
        e2o = sb("e2o", [P, 2, 2, NT])
        r2 = sb("r2", [P, 2, NT])
        st1 = sb("st1", [P, 2, NT, 6])
        mv1 = sb("mv1", [P, 2, NT, 2])
        t1s = sb("t1s", [P, 2, NT])
        s1 = sb("s1", [P, 2, NT])

        att = w_all[:, :, :, :, :, :].rearrange("p l w f h n -> p (l w f h n)")

        def att_buf(first, width):
            return att[:, first:first + 2 * width].rearrange("p (k n) -> p k n", k=2)
        KEXP = S + NMEM
        xc = att_buf(0, NT * D2)
        zf = att_buf(512, NT * D2)
        zst = att_buf(1024, NT * 2 * D2)
        kexp = att_buf(2048, KEXP)
        v_sb = att_buf(3080, S)
        q_sb = att_buf(4104, S)
        kT = att_buf(5128, S)
        qT = att_buf(6152, S)
        ctm = att_buf(7176, P)
        mx_sb = att_buf(7432, D2)
        memT = att_buf(7560, P)
        zt = xn_hi
        qmax = sb("qmax", [P, 2, NT * HEADS])
        qsum = sb("qsum", [P, 2, NT * HEADS])
        qrec = sb("qrec", [P, 2, NT * HEADS])
        kstat = sb("kstat", [P, 2, 6])

        R = B * NT
        zst1 = hid[:, :, :, :].rearrange("p a f s -> p (a f s)")
        lg, eq1, oh1, eq2, oh2, wgt = (scratch[:, n // 2, n % 2 * R * E:(n % 2 + 1) * R * E]
                                       .rearrange("p (r e) -> p r e", e=E) for n in range(6))
        w32 = scratch[:, 6:8, :].rearrange("p a (r n) -> p (a r) n", n=4 * E)
        top = sb("top", [P, 8, R])
        z_all = hid_hi[:, :, :, :].rearrange("p a f s -> p (a f s)")
        wT_all = hid_lo[0:4 * E, :, :, :].rearrange("p a f s -> p (a f s)")
        NSLOT = 4
        hg = hid[:, 0, :, :]
        hw = hid[:, 1, :, :]
        hw_hi = w_cur[:, :, :, :, :].rearrange("p w f h n -> p (w f h n)")
        y_sb = scratch[:, 0:2, :]
        t_sb = tbuf[:, :, :]

        def hw_lo(s):
            return (xn_hi, xn_lo)[s // 2][:, s % 2, :]

        ps = ctx.enter_context(nc.psum_tensor("ps", [P, 8, 512], fp32))
        bank = [ps[:, n, :] for n in range(8)]
        YB, TB, BB = 4, 6, 7

        ld = {n: sem("ld_" + n) for n in
              ("cons", "cols", "rows", "emb", "wupd", "wf", "w1", "w2", "headw", "wqkv", "wout",
               "memv", "wr", "ew1", "ew2", "eb2")}
        ld_tok = [sem(f"ld_tok{c}") for c in range(TOKC)]
        own_dve, own_pool = sem("own_dve"), sem("own_pool")
        mhalf_set = sem("mhalf_set")

        passed = {n: sem("passed_" + n) for n in ("act", "dve", "pool", "pe")}

        def alone(engine, name):
            engine.sem_inc(passed[name], 1)
        embt_done, embt_copied = sem("embt_done"), sem("embt_copied")
        u_done, u_ready = sem("u_done"), sem("u_ready")
        tmem_done = sem("tmem_done")
        tanh_done = sem("tanh_done")
        tables_ready = sem("tables_ready")
        w1_scaled, w1_centred = sem("w1_scaled"), sem("w1_centred")
        w1_hi_ready, w1_lo_ready = sem("w1_hi_ready"), sem("w1_lo_ready")
        w2_hi_ready, w2_lo_ready = sem("w2_hi_ready"), sem("w2_lo_ready")
        folds_done, folds_ready = sem("folds_done"), sem("folds_ready")
        late_weights = sem("late_weights")
        onehot_ready, decay_done, looked_up = sem("onehot_ready"), sem("decay_done"), sem("looked_up")
        decay_copied, scanned, pre_ready = sem("decay_copied"), sem("scanned"), sem("pre_ready")
        x_t, stats_ready, rstd_ready = sem("x_transposed"), sem("stats_ready"), sem("rstd_ready")
        rstd_bc, normed, x_ready = sem("rstd_broadcast"), sem("normed"), sem("x_ready")
        x0_ready, memory_looked_up = sem("x0_ready"), sem("memory_looked_up")
        late_folds_done = sem("late_folds_done")
        xhi_ready, xlo_ready = sem("xhi_ready"), sem("xlo_ready")
        mm1_done, gelu_done = sem("mm1_done"), sem("gelu_done")
        hhi_ready, hlo_ready, mm2_done = sem("hhi_ready"), sem("hlo_ready"), sem("mm2_done")
        w1_loaded = [sem(f"w1_loaded{f}") for f in range(F)]
        w2_loaded = sem("w2_loaded")
        head_done, h0_ready, mv0_ready = sem("head_done"), sem("h0_ready"), sem("mv0_ready")
        s0_ready = sem("s0_ready")
        z_ready, zhi_ready, zlo_ready = sem("z_ready"), sem("zhi_ready"), sem("zlo_ready")
        res_ready = sem("residual_ready")
        z_t, zt_ready = sem("z_transposed"), sem("zt_ready")
        k_done, qv_done = sem("k_done"), sem("qv_done")
        kmax_ready, kexp_ready, v_ready = sem("kmax_ready"), sem("kexp_ready"), sem("v_ready")
        qsub_ready, qexp_ready, qn_ready = sem("qsub_ready"), sem("qexp_ready"), sem("qn_ready")
        k_t, kt_ready, q_t, qt_ready = sem("k_t"), sem("kt_ready"), sem("q_t"), sem("qt_ready")
        ctx_done, ctm_ready, m_done, m_ready = (sem("ctx_done"), sem("ctm_ready"), sem("m_done"),
                                                sem("m_ready"))
        o_done, o_ready, mvo_ready, r2_ready = (sem("o_done"), sem("o_ready"), sem("mvo_ready"),
                                                sem("r2_ready"))
        h1_ready, mv1_ready, s1_ready = sem("h1_ready"), sem("mv1_ready"), sem("s1_ready")
        ez_ready, ezhi_ready, ezlo_ready = sem("ez_ready"), sem("ezhi_ready"), sem("ezlo_ready")
        ez_t, ezt_ready, eza_ready = sem("ez_t"), sem("ezt_ready"), sem("eza_ready")
        router_done, gap_ready, gate_tanh = sem("router_done"), sem("gap_ready"), sem("gate_tanh")
        gates_ready, gates_t, gates_copied = sem("gates_ready"), sem("gates_t"), sem("gates_copied")
        e1_done, wb_done, eg_done = sem("e1_done"), sem("wb_done"), sem("eg_done")
        hw_ready, hwhi_ready, hwlo_ready = sem("hw_ready"), sem("hwhi_ready"), sem("hwlo_ready")
        e2_done, y_done, y_copied = sem("e2_done"), sem("y_done"), sem("y_copied")
        yt_done, out_ready = sem("yt_done"), sem("out_ready")
        stored = [sem("stored0"), sem("stored1")]

        def per_tile(ap, width):
            return ap.unsqueeze(2).broadcast_to([P, NT, width])

        def tiles(ap, width=D2):
            return ap.rearrange("p (t c) -> p t c", c=width)

        def at(buf, b):
            return buf[:, bass.ds(b, 1), :].rearrange("p o n -> p (o n)")

        def at_stat(buf, b, c):
            return buf[:, bass.ds(b, 1), :, c].rearrange("p o t -> p (o t)")

        def row64(first):
            return rows[:, first:first + D2].unsqueeze(1).broadcast_to([P, NT, D2])

        def qv_view(k):
            both = ps[:, 4 * k + 2:4 * k + 4, :].rearrange("p a n -> p (a n)")
            return both.rearrange("p (t w c) -> p t w c", t=NT, w=2)

        block = ctx.enter_context(nc.Block())

        @block.sync
        def _(sp):
            def load(name, dst, src):
                sp.dma_start(dst, src).then_inc(ld[name], 16)

            def load_tokens(c):
                piece = slice(c * (B * S // TOKC), (c + 1) * (B * S // TOKC))
                sp.dma_start(toks[:, piece], tok_in[piece].partition_broadcast(P)).then_inc(ld_tok[c], 16)

            load("cons", cons[:, :], cons_in)
            load("emb", emb2, emb_in)
            load("wupd", wupd, wupd_in)
            load("cols", cols[:, :], cols_in)
            load("rows", rows[:, :], rows_in.partition_broadcast(P))
            load("wf", wf, wf_in)
            for c in range(3):
                load_tokens(c)
            load("w1", w1_raw.rearrange("p l n -> p (l n)"), w1_in)
            for c in range(3, 5):
                load_tokens(c)
            load("w2", w2_raw.rearrange("p l n -> p (l n)"), w2_in)
            for c in range(5, TOKC):
                load_tokens(c)
            load("headw", headw[:, :], headw_in)
            load("wqkv", wqkv_raw[:, :], wqkv_in)
            load("wout", wout[:, :], wout_in)
            load("memv", memv[:, :], memv_in)
            load("wr", wr_raw[:, :], wr_in)
            load("ew1", ew1_raw[:, :], ew1_in)
            load("ew2", ew2_raw[:, :, :].rearrange("p e n -> p (e n)"), ew2_in)
            load("eb2", eb2_raw[:, :], eb2_in)

            for n in (1, L):
                sp.wait_ge(w1_hi_ready, n)
                sp.wait_ge(w1_lo_ready, n)
                sp.wait_ge(w2_hi_ready, n)
                sp.wait_ge(w2_lo_ready, n)
                if n == 1:
                    for f in range(F):
                        sp.dma_start(w_cur[:, 0, f, :, :].bitcast(fp32), w_all[:, 0, 0, f, :, :]).then_inc(w1_loaded[f], 16)
                    sp.dma_start(w_cur[:, 1, :, :, :].bitcast(fp32), w_all[:, 0, 1, :, :, :]).then_inc(w2_loaded, 16)
            with sp.Fori(1, L) as l:
                for f in range(F):
                    sp.wait_ge(mm1_done, l * (B * F) + (f + 1 - F))
                    sp.dma_start(w_cur[:, 0, f, :, :].bitcast(fp32),
                                 w_all[:, bass.ds(l, 1), 0, f, :, :]).then_inc(w1_loaded[f], 16)
                sp.wait_ge(mm2_done, l * B)
                sp.dma_start(w_cur[:, 1, :, :, :].bitcast(fp32),
                             w_all[:, bass.ds(l, 1), 1, :, :, :]).then_inc(w2_loaded, 16)

            with sp.Fori(0, B // 2) as g:
                for k in range(2):
                    sp.wait_ge(out_ready, g * 2 + (k + 1) + FREE)
                    dst = out_hbm[bass.ds(g * 2 + k, 1), :, :].rearrange("o (t p) c -> p (o t) c", p=P)
                    src = h1[:, bass.ds(g * 2 + k, 1), :].rearrange("p o n -> p (o n)")
                    sp.dma_start(dst, tiles(src)).then_inc(stored[k], 16)
            sp.wait_ge(stored[0], 16 * (B // 2))
            sp.wait_ge(stored[1], 16 * (B // 2))

        @block.gpsimd
        def _(pool):
            own = Own(pool, own_pool)
            pool.memset(two[:, :], 2.0)
            pool.memset(eps_row[:, :], EPS)
            pool.memset(mhalf[:, :], -0.5).then_inc(mhalf_set, 1)

            def w2_lo(l):
                pool.wait_ge(w2_hi_ready, l + 1)
                pool.tensor_tensor(w_all[:, l, 1, :, 1, :].bitcast(fp32r),
                                   w2_raw[:, l, :].rearrange("p (f n) -> p f n", f=F),
                                   w_all[:, l, 1, :, 0, :], ALU.subtract).then_inc(w2_lo_ready, 1)

            def inverse_root_of_pair(n):
                pool.wait_ge(stats_ready, n + 2 + FREE)
                st, vi = stats6[:, n % 4:n % 4 + 2, :, :], var_in[:, n % 4:n % 4 + 2, :, :]
                own.inc(pool.tensor_tensor(vi[:, :, 0, :], st[:, :, :, 1], st[:, :, :, 4], ALU.subtract))
                v = own.inc(pool.tensor_tensor(vi[:, :, 1, :], st[:, :, :, 2], st[:, :, :, 5], ALU.add))
                own.wait(v)
                v = own.inc(pool.tensor_scalar(vi[:, :, 1, :], vi[:, :, 1, :], 4.0 / D, 4.0 * EPS, ALU.mult, ALU.add))
                own.inc(pool.tensor_tensor(vi[:, :, 0, :], vi[:, :, 0, :], vi[:, :, 0, :], ALU.mult))
                own.wait(v + 1)
                v = own.inc(pool.tensor_tensor(vi[:, :, 2, :], vi[:, :, 0, :], vi[:, :, 1, :], ALU.add))
                own.wait(v)
                half = mhalf[:, :].rearrange("p (k t) -> p k t", t=NT)
                v = own.inc(pool.tensor_tensor(vi[:, :, 0, :], vi[:, :, 2, :], half, ALU.pow))
                own.wait(v)
                twos = two[:, :].unsqueeze(1).broadcast_to([P, 2, NT])
                pool.tensor_tensor(rstd[:, n % 4:n % 4 + 2, :], vi[:, :, 0, :], twos, ALU.mult).then_inc(rstd_ready, 2)

            def inverse_root_of_row(n, slot):
                pool.wait_ge(stats_ready, n + 1 + FREE)
                st, vi = stats6[:, slot, :, :], var_in[:, slot, :, :]
                own.inc(pool.tensor_tensor(vi[:, 0, :], st[:, :, 1], st[:, :, 4], ALU.subtract))
                v = own.inc(pool.tensor_tensor(vi[:, 1, :], st[:, :, 2], st[:, :, 5], ALU.add))
                own.wait(v)
                alone(pool, "pool")
                v = own.inc(pool.tensor_scalar(vi[:, 1, :], vi[:, 1, :], 4.0 / D, 4.0 * EPS, ALU.mult, ALU.add))
                own.inc(pool.tensor_tensor(vi[:, 0, :], vi[:, 0, :], vi[:, 0, :], ALU.mult))
                own.wait(v + 1)
                v = own.inc(pool.tensor_tensor(vi[:, 2, :], vi[:, 0, :], vi[:, 1, :], ALU.add))
                own.wait(v)
                v = own.inc(pool.tensor_tensor(vi[:, 0, :], vi[:, 2, :], mhalf[:, 0:NT], ALU.pow))
                own.wait(v)
                pool.tensor_tensor(rstd[:, slot, :], vi[:, 0, :], two[:, 0:NT], ALU.mult).then_inc(rstd_ready, 1)

            pool.wait_ge(mhalf_set, 1)
            inverse_root_of_pair(0)
            inverse_root_of_pair(2)
            pool.wait_ge(ld["w2"], 16)
            w2_lo(0)
            w2_lo(1)
            inverse_root_of_pair(4)
            w2_lo(2)
            w2_lo(3)
            inverse_root_of_pair(6)
            for n in range(2):
                inverse_root_of_row(B + n, n % 4)
            with pool.Fori(0, L) as l:
                own.enter(l, B * 6)
                for i in range(B):
                    inverse_root_of_row(l * B + (B + i + 2), (i + 2) % 4)
                own.leave(L)

            for b in range(B):
                pool.wait_ge(mv0_ready, b + 1)
                v = own.inc(pool.tensor_scalar(s0_in[:, b, :], mv0[:, b, :, 1], EPS / 64e24, None, ALU.max))
                own.wait(v)
                pool.tensor_tensor(s0[:, b, :], s0_in[:, b, :], mhalf[:, 0:NT], ALU.pow).then_inc(s0_ready, 1)

            def residual_base(b, k):
                v = own.inc(pool.tensor_tensor(r0_in[:, k, 0:NT], at_stat(mv0, b, 1), eps_row[:, 0:NT], ALU.add))
                own.wait(v)
                own.inc(pool.tensor_tensor(r0_in[:, k, NT:2 * NT], r0_in[:, k, 0:NT], mhalf[:, 0:NT], ALU.pow))
                v = own.inc(pool.tensor_tensor(tiles(xc[:, k, :]), tiles(at(h0, b)), per_tile(at_stat(mv0, b, 0), D2),
                                               ALU.subtract))
                own.wait(v)
                v = own.inc(pool.tensor_tensor(tiles(xc[:, k, :]), tiles(xc[:, k, :]),
                                               per_tile(r0_in[:, k, NT:2 * NT], D2), ALU.mult))
                pool.wait_ge(z_ready, b + 1)
                alone(pool, "pool")
                own.wait(v)
                alone(pool, "pool")
                pool.tensor_tensor(at(h0, b), at(h0, b), xc[:, k, :], ALU.add).then_inc(res_ready, 1)

            def output_norm(b, k):
                pool.wait_ge(mvo_ready, b + 1)
                v = own.inc(pool.tensor_tensor(e2o[:, k, 0, :], mvo[:, k, :, 0], mvo[:, k, :, 0], ALU.mult))
                own.wait(v)
                v = own.inc(pool.tensor_tensor(e2o[:, k, 1, :], e2o[:, k, 0, :], mvo[:, k, :, 1], ALU.add))
                own.wait(v)
                alone(pool, "pool")
                v = own.inc(pool.tensor_scalar(e2o[:, k, 0, :], e2o[:, k, 1, :], 1e-24 / D2, None, ALU.max))
                own.wait(v)
                pool.tensor_tensor(r2[:, k, :], e2o[:, k, 0, :], mhalf[:, 0:NT], ALU.pow).then_inc(r2_ready, 1)

            def expert_norm(b, k):
                pool.wait_ge(mv1_ready, b + 1)
                alone(pool, "pool")
                v = own.inc(pool.tensor_scalar(t1s[:, k, :], mv1[:, k, :, 1], 1.0 + EPS, EPS * EPS, ALU.mult, ALU.add))
                own.wait(v)
                pool.tensor_tensor(s1[:, k, :], t1s[:, k, :], mhalf[:, 0:NT], ALU.pow).then_inc(s1_ready, 1)

            def pool_turn(g, more):
                for k in range(2):
                    output_norm(g * 2 + k, k)
                for k in range(2):
                    expert_norm(g * 2 + k, k)
                if more:
                    for k in range(2):
                        residual_base(g * 2 + (k + 2), k)

            for k in range(2):
                residual_base(k, k)
            with pool.Fori(0, B // 2 - 1) as g:
                own.enter(g, 2 * 8)
                pool_turn(g, True)
                own.leave(B // 2 - 1)
            pool_turn(B // 2 - 1, False)

        @block.scalar
        def _(act):
            act.preload_act_table(ACT.Gelu)
            act.wait_ge(ld["rows"], 16)
            act.activation(small[:, 0:1], rows[:, R_DECAY:R_DECAY + 1], ACT.Tanh, scale=0.5).then_inc(tanh_done, 1)

            def decays(n):
                act.wait_ge(decay_done, n + 1)
                if n >= 2:
                    act.wait_ge(scanned, n - 1 + FREE)
                act.activation(scratch[:, 2 + n % 2, :], bank[n % 2], ACT.Copy).then_inc(decay_copied, 1)

            def affine(n):
                act.wait_ge(normed, n + 1 + FREE)
                act.activation(x[:, n, :], scratch[:, 4 + n % 4, :], ACT.Identity, bias=cols[:, C_NB:C_NB + 1],
                               scale=cols[:, C_NG:C_NG + 1]).then_inc(x0_ready, 1)

            def weights_in(l):
                act.activation(scratch[:, l % 2, :], w1_raw[:, l, :], ACT.Copy,
                               scale=cols[:, C_LNG + l:C_LNG + l + 1]).then_inc(w1_scaled, 1)
                if l == 0:
                    act.wait_ge(ld["w2"], 16)
                act.activation(w_all[:, l, 1, :, 0, :].bitcast(fp32r),
                               w2_raw[:, l, :].rearrange("p (f n) -> p f n", f=F), ACT.Copy).then_inc(w2_hi_ready, 1)

            def w1_hi(l):
                act.wait_ge(w1_centred, l + 1)
                act.activation(w_all[:, l, 0, :, 0, :].bitcast(fp32r),
                               bank[5].rearrange("p (f n) -> p f n", f=F), ACT.Copy).then_inc(w1_hi_ready, 1)

            act.wait_ge(ld["cols"], 16)
            for n in range(B + 4):
                if n < B:
                    decays(n)
                if n == 4:
                    act.wait_ge(ld["w1"], 16)
                if n >= 4:
                    affine(n - 4)
                if n >= W1_STEP + 1 and n - W1_STEP - 1 < L:
                    w1_hi(n - W1_STEP - 1)
                if n >= W1_STEP - 1 and n - W1_STEP + 1 < L:
                    weights_in(n - W1_STEP + 1)
            act.wait_ge(folds_ready, 1)

            def xhi(j, i):
                act.wait_ge(normed, j + (B + 1) + FREE)
                act.activation(xn_hi[:, i % 2, :], xn[:, i % 2, :], ACT.Copy).then_inc(xhi_ready, 1)

            xhi(0, 0)
            with act.Fori(0, L) as l:
                for i in range(B):
                    j = l * B + i
                    for f in range(F):
                        act.wait_ge(mm1_done, j * F + (f + 1))
                        alone(act, "act")
                        act.activation(hid[:, i % 2, f, :], bank[f], ACT.Gelu,
                                       bias=b1_fold[:, bass.ds(l * F + f, 1)]).then_inc(gelu_done, 1)
                        if f % 2:
                            act.wait_ge(gelu_done, j * F + (f + 1))
                            act.activation(hid_hi[:, i % 2, f - 1:f + 1, :], hid[:, i % 2, f - 1:f + 1, :],
                                           ACT.Copy).then_inc(hhi_ready, 1)
                        if f == 1 and i < B - 1:
                            xhi(j + 1, i + 1)
                xhi(l * B + B, 0)

            def z_hi(b, k):
                act.wait_ge(z_ready, b + 1)
                act.activation(tiles(zst[:, k, :], 2 * D2)[:, :, 0:D2].bitcast(fp32r), tiles(zf[:, k, :]),
                               ACT.Copy).then_inc(zhi_ready, 1)

            def z_turned(b, k):
                act.wait_ge(z_t, b + 1)
                act.activation(zt[:, k, :], bank[4 * k], ACT.Copy).then_inc(zt_ready, 1)

            def exp_k(b, k):
                act.wait_ge(kmax_ready, b + 1)
                act.activation(kexp[:, k, 0:S], bank[4 * k + 1], ACT.Exp, bias=kstat[:, k, 1:2],
                               accum_out=kstat[:, k, 2:3])
                act.activation(kexp[:, k, S:S + NMEM], cols[:, C_MK:C_MK + NMEM], ACT.Exp,
                               bias=kstat[:, k, 1:2], accum_out=kstat[:, k, 3:4]).then_inc(kexp_ready, 1)

            def exp_q(b, k):
                act.wait_ge(qsub_ready, b + 1)
                act.activation(q_sb[:, k, :], q_sb[:, k, :], ACT.Exp).then_inc(qexp_ready, 1)

            def copy_v(b, k):
                act.wait_ge(qsub_ready, b + 1)
                act.activation(tiles(v_sb[:, k, :], P), qv_view(k)[:, :, 1, :], ACT.Copy).then_inc(v_ready, 1)

            def k_turned(b, k):
                act.wait_ge(k_t, b + 1)
                act.activation(kT[:, k, :], bank[4 * k], ACT.Copy)
                act.activation(memT[0:NMEM, k, :], bank[4 * k + 1][0:NMEM, 0:P], ACT.Copy).then_inc(kt_ready, 1)

            def q_turned(b, k):
                act.wait_ge(q_t, b + 1)
                act.activation(qT[:, k, :], bank[4 * k], ACT.Copy).then_inc(qt_ready, 1)

            def ez_hi(b, k):
                act.wait_ge(ez_ready, b + 1)
                alone(act, "act")
                act.activation(tiles(zst1[:, bass.ds(b * S, S)], 2 * D2)[:, :, 0:D2].bitcast(fp32r),
                               tiles(zf[:, k, :]), ACT.Copy).then_inc(ezhi_ready, 1)

            def act_pair(steps, b):
                for step in steps:
                    for k in range(2):
                        step(b + k, k)

            def act_turn(g, more):
                now, nxt = g * 2, g * 2 + 2
                act_pair((k_turned,), now)
                if more:
                    act_pair((z_hi,), nxt)
                act_pair((q_turned,), now)
                if more:
                    act_pair((z_turned, exp_k, exp_q, copy_v), nxt)
                act_pair((ez_hi,), now)

            act.preload_act_table(ACT.Exp)
            act_pair((z_hi, z_turned, exp_k, exp_q, copy_v), 0)
            with act.Fori(0, B // 2 - 1) as g:
                act_turn(g, True)
            act_turn(B // 2 - 1, False)

            act.preload_act_table(ACT.Gelu)
            for b in range(B):
                act.wait_ge(ez_t, b + 1)
                act.activation(z_all[:, b * S:(b + 1) * S], bank[b % 2], ACT.Copy).then_inc(eza_ready, 1)
            act.wait_ge(gap_ready, 1)
            act.activation(top[:, 5, :], top[:, 4, :], ACT.Tanh, scale=0.5).then_inc(gate_tanh, 1)
            for b in range(B):
                act.wait_ge(gates_t, b + 1)
                act.activation(wT_all[:, b * S:(b + 1) * S], bank[4 + b % 4][0:4 * E, :],
                               ACT.Copy).then_inc(gates_copied, 1)

            def copy_sum(g, k):
                act.wait_ge(y_done, g * 2 + (k + 1))
                act.activation(y_sb[:, k, :], bank[6 + k], ACT.Copy).then_inc(y_copied, 1)

            with act.Fori(0, B // 2) as g:
                for m in range(2 * E + 1):
                    n = g * (2 * E) + m
                    if m < 2 * E:
                        act.wait_ge(e1_done, n + 1)
                        act.activation(hg[:, m % NSLOT, :], bank[m % 3], ACT.Gelu,
                                       bias=eb1_fold[:, m % E:m % E + 1]).then_inc(eg_done, 1)
                    if m >= 1:
                        act.wait_ge(hw_ready, n)
                        act.activation(hw_hi[:, (m - 1) % NSLOT * S:((m - 1) % NSLOT + 1) * S],
                                       hw[:, (m - 1) % NSLOT, :], ACT.Copy).then_inc(hwhi_ready, 1)
                    if m == E + 4:
                        copy_sum(g, 0)
                copy_sum(g, 1)

        @block.vector
        def _(dve):
            own = Own(dve, own_dve)
            for free in (stats_ready, normed, scanned, out_ready):
                dve.sem_inc(free, FREE)
            dve.wait_ge(embt_done, 1)
            dve.tensor_copy(embT, bank[6][:, 0:P]).then_inc(embt_copied, 1)
            dve.wait_ge(ld["cols"], 16)
            dve.wait_ge(u_done, 1)
            v = own.inc(dve.tensor_scalar(uT, bank[7][:, 0:P], cols[:, C_BUPD:C_BUPD + 1], None, ALU.add))
            own.wait(v)
            dve.memset(xn[:, 0, 2 * P:2 * P + 1], 0.0).then_inc(u_ready, 1)
            dve.memset(xn[:, 0, 2 * P + V:2 * P + V + 1], 0.0).then_inc(u_ready, 1)
            dve.wait_ge(tanh_done, 1)
            dve.wait_ge(ld["cons"], 16)
            own.inc(dve.tensor_scalar(small[:, 1:2], small[:, 0:1], 0.5, 0.5, ALU.mult, ALU.add))
            own.inc(dve.tensor_scalar(small[:, 2:3], small[:, 0:1], -0.5, 0.5, ALU.mult, ALU.add))
            v = own.inc(dve.tensor_scalar(small[:, 3:4], vocab_id, 0.0, None, ALU.is_equal))
            own.wait(v)
            v = own.inc(dve.scalar_tensor_tensor(small[:, 4:5], small[:, 2:3], small[:, 3:4], small[:, 1:2],
                                                 ALU.mult, ALU.add))
            own.wait(v)
            own.inc(dve.tensor_copy(tab_full[:, 0, :], small[:, 4:5].broadcast_to([P, P])))
            dve.wait_ge(ld["emb"], 16)
            own.inc(dve.reduce_sum(small[:, 5:6], emb2, AX.X))
            dve.wait_ge(tmem_done, 1)
            own.inc(dve.tensor_copy(small[:, 9:10], bank[4][:, 0:1]))
            v = own.inc(dve.reduce_sum(small[:, 6:7], bank[5][:, 0:P], AX.X))
            own.wait(v)
            v = own.inc(dve.tensor_scalar(small[:, 7:9], small[:, 5:7], -1.0 / D, None, ALU.mult))
            own.wait(v)
            own.inc(dve.tensor_scalar(tab_full[:, 2, :], emb2, small[:, 7:8], None, ALU.add))
            v = own.inc(dve.tensor_scalar(tab_full[:, 1, :], bank[5][:, 0:P], small[:, 8:9], None, ALU.add))
            own.wait(v)
            own.inc(dve.tensor_copy(tab[0:V], tab_full[0:V]))
            v = own.inc(dve.tensor_copy(tab_hi[V:P], tab_full[V:P]))
            own.wait(v)
            dve.tensor_tensor(tab[V:P], tab_full[V:P], tab_hi[V:P].bitcast(fp32), ALU.subtract).then_inc(tables_ready, 1)

            def row_stats(slot, waited):
                dve.wait_ge(x_t, waited)
                for t in range(NT):
                    last = dve.bn_stats(stats6[:, slot, t, :], bank[TB][:, t * P:(t + 1) * P])
                last.then_inc(stats_ready, 1)

            def one_hot(n):
                dve.wait_ge(ld_tok[n], 16)
                dve.tensor_scalar(onehot[:, n * S:(n + 1) * S], toks[:, n * S:(n + 1) * S], vocab_id, None,
                                  ALU.is_equal).then_inc(onehot_ready, 1)

            def scan(n):
                dve.wait_ge(decay_copied, n + 1)
                dve.wait_ge(memory_looked_up, n + 1)
                dve.tensor_tensor_scan(scratch[:, 4 + n % 4, :], scratch[:, 2 + n % 2, :], bank[2 + n % 2], 0.0,
                                       ALU.mult, ALU.add).then_inc(scanned, 1)

            def pre(n):
                dve.wait_ge(scanned, n + 1 + FREE)
                dve.wait_ge(looked_up, n + 1)
                dve.scalar_tensor_tensor(scratch[:, 4 + n % 4, :], scratch[:, 4 + n % 4, :], small[:, 9:10],
                                         bank[4], ALU.add, ALU.add).then_inc(pre_ready, 1)

            def norm(n):
                dve.wait_ge(rstd_bc, n + 1)
                dve.tensor_tensor(scratch[:, 4 + n % 4, :], scratch[:, 4 + n % 4, :], bank[BB],
                                  ALU.mult).then_inc(normed, 1)

            def w1_lo(l):
                dve.wait_ge(w1_hi_ready, l + 1)
                dve.tensor_tensor(w_all[:, l, 0, :, 1, :].bitcast(fp32r),
                                  bank[5].rearrange("p (f n) -> p f n", f=F),
                                  w_all[:, l, 0, :, 0, :], ALU.subtract).then_inc(w1_lo_ready, 1)

            one_hot(0)
            one_hot(1)
            for n in range(B + 4):
                if n + 2 < B:
                    one_hot(n + 2)
                if n >= 4:
                    norm(n - 4)
                if 1 <= n <= B:
                    row_stats((n - 1) % 4, n)
                if n == B + 1:
                    row_stats(0, B + 1)
                    row_stats(1, B + 2)
                if n < B:
                    if n >= 4:
                        dve.wait_ge(x0_ready, n - 3)
                    scan(n)
                if n == W1_STEP:
                    dve.wait_ge(folds_done, 1)
                    dve.tensor_tensor(b1_fold[:, :], bank[5][:, 0:L * F], cols[:, C_B1:C_B1 + L * F],
                                      ALU.add).then_inc(folds_ready, 1)
                if n > W1_STEP and n - W1_STEP - 1 < L:
                    w1_lo(n - W1_STEP - 1)
                if n < B:
                    pre(n)

            def norm_x(j, i):
                dve.wait_ge(rstd_bc, j + (B + 1))
                dve.tensor_tensor(xn[:, i % 2, :], x[:, i % B, :], bank[BB], ALU.mult).then_inc(normed, 1)

            def x_lo(j, i):
                dve.wait_ge(xhi_ready, j + 1)
                dve.tensor_tensor(xn_lo[:, i % 2, :], xn[:, i % 2, :], xn_hi[:, i % 2, :].bitcast(fp32),
                                  ALU.subtract).then_inc(xlo_ready, 1)

            def h_lo(j, i, p):
                dve.wait_ge(hhi_ready, j * 2 + (p + 1))
                dve.tensor_tensor(hid_lo[:, i % 2, 2 * p:2 * p + 2, :], hid[:, i % 2, 2 * p:2 * p + 2, :],
                                  hid_hi[:, i % 2, 2 * p:2 * p + 2, :].bitcast(fp32),
                                  ALU.subtract).then_inc(hlo_ready, 1)

            def residual(j, i, l):
                dve.wait_ge(mm2_done, j + 1)
                dve.scalar_tensor_tensor(x[:, i, :], bank[YB + i % 2], cols[:, bass.ds(l + C_B2, 1)],
                                         x[:, i, :], ALU.add, ALU.add).then_inc(x_ready, 1)

            norm_x(0, 0)
            x_lo(0, 0)
            dve.wait_ge(x0_ready, B)
            dve.sem_inc(x_ready, B)
            with dve.Fori(0, L) as l:
                for i in range(B):
                    j = l * B + i
                    if i < B - 1:
                        row_stats((i + 2) % 4, j + (B + 3))
                        norm_x(j + 1, i + 1)
                    if i >= 2:
                        residual(j - 2, i - 2, l)
                    h_lo(j, i, 0)
                    if i < B - 1:
                        x_lo(j + 1, i + 1)
                    h_lo(j, i, 1)
                j = l * B + B
                row_stats(1, j + (B + 2))
                norm_x(j, B)
                residual(j - 2, B - 2, l)
                x_lo(j, B)
                residual(j - 1, B - 1, l)

            for n in ("wqkv", "wr", "ew1", "ew2", "eb2"):
                dve.wait_ge(ld[n], 16)
            dve.wait_ge(late_folds_done, 1)
            own.inc(dve.tensor_tensor(eb1_fold[:, :], bank[BB][:, 0:E], cols[:, C_EB1:C_EB1 + E], ALU.add))
            own.inc(dve.tensor_tensor(br_fold[:, :], bank[BB][:, E:2 * E], rows[:, R_BR:R_BR + E], ALU.add))
            own.inc(dve.tensor_scalar(wqkv_g[:, :], wqkv_raw[:, :], cols[:, C_GPRE:C_GPRE + 1], None, ALU.mult))
            own.inc(dve.tensor_scalar(wr_g[:, :], wr_raw[:, :], cols[:, C_GAMMA:C_GAMMA + 1], None, ALU.mult))
            own.inc(dve.tensor_scalar(ew1_raw[:, :], ew1_raw[:, :], cols[:, C_GAMMA:C_GAMMA + 1], None, ALU.mult))
            own.inc(dve.tensor_copy(ew2[:, :, 0, :], ew2_raw[:, :, :]))
            own.inc(dve.tensor_copy(eb2_hi[:, :], eb2_raw[:, :]))
            own.inc(dve.tensor_copy(sel[:, :], cons[0:4 * E, K_SEL:K_SEL + E]))
            own.inc(dve.reduce_max(mk_max[:, :], cols[:, C_MK:C_MK + NMEM], AX.X))
            v = own.inc(dve.memset(eb2[:, D2:P].bitcast(fp32), 0.0))
            own.wait(v)
            own.inc(dve.tensor_copy(wqkv[:, 0, :], wqkv_g[:, :]))
            own.inc(dve.tensor_copy(wr[:, 0, :], wr_g[:, :]))
            own.inc(dve.tensor_copy(ew1[:, 0, :], ew1_raw[:, :]))
            v = own.inc(dve.tensor_tensor(eb2_lo[:, :], eb2_raw[:, :], eb2_hi[:, :].bitcast(fp32), ALU.subtract))
            own.wait(v)
            own.inc(dve.tensor_tensor(wqkv[:, 1, :], wqkv_g[:, :], wqkv[:, 0, :].bitcast(fp32), ALU.subtract))
            own.inc(dve.tensor_tensor(wr[:, 1, :], wr_g[:, :], wr[:, 0, :].bitcast(fp32), ALU.subtract))
            own.inc(dve.tensor_tensor(ew1[:, 1, :], ew1_raw[:, :], ew1[:, 0, :].bitcast(fp32), ALU.subtract))
            own.inc(dve.tensor_tensor(ew2[:, :, 1, :], ew2_raw[:, :, :], ew2[:, :, 0, :].bitcast(fp32), ALU.subtract))
            half = cons[0:4 * E, K_HALF:K_HALF + 1]
            v = own.inc(dve.tensor_tensor(eb2_mix[:, :], eb2_lo[:, :], eb2_hi[:, :].bitcast(fp32), ALU.subtract))
            own.wait(v)
            v = own.inc(dve.tensor_scalar(eb2_mix[:, :], eb2_mix[:, :], half, None, ALU.mult))
            own.wait(v)
            dve.tensor_tensor(eb2[:, 0:D2], eb2_mix[:, :], eb2_hi[:, :].bitcast(fp32), ALU.add).then_inc(late_weights, 1)
            dve.wait_ge(late_weights, 1)

            def row_moments(src, st, out):
                for t in range(NT):
                    v = own.inc(dve.bn_stats(st[:, t, :], src[:, t, :]))
                own.wait(v)
                alone(dve, "dve")
                for t in range(NT):
                    last = dve.bn_aggr(out[:, t, :], st[:, t, :])
                return last

            def head_moments(b):
                dve.wait_ge(h0_ready, b + 1)
                row_moments(tiles(h0[:, b, :]), st0[:, b, :, :], mv0[:, b, :, :]).then_inc(mv0_ready, 1)

            for b in range(B):
                dve.wait_ge(head_done, b + 1)
                dve.tensor_tensor(tiles(h0[:, b, :]), tiles(bank[b % 4][:, 0:NT * D2]), row64(R_HEADB),
                                  ALU.add).then_inc(h0_ready, 1)
                if b:
                    head_moments(b - 1)
            head_moments(B - 1)

            def centred(b, k):
                own.inc(dve.tensor_tensor(tiles(t_sb[:, k, :]), tiles(at(h0, b)), per_tile(at_stat(mv0, b, 0), D2),
                                          ALU.subtract))

            def z_of(b, k, v):
                own.wait(v)
                dve.tensor_tensor(tiles(zf[:, k, :]), tiles(t_sb[:, k, :]), per_tile(at(s0, b), D2),
                                  ALU.mult).then_inc(z_ready, 1)

            def z_lo(b, k):
                dve.wait_ge(zhi_ready, b + 1)
                st = tiles(zst[:, k, :], 2 * D2)
                dve.tensor_tensor(st[:, :, D2:2 * D2].bitcast(fp32r), tiles(zf[:, k, :]), st[:, :, 0:D2],
                                  ALU.subtract).then_inc(zlo_ready, 1)

            def max_k(b, k):
                dve.wait_ge(k_done, b + 1)
                own.inc(dve.reduce_max(kstat[:, k, 0:1], bank[4 * k + 1], AX.X))

            def negated(b, k, v):
                own.wait(v)
                dve.tensor_scalar(kstat[:, k, 1:2], kstat[:, k, 0:1], mk_max[:, 0:1], -1.0, ALU.max,
                                  ALU.mult).then_inc(kmax_ready, 1)

            def q_heads(k):
                return qv_view(k)[:, :, 0, :].rearrange("p t (h d) -> p t h d", h=HEADS)

            def max_q(b, k):
                dve.wait_ge(qv_done, b + 1)
                own.inc(dve.reduce_max(qmax[:, k, :].rearrange("p (t h) -> p t h", h=HEADS), q_heads(k), AX.X))

            def sub_q(b, k, v):
                own.wait(v)
                dve.tensor_tensor(q_sb[:, k, :].rearrange("p (t h d) -> p t h d", t=NT, h=HEADS), q_heads(k),
                                  qmax[:, k, :].rearrange("p (t h) -> p t h", h=HEADS).unsqueeze(3)
                                  .broadcast_to([P, NT, HEADS, DH]), ALU.subtract).then_inc(qsub_ready, 1)

            def q_by_head(k):
                return q_sb[:, k, :].rearrange("p (a d) -> p a d", d=DH)

            def sum_q(b, k):
                dve.wait_ge(qexp_ready, b + 1)
                own.inc(dve.reduce_sum(qsum[:, k, :], q_by_head(k), AX.X))

            def one_over_sum(b, k, v):
                own.wait(v)
                own.inc(dve.reciprocal(qrec[:, k, :], qsum[:, k, :]))

            def normed_q(b, k, v):
                own.wait(v)
                dve.tensor_tensor(q_by_head(k), q_by_head(k), qrec[:, k, :].unsqueeze(2)
                                  .broadcast_to([P, NT * HEADS, DH]), ALU.mult).then_inc(qn_ready, 1)

            def k_total(b, k):
                own.inc(dve.tensor_tensor(kstat[:, k, 4:5], kstat[:, k, 2:3], kstat[:, k, 3:4], ALU.add))

            def one_over_total(b, k, v):
                own.wait(v)
                own.inc(dve.reciprocal(kstat[:, k, 5:6], kstat[:, k, 4:5]))

            def masked_context(b, k):
                dve.wait_ge(ctx_done, b + 1)
                dve.tensor_tensor(ctm[:, k, :], bank[4 * k + 1][:, P:2 * P], blkmask, ALU.mult).then_inc(ctm_ready, 1)

            def scaled_m(b, k, v):
                own.wait(v)
                dve.wait_ge(m_done, b + 1)
                dve.tensor_scalar(mx_sb[:, k, :], bank[4 * k + 1][:, 2 * P:2 * P + D2], kstat[:, k, 5:6],
                                  float(DH) ** -0.5, ALU.mult, ALU.mult).then_inc(m_ready, 1)

            def attended(b, k):
                dve.wait_ge(o_done, b + 1)
                dve.tensor_tensor(tiles(at(h1, b)), tiles(bank[4 * k + 1][:, 2 * P:4 * P]), row64(R_BOUT),
                                  ALU.add).then_inc(o_ready, 1)

            def moments(b, src_ready, st, mv, done):
                for k in range(2):
                    dve.wait_ge(src_ready, b + (k + 1))
                    alone(dve, "dve")
                    for t in range(NT):
                        v = own.inc(dve.bn_stats(st[:, k, t, :], tiles(at(h1, b + k))[:, t, :]))
                for k in range(2):
                    own.wait(v - NT * (1 - k))
                    alone(dve, "dve")
                    for t in range(NT):
                        last = dve.bn_aggr(mv[:, k, t, :], st[:, k, t, :])
                    last.then_inc(done, 1)

            def scaled_output(b, k):
                dve.wait_ge(r2_ready, b + 1)
                own.inc(dve.tensor_tensor(tiles(t_sb[:, k, :]), tiles(at(h1, b)), per_tile(r2[:, k, :], D2), ALU.mult))

            def gained_output(b, k, v):
                own.wait(v)
                own.inc(dve.tensor_tensor(tiles(t_sb[:, k, :]), tiles(t_sb[:, k, :]), row64(R_GOUT), ALU.mult))

            def add_base(b, k, v):
                dve.wait_ge(res_ready, b + 1)
                own.wait(v)
                dve.tensor_tensor(at(h1, b), t_sb[:, k, :], at(h0, b), ALU.add).then_inc(h1_ready, 1)

            def expert_centred(b, k):
                dve.wait_ge(mv1_ready, b + 1)
                own.inc(dve.tensor_tensor(tiles(t_sb[:, k, :]), tiles(at(h1, b)), per_tile(mv1[:, k, :, 0], D2),
                                          ALU.subtract))

            def expert_z(b, k, v):
                own.wait(v)
                dve.wait_ge(s1_ready, b + 1)
                dve.tensor_tensor(tiles(zf[:, k, :]), tiles(t_sb[:, k, :]), per_tile(s1[:, k, :], D2),
                                  ALU.mult).then_inc(ez_ready, 1)

            def expert_z_lo(b, k):
                dve.wait_ge(ezhi_ready, b + 1)
                alone(dve, "dve")
                st = tiles(zst1[:, bass.ds(b * S, S)], 2 * D2)
                dve.tensor_tensor(st[:, :, D2:2 * D2].bitcast(fp32r), tiles(zf[:, k, :]), st[:, :, 0:D2],
                                  ALU.subtract).then_inc(ezlo_ready, 1)

            def both(step, b):
                for k in range(2):
                    step(b + k, k)

            def both_own(step, b, each=1):
                v = own.base + own.n
                for k in range(2):
                    step(b + k, k, v - each * (1 - k))

            def dve_turn(g, more):
                now, nxt = g * 2, g * 2 + 2
                both(sum_q, now)
                both_own(one_over_sum, now)
                both_own(normed_q, now)
                both(k_total, now)
                both_own(one_over_total, now)
                v_total = own.base + own.n
                if more:
                    both(centred, nxt)
                    both_own(z_of, nxt)
                both(masked_context, now)
                for k in range(2):
                    scaled_m(now + k, k, v_total)
                if more:
                    both(z_lo, nxt)
                both(attended, now)
                moments(now, o_ready, sto, mvo, mvo_ready)
                if more:
                    both(max_k, nxt)
                    both_own(negated, nxt)
                    both(max_q, nxt)
                    v_max = own.base + own.n
                both(scaled_output, now)
                both_own(gained_output, now)
                both_own(add_base, now)
                moments(now, h1_ready, st1, mv1, mv1_ready)
                if more:
                    for k in range(2):
                        sub_q(nxt + k, k, v_max)
                both(expert_centred, now)
                both_own(expert_z, now)
                both(expert_z_lo, now)

            dve.wait_ge(s0_ready, B)
            both(centred, 0)
            both_own(z_of, 0)
            both(z_lo, 0)
            both(max_k, 0)
            both_own(negated, 0)
            both(max_q, 0)
            both_own(sub_q, 0)
            with dve.Fori(0, B // 2 - 1) as g:
                own.enter(g, TURN_OWN)
                dve_turn(g, True)
                own.leave(B // 2 - 1)
            dve_turn(B // 2 - 1, False)

            dve.wait_ge(router_done, B)

            def chain(instruction):
                own.wait(own.inc(instruction))

            def each(ap):
                return ap.unsqueeze(2).broadcast_to([P, R, E])

            later = back8.unsqueeze(1).broadcast_to([P, R, E])
            chain(dve.tensor_tensor(lg.rearrange("p (b t) e -> p b t e", t=NT),
                                    bank[2][:, 0:R * E].rearrange("p (b t e) -> p b t e", t=NT, e=E),
                                    br_fold[:, :].unsqueeze(1).unsqueeze(1).broadcast_to([P, B, NT, E]), ALU.add))
            chain(dve.reduce_max(top[:, 0, :], lg, AX.X))
            chain(dve.tensor_tensor(eq1, lg, each(top[:, 0, :]), ALU.is_equal))
            chain(dve.tensor_tensor(eq1, eq1, later, ALU.mult))
            chain(dve.reduce_max(top[:, 1, :], eq1, AX.X))
            chain(dve.tensor_tensor(oh1, eq1, each(top[:, 1, :]), ALU.is_equal))
            chain(dve.scalar_tensor_tensor(lg, oh1, -3e38, lg, ALU.mult, ALU.add))
            chain(dve.reduce_max(top[:, 2, :], lg, AX.X))
            dve.tensor_tensor(top[:, 4, :], top[:, 0, :], top[:, 2, :], ALU.subtract).then_inc(gap_ready, 1)
            chain(dve.tensor_tensor(eq2, lg, each(top[:, 2, :]), ALU.is_equal))
            chain(dve.tensor_tensor(eq2, eq2, later, ALU.mult))
            chain(dve.reduce_max(top[:, 3, :], eq2, AX.X))
            own.inc(dve.tensor_tensor(oh2, eq2, each(top[:, 3, :]), ALU.is_equal))
            dve.wait_ge(gate_tanh, 1)
            own.inc(dve.tensor_scalar(top[:, 6, :], top[:, 5, :], 0.5, 0.5, ALU.mult, ALU.add))
            chain(dve.tensor_scalar(top[:, 7, :], top[:, 5, :], -0.5, 0.5, ALU.mult, ALU.add))
            own.inc(dve.tensor_tensor(oh1, oh1, each(top[:, 6, :]), ALU.mult))
            chain(dve.tensor_tensor(oh2, oh2, each(top[:, 7, :]), ALU.mult))
            chain(dve.tensor_tensor(wgt, oh1, oh2, ALU.add))
            for half in range(2):
                w5 = w32[:, :, half * 2 * E:(half + 1) * 2 * E]
                v = own.inc(dve.tensor_copy(w5[:, :, 0:E].bitcast(fp32r), wgt))
            for half in range(2):
                w5 = w32[:, :, half * 2 * E:(half + 1) * 2 * E]
                own.wait(v - 1 + half)
                dve.tensor_tensor(w5[:, :, E:2 * E].bitcast(fp32r), wgt, w5[:, :, 0:E], ALU.subtract).then_inc(gates_ready, 1)

            with dve.Fori(0, B // 2) as g:
                for m in range(2 * E + 1):
                    n = g * (2 * E) + m
                    if m < 2 * E:
                        dve.wait_ge(eg_done, n + 1)
                        dve.wait_ge(wb_done, n + 1)
                        dve.tensor_tensor(hw[:, m % NSLOT, :], hg[:, m % NSLOT, :], bank[3 + m % 3],
                                          ALU.mult).then_inc(hw_ready, 1)
                    if m >= 1:
                        slot = (m - 1) % NSLOT
                        dve.wait_ge(hwhi_ready, n)
                        dve.tensor_tensor(hw_lo(slot), hw[:, slot, :], hw_hi[:, slot * S:(slot + 1) * S].bitcast(fp32),
                                          ALU.subtract).then_inc(hwlo_ready, 1)
                for k in range(2):
                    b = g * 2 + k
                    dve.wait_ge(yt_done, b + 1)
                    dve.tensor_tensor(at(h1, b), bank[6 + k][:, 0:NT * D2], at(h1, b), ALU.add).then_inc(out_ready, 1)

        @block.tensor
        def _(pe):
            def mm(out, lhsT, rhs, start=True, stop=True):
                return pe.matmul(out, lhsT, rhs, start=start, stop=stop)

            pe.wait_ge(ld["cons"], 16)
            pe.wait_ge(ld["emb"], 16)
            pe.transpose(bank[6][:, 0:P], emb2, ident).then_inc(embt_done, 1)
            pe.wait_ge(ld["wupd"], 16)
            pe.wait_ge(embt_copied, 1)
            mm(bank[7][:, 0:P], wupd, embT).then_inc(u_done, 1)
            pe.wait_ge(ld["wf"], 16)
            pe.wait_ge(ld["cols"], 16)
            pe.wait_ge(u_ready, 2)
            mm(bank[4][:, 0:1], centre, cols[:, C_BF:C_BF + 1])
            mm(bank[5][:, 0:P], uT, wf).then_inc(tmem_done, 1)

            def turn(src, ready, count, n):
                pe.wait_ge(ready, count)
                pe.wait_ge(stats_ready, n + FREE)
                for t in range(NT):
                    last = pe.transpose(bank[TB][:, t * P:(t + 1) * P], src[:, t * P:(t + 1) * P], ident)
                last.then_inc(x_t, 1)

            def broadcast(slot, n):
                pe.wait_ge(rstd_ready, n + 1)
                pe.wait_ge(normed, n + FREE)
                for t in range(NT):
                    last = pe.transpose(bank[BB][:, t * P:(t + 1) * P], rstd[:, slot, t:t + 1].broadcast_to([P, P]), ident)
                last.then_inc(rstd_bc, 1)

            def look_up(n):
                row = onehot[:, n * S:(n + 1) * S]
                pe.wait_ge(onehot_ready, n + 1)
                if n >= 2:
                    pe.wait_ge(decay_copied, n - 1)
                mm(bank[n % 2], tab[:, 0, :], row).then_inc(decay_done, 1)
                if n >= 2:
                    pe.wait_ge(scanned, n - 1 + FREE)
                mm(bank[2 + n % 2], tab[:, 1, :], row).then_inc(memory_looked_up, 1)

            def look_up_embedding(n):
                if n >= 1:
                    pe.wait_ge(pre_ready, n)
                mm(bank[4], tab[:, 2, :], onehot[:, n * S:(n + 1) * S]).then_inc(looked_up, 1)

            def bias_fold(l):
                for f in range(F):
                    last = mm(bank[5][:, l * F + f:l * F + f + 1], w1_raw[:, l, f * P:(f + 1) * P],
                              cols[:, C_LNB + l:C_LNB + l + 1])
                if l == L - 1:
                    last.then_inc(folds_done, 1)

            def centre_w1(l):
                pe.wait_ge(w1_scaled, l + 1)
                if l:
                    pe.wait_ge(w1_lo_ready, l)
                else:
                    pe.wait_ge(folds_ready, 1)
                mm(bank[5], centre, scratch[:, l % 2, :]).then_inc(w1_centred, 1)

            pe.wait_ge(tables_ready, 1)
            look_up(0)
            look_up_embedding(0)
            for n in range(B + 4):
                if n + 1 < B:
                    look_up(n + 1)
                if n < B:
                    turn(scratch[:, 4 + n % 4, :], pre_ready, n + 1, n)
                if n + 1 < B:
                    look_up_embedding(n + 1)
                if n == W1_STEP - 3:
                    pe.wait_ge(ld["w1"], 16)
                    bias_fold(0)
                    bias_fold(1)
                if n == W1_STEP - 2:
                    bias_fold(2)
                    bias_fold(3)
                if n >= W1_STEP and n - W1_STEP < L:
                    centre_w1(n - W1_STEP)
                if n >= 3 and n - 3 < B:
                    broadcast((n - 3) % 4, n - 3)
                if n == B:
                    for i in range(2):
                        turn(x[:, i, :], x0_ready, i + 1, B + i)
            broadcast(0, B)

            def up(j, i):
                pe.wait_ge(xlo_ready, j + 1)
                for f in range(F):
                    if i == 0:
                        pe.wait_ge(w1_loaded[f], l * 16 + 16)
                    else:
                        pe.wait_ge(gelu_done, j * F + (f + 1 - F))
                    hi, lo = w_cur[:, 0, f, 0, :], w_cur[:, 0, f, 1, :]
                    mm(bank[f], hi, xn_hi[:, i % 2, :], stop=False)
                    mm(bank[f], hi, xn_lo[:, i % 2, :], start=False, stop=False)
                    mm(bank[f], lo, xn_hi[:, i % 2, :], start=False).then_inc(mm1_done, 1)

            def down(j, i):
                if i == 0:
                    pe.wait_ge(w2_loaded, l * 16 + 16)
                pe.wait_ge(x_ready, j + (B - 1))
                for f in range(F):
                    if f % 2 == 0:
                        pe.wait_ge(hlo_ready, j * 2 + (f // 2 + 1))
                    hi, lo = w_cur[:, 1, f, 0, :], w_cur[:, 1, f, 1, :]
                    mm(bank[YB + i % 2], hi, hid_hi[:, i % 2, f, :], start=f == 0, stop=False)
                    mm(bank[YB + i % 2], hi, hid_lo[:, i % 2, f, :], start=False, stop=False)
                    last = mm(bank[YB + i % 2], lo, hid_hi[:, i % 2, f, :], start=False, stop=f == F - 1)
                last.then_inc(mm2_done, 1)

            with pe.Fori(0, L) as l:
                for i in range(B):
                    j = l * B + i
                    if i < B - 1:
                        turn(x[:, (i + 2) % B, :], x_ready, j + 3, j + (B + 2))
                        broadcast((i + 1) % 4, j + (B + 1))
                    up(j, i)
                    if i:
                        down(j - 1, i - 1)
                j = l * B + B
                turn(x[:, 1, :], x_ready, j + 2, j + (B + 1))
                broadcast(0, j + B)
                down(j - 1, B - 1)

            for n in ("ew1", "wr"):
                pe.wait_ge(ld[n], 16)
            pe.wait_ge(normed, B * (L + 1) + 1 + FREE)
            beta = cols[0:D2, C_BETA:C_BETA + 1]
            for e in range(E):
                mm(bank[BB][:, e:e + 1], ew1_raw[0:D2, e * P:(e + 1) * P], beta)
            mm(bank[BB][:, E:2 * E], beta.broadcast_to([D2, P]), wr_raw[0:D2, :]).then_inc(late_folds_done, 1)

            pe.wait_ge(ld["headw"], 16)
            pe.wait_ge(gelu_done, L * B * F)
            for b in range(B):
                pe.wait_ge(x_ready, B * L + b + 1)
                if b >= 4:
                    pe.wait_ge(h0_ready, b - 3)
                for t in range(NT):
                    last = mm(bank[b % 4][:, t * D2:(t + 1) * D2], x[:, b, t * P:(t + 1) * P], headw[:, :])
                last.then_inc(head_done, 1)

            for n in ("wout", "memv"):
                pe.wait_ge(ld[n], 16)
            pe.wait_ge(late_weights, 1)
            pe.wait_ge(h0_ready, B)
            pe.wait_ge(x_ready, B * (L + 1))
            pe.wait_ge(normed, B * (L + 1) + 1 + FREE)

            def turn_z(src, dst):
                for t in range(NT):
                    last = pe.transpose(dst[:, t * P:(t + 1) * P], src[:, t * P:(t + 1) * P], ident)
                return last

            def z_transposes(b, k):
                pe.wait_ge(zlo_ready, b + 1)
                turn_z(zst[:, k, :], bank[4 * k]).then_inc(z_t, 1)

            def qkv(b, k):
                kb = bank[4 * k + 1]
                pe.wait_ge(zt_ready, b + 1)
                mm(kb, wqkv[:, 0, P:2 * P], zt[:, k, :], stop=False)
                mm(kb, wqkv[:, 1, P:2 * P], zt[:, k, :], start=False).then_inc(k_done, 1)
                qv = qv_view(k)
                for t in range(NT):
                    for h in range(2):
                        w = wqkv[:, h, :].rearrange("p (c n) -> p c n", c=3)[:, 0:3:2, :]
                        last = mm(qv[:, t, :, :], zt[:, k, t * P:(t + 1) * P], w, start=h == 0, stop=h == 1)
                last.then_inc(qv_done, 1)

            def k_transposes(b, k):
                pe.wait_ge(kexp_ready, b + 1)
                for t in range(NT):
                    pe.transpose(bank[4 * k][:, t * P:(t + 1) * P], kexp[:, k, t * P:(t + 1) * P], ident)
                pe.transpose(bank[4 * k + 1][0:NMEM, 0:P], kexp[:, k, S:S + NMEM], ident).then_inc(k_t, 1)

            def context(b, k):
                pe.wait_ge(kt_ready, b + 1)
                pe.wait_ge(v_ready, b + 1)
                cb = bank[4 * k + 1][:, P:2 * P]
                for t in range(NT):
                    mm(cb, v_sb[:, k, t * P:(t + 1) * P], kT[:, k, t * P:(t + 1) * P], start=t == 0, stop=False)
                mm(cb, memv[:, :], memT[0:NMEM, k, :], start=False).then_inc(ctx_done, 1)

            def q_transposes(b, k):
                pe.wait_ge(qn_ready, b + 1)
                for t in range(NT):
                    last = pe.transpose(bank[4 * k][:, t * P:(t + 1) * P], q_sb[:, k, t * P:(t + 1) * P], ident)
                last.then_inc(q_t, 1)

            def projected_context(b, k):
                pe.wait_ge(ctm_ready, b + 1)
                mm(bank[4 * k + 1][:, 2 * P:2 * P + D2], ctm[:, k, :], wout[:, :]).then_inc(m_done, 1)

            def attend(b, k):
                pe.wait_ge(m_ready, b + 1)
                pe.wait_ge(qt_ready, b + 1)
                for t in range(NT):
                    last = mm(bank[4 * k + 1][:, 2 * P + t * D2:2 * P + (t + 1) * D2], qT[:, k, t * P:(t + 1) * P],
                              mx_sb[:, k, :])
                last.then_inc(o_done, 1)

            def pe_turn(g, more):
                for step in (k_transposes, context, q_transposes, projected_context, attend):
                    for k in range(2):
                        step(g * 2 + k, k)
                if more:
                    for k in range(2):
                        z_transposes(g * 2 + (k + 2), k)
                    for k in range(2):
                        pe.wait_ge(o_ready, g * 2 + (k + 1))
                        qkv(g * 2 + (k + 2), k)

            for step in (z_transposes, qkv):
                for k in range(2):
                    step(k, k)
            with pe.Fori(0, B // 2 - 1) as g:
                pe_turn(g, True)
            pe_turn(B // 2 - 1, False)

            pe.wait_ge(o_ready, B)

            def route(b):
                pe.wait_ge(eza_ready, b + 1)
                for t in range(NT):
                    for h in range(2):
                        last = mm(bank[2][:, (b * NT + t) * E:(b * NT + t + 1) * E],
                                  z_all[:, b * S + t * P:b * S + (t + 1) * P], wr[:, h, :], start=h == 0, stop=h == 1)
                last.then_inc(router_done, 1)

            for b in range(B):
                pe.wait_ge(ezlo_ready, b + 1)
                if b >= 2:
                    pe.wait_ge(eza_ready, b - 1)
                turn_z(zst1[:, b * S:(b + 1) * S], bank[b % 2]).then_inc(ez_t, 1)
                if b:
                    route(b - 1)
            route(B - 1)
            pe.wait_ge(gates_ready, 2)
            for b in range(B):
                if b >= 4:
                    pe.wait_ge(gates_copied, b - 3)
                for t in range(NT):
                    last = pe.transpose(bank[4 + b % 4][0:4 * E, t * P:(t + 1) * P], w32[:, b * NT + t, :], ident)
                last.then_inc(gates_t, 1)

            SKEW = 3
            pe.wait_ge(gates_copied, B)
            with pe.Fori(0, B // 2) as g:
                for m in range(2 * E + SKEW):
                    n = g * (2 * E) + m
                    if m < 2 * E:
                        k, e = m // E, m % E
                        z_b = z_all[:, bass.ds(g * (2 * S) + k * S, S)]
                        w_b = wT_all[:, bass.ds(g * (2 * S) + k * S, S)]
                        if m >= 3:
                            pe.wait_ge(eg_done, n - 2)
                        mm(bank[m % 3], ew1[:, 0, e * P:(e + 1) * P], z_b, stop=False)
                        mm(bank[m % 3], ew1[:, 1, e * P:(e + 1) * P], z_b, start=False).then_inc(e1_done, 1)
                        if m >= 3:
                            pe.wait_ge(hw_ready, n - 2)
                            alone(pe, "pe")
                        mm(bank[3 + m % 3], sel[:, e:e + 1].broadcast_to([4 * E, P]), w_b).then_inc(wb_done, 1)
                        if e == 0:
                            if k == 0:
                                pe.wait_ge(out_ready, g * 2 + FREE)
                                alone(pe, "pe")
                            mm(bank[6 + k], eb2[:, :], w_b, stop=False)
                    if m >= SKEW:
                        k, e, slot = (m - SKEW) // E, (m - SKEW) % E, (m - SKEW) % NSLOT
                        w = ew2[:, e, :, :].rearrange("p h n -> p (h n)")
                        pe.wait_ge(hwlo_ready, n - (SKEW - 1))
                        mm(bank[6 + k], w, hw_hi[:, slot * S:(slot + 1) * S], start=False, stop=False)
                        last = mm(bank[6 + k], w, hw_lo(slot), start=False, stop=e == E - 1)
                        if e == E - 1:
                            last.then_inc(y_done, 1)
                    if m >= 2 * E + SKEW - 2:
                        k = m - (2 * E + SKEW - 2)
                        pe.wait_ge(y_copied, g * 2 + (k + 1))
                        for t in range(NT):
                            last = mm(bank[6 + k][:, t * D2:(t + 1) * D2], y_sb[:, k, t * P:(t + 1) * P], stack2)
                        last.then_inc(yt_done, 1)


def kernel(**inputs):
    import numpy as np
    import concourse.bacc as bacc
    from concourse.bass_utils import run_bass_kernel_spmd

    a = {n: np.asarray(t) for n, t in inputs.items()}
    tok = {n[7:]: t for n, t in a.items() if n.startswith("L0_tok_")}
    att = {n[8:]: t for n, t in a.items() if n.startswith("L0_attn_")}
    ffn = {n[7:]: t for n, t in a.items() if n.startswith("L0_ffn_")}

    def twice(t):
        return np.concatenate([t, t], axis=0)

    cols = np.concatenate([
        tok["b_upd"][:, None], tok["b_f"][:, None], tok["norm_g"][:, None], tok["norm_b"][:, None],
        tok["cms_ln_g"].T, tok["cms_ln_b"].T, tok["cms_b2"].T,
        tok["cms_b1"].reshape(L * F, P).T,
        twice(att["g_pre"][:, None]), twice(ffn["gamma"][:, None]), twice(ffn["beta"][:, None]),
        ffn["b1"].T, att["mem_kv"][0].reshape(P, NMEM)], axis=1)
    rows = np.concatenate([tok["head_b"], att["b_out"], att["g_out"], ffn["br"], tok["decay_param"]])

    cons = np.zeros((P, NCON), np.float32)
    lane = np.arange(P)
    cons[:, K_ID:K_ID + P] = np.eye(P)
    cons[:, K_CEN:K_CEN + P] = np.eye(P) - 1.0 / P
    cons[:, K_BLK:K_BLK + P] = lane[:, None] // DH == lane[None, :] // DH
    cons[:, K_II:K_II + D2] = lane[:, None] % D2 == np.arange(D2)
    cons[:, K_BACK8:K_BACK8 + E] = E - np.arange(E)
    cons[:, K_VOC] = lane % V
    cons[:2 * E, K_SEL:K_SEL + E] = lane[:2 * E, None] % E == np.arange(E)
    cons[2 * E:4 * E, K_HALF] = 1.0

    arrays = {
        "tokens": a["x"].reshape(B * S),
        "emb": twice(tok["emb"]),
        "w_upd": tok["W_upd"],
        "w_f": tok["W_f"],
        "w1": tok["cms_W1"].transpose(1, 0, 2).reshape(P, L * F * P),
        "w2": tok["cms_W2"].reshape(L, F, P, D).transpose(2, 0, 1, 3).reshape(P, L * F * D),
        "head_w": tok["head_W"],
        "cols": cols,
        "rows": rows,
        "constants": cons,
        "w_qkv": twice(att["w_qkv"]),
        "w_out": att["w_out"],
        "mem_v": att["mem_kv"][1].reshape(P, NMEM).T,
        "w_r": twice(ffn["Wr"]),
        "expert_w1": twice(ffn["W1"].transpose(1, 0, 2).reshape(D2, E * P)),
        "expert_w2": ffn["W2"].transpose(1, 0, 2).reshape(P, E * D2),
        "expert_b2": np.concatenate([ffn["b2"]] * 4, axis=0),
    }
    arrays = {n: np.ascontiguousarray(t) for n, t in arrays.items()}
    nc = bacc.Bacc("TRN2", target_bir_lowering=False, num_devices=1)
    args = [nc.dram_tensor("in_" + n, t.shape, mybir.dt.from_np(t.dtype), kind="ExternalInput").ap()
            for n, t in arrays.items()]
    out = nc.dram_tensor("out", (B, S, D2), fp32, kind="ExternalOutput").ap()
    build(nc, *args, out)
    r = run_bass_kernel_spmd(nc, [{"in_" + n: t for n, t in arrays.items()}], core_ids=[0])
    return r.results[0]["out"]
```

```python
import concourse.bass as bass
from concourse import mybir
from contextlib import ExitStack

fp32 = mybir.dt.float32
fp32r = mybir.dt.float32r
i32 = mybir.dt.int32
u32 = mybir.dt.uint32
ALU = mybir.AluOpType
ACT = mybir.ActivationFunctionType
AX = mybir.AxisListType

P = 128
B, S, V = 8, 512, 64
NT = S // P
D, L = 128, 4
F = 4 * D // P
D2 = 64
HEADS, DH, NMEM = 4, 32, 4
E = 8
EPS = 1e-5
FREE = 1
TURN_OWN = 20 + 4 * NT
SKEW = 3
AHEAD = 5
HALF = B // 2
W1_STEP = 6
GATES_BANK = (4, 6, 7, 4, 7, 7, 7, 7)
LOGITS_BANK = (0, 5)
HEAD_BANK = (2, 3, 6, 7)
Z_ROW = 4
W1_BANK = (5, 0, 1, 2)
TOKC = B

C_BUPD, C_BF, C_NG, C_NB = 0, 1, 2, 3
C_LNG, C_LNB, C_B2 = 4, 8, 12
C_B1 = 16
C_GPRE, C_GAMMA, C_BETA = 32, 33, 34
C_EB1 = 35
C_MK = 43
NCOL = 47
R_HEADB, R_BOUT, R_GOUT, R_BR, R_DECAY = 0, 64, 128, 192, 200
NROW = 201
K_ID, K_CEN, K_BLK, K_II, K_BACK8, K_VOC, K_SEL, K_HALF = 0, 128, 256, 384, 448, 456, 457, 465
NCON = 466


class Own:

    def __init__(self, engine, semaphore):
        self.engine, self.semaphore, self.base, self.n = engine, semaphore, 0, 0

    def inc(self, instruction):
        instruction.then_inc(self.semaphore, 1)
        self.n += 1
        return self.base + self.n

    def wait(self, value):
        self.engine.wait_ge(self.semaphore, value)

    def enter(self, i, per_turn, first=0):
        self.start, self.per_turn = self.base + self.n, per_turn
        self.base, self.n = i * per_turn + (self.start - first * per_turn), 0

    def leave(self, turns):
        assert self.n == self.per_turn, (self.n, self.per_turn)
        self.base, self.n = self.start + turns * self.per_turn, 0


def build(nc, tok_in, emb_in, wupd_in, wf_in, w1_in, w2_in, headw_in, cols_in, rows_in, cons_in,
          wqkv_in, wout_in, memv_in, wr_in, ew1_in, ew2_in, eb2_in, out_hbm):
    ctx = ExitStack()
    with ctx:
        def sb(name, shape, dt=fp32):
            return ctx.enter_context(nc.sbuf_tensor(name, shape, dt))

        def sem(name):
            return ctx.enter_context(nc.semaphore(name))

        x = sb("x", [P, B, S])
        w_all = sb("w_all", [P, L, 2, F, 2, P])
        w_cur = sb("w_cur", [P, 2, F, 2, P], fp32r)
        hid = sb("hid", [P, 2, F, S])
        hid_hi = sb("hid_hi", [P, 2, F, S], fp32r)
        hid_lo = sb("hid_lo", [P, 2, F, S], fp32r)
        xn = sb("xn", [P, 2, S])
        xn_hi = sb("xn_hi", [P, 2, S], fp32r)
        xn_lo = sb("xn_lo", [P, 2, S], fp32r)
        hh = sb("hh", [P, 2, B, NT * D2])
        cols = sb("cols", [P, NCOL])
        rows = sb("rows", [P, NROW])
        cons = sb("cons", [P, NCON])
        headw = sb("headw", [P, D2])
        b1_fold = sb("b1_fold", [P, L * F])
        stats6 = sb("stats6", [P, 4, NT, 6])
        var_in = sb("var_in", [P, 4, 3, NT])
        rstd = sb("rstd", [P, 4, NT])
        mhalf = sb("mhalf", [P, 8])
        two = sb("two", [P, NT])
        eps_row = sb("eps_row", [P, NT])
        small = sb("small", [P, 16])
        scratch = sb("scratch", [P, 8, S])
        tab_full = sb("tab_full", [P, 3, P])
        tab_hi = sb("tab_hi", [P, 3, P], fp32r)
        tab = sb("tab", [P, 3, P], fp32r)

        ident = cons[:, K_ID:K_ID + P]
        centre = cons[:, K_CEN:K_CEN + P]
        blkmask = cons[:, K_BLK:K_BLK + P]
        stack2 = cons[:, K_II:K_II + D2]
        back8 = cons[:, K_BACK8:K_BACK8 + E]
        vocab_id = cons[:, K_VOC:K_VOC + 1]

        w1_raw = hid[:, 0, :, :]
        w2_raw = hid[:, 1, :, :]
        onehot = hid_lo[:, :, :, :].rearrange("p a f s -> p (a f s)")
        emb2, embT, uT = xn[:, 0, 0:P], xn[:, 0, P:2 * P], xn[:, 0, 2 * P:3 * P]
        wupd, wf = xn[:, 1, 0:P], xn[:, 1, P:2 * P]
        toks = hh[:, :, :, :].rearrange("p a b n -> p (a b n)").bitcast(i32)

        h0 = hh[:, 0, :, :]
        h1 = hh[:, 1, :, :]

        wqkv_raw = sb("wqkv_raw", [P, 3 * P])
        wqkv_g = sb("wqkv_g", [P, 3 * P])
        wqkv = sb("wqkv", [P, 2, 3 * P], fp32r)
        wout = sb("wout", [P, D2])
        memv = sb("memv", [NMEM, P])
        mk_max = sb("mk_max", [P, 1])
        ew1_raw = sb("ew1_raw", [P, E * P])
        ew1 = sb("ew1", [P, 2, E * P], fp32r)
        ew2_raw = sb("ew2_raw", [P, E, D2])
        ew2 = sb("ew2", [P, E, 2, D2], fp32r)
        wr_raw = sb("wr_raw", [P, E])
        wr_g = sb("wr_g", [P, E])
        wr = sb("wr", [P, 2, E], fp32r)
        eb2_raw = sb("eb2_raw", [4 * E, D2])
        eb2_hi = sb("eb2_hi", [4 * E, D2], fp32r)
        eb2_lo = sb("eb2_lo", [4 * E, D2])
        eb2_mix = sb("eb2_mix", [4 * E, D2])
        eb2 = sb("eb2", [4 * E, P], fp32r)
        sel = sb("sel", [4 * E, E], fp32r)
        br_fold = sb("br_fold", [P, E])
        eb1_fold = sb("eb1_fold", [P, E])
        bout_share = sb("bout_share", [P, D2])
        tbuf = sb("tbuf", [P, 2, NT * D2])

        st0 = sb("st0", [P, B, NT, 6])
        mv0 = sb("mv0", [P, B, NT, 2])
        s0_in = sb("s0_in", [P, B, NT])
        r0_in = sb("r0_in", [P, 2, 2 * NT])
        s0 = sb("s0", [P, B, NT])
        sto = sb("sto", [P, 2, NT, 6])
        mvo = sb("mvo", [P, 2, NT, 2])
        e2o = sb("e2o", [P, 2, 2, NT])
        r2 = sb("r2", [P, 2, NT])
        st1 = sb("st1", [P, 2, NT, 6])
        mv1 = sb("mv1", [P, 2, NT, 2])
        t1s = sb("t1s", [P, 2, NT])
        s1 = sb("s1", [P, 2, NT])

        att = w_all[:, :, :, :, :, :].rearrange("p l w f h n -> p (l w f h n)")

        def att_buf(first, width):
            return att[:, first:first + 2 * width].rearrange("p (k n) -> p k n", k=2)
        KEXP = S + NMEM
        xc = att_buf(0, NT * D2)
        zf = att_buf(512, NT * D2)
        zst = att_buf(1024, NT * 2 * D2)
        kexp = att_buf(2048, KEXP)
        v_sb = att_buf(3080, S)
        q_sb = att_buf(4104, S)
        kT = att_buf(5128, S)
        qT = att_buf(6152, S)
        ctm = att_buf(7176, P)
        mx_sb = att_buf(7432, D2)
        memT = att_buf(7560, P)
        zt = xn_hi
        qmax = sb("qmax", [P, 2, NT * HEADS])
        qsum = sb("qsum", [P, 2, NT * HEADS])
        qrec = sb("qrec", [P, 2, NT * HEADS])
        kstat = sb("kstat", [P, 2, 6])

        lt_sb = xn
        R = B * NT
        zst1 = hid[:, :, :, :].rearrange("p a f s -> p (a f s)")
        lg, eq1, oh1, eq2, oh2, wgt = (scratch[:, n // 2, n % 2 * R * E:(n % 2 + 1) * R * E]
                                       .rearrange("p (r e) -> p r e", e=E) for n in range(6))
        w32 = scratch[:, 6:8, :].rearrange("p a (r n) -> p (a r) n", n=4 * E)
        top = sb("top", [P, 8, R])
        z_all = hid_hi[:, :, :, :].rearrange("p a f s -> p (a f s)")
        wT_all = hid_lo[0:4 * E, :, :, :].rearrange("p a f s -> p (a f s)")
        NSLOT = 4
        hg = hid[:, 0, :, :]
        hw = hid[:, 1, :, :]
        hw_hi = w_cur[:, :, :, :, :].rearrange("p w f h n -> p (w f h n)")
        y_sb = scratch[:, 0:2, :]
        t_sb = tbuf[:, :, :]

        def hw_lo(s):
            return (xn_hi, xn_lo)[s // 2][:, s % 2, :]

        ps = ctx.enter_context(nc.psum_tensor("ps", [P, 8, 512], fp32))
        bank = [ps[:, n, :] for n in range(8)]
        YB, TB, BB = 4, 6, 7

        ld = {n: sem("ld_" + n) for n in
              ("cons", "cols", "rows", "emb", "wupd", "wf", "w1", "w2", "headw", "wqkv", "wout",
               "memv", "wr", "ew1", "ew2", "eb2")}
        ld_tok = [sem(f"ld_tok{c}") for c in range(TOKC)]
        own_dve, own_pool = sem("own_dve"), sem("own_pool")
        mhalf_set = sem("mhalf_set")

        passed = {n: sem("passed_" + n) for n in ("act", "dve", "pool", "pe")}

        def alone(engine, name):
            engine.sem_inc(passed[name], 1)
        embt_done, embt_copied = sem("embt_done"), sem("embt_copied")
        u_done, u_ready = sem("u_done"), sem("u_ready")
        tmem_done = sem("tmem_done")
        tanh_done = sem("tanh_done")
        tables_ready = sem("tables_ready")
        w1_scaled, w1_centred = sem("w1_scaled"), sem("w1_centred")
        w1_hi_ready, w1_lo_ready = sem("w1_hi_ready"), sem("w1_lo_ready")
        w2_hi_ready, w2_lo_ready = sem("w2_hi_ready"), sem("w2_lo_ready")
        folds_done, folds_ready = sem("folds_done"), sem("folds_ready")
        late_scaled, late_hi_ready = sem("late_scaled"), sem("late_hi_ready")
        wqkv_ready, late_weights = sem("wqkv_ready"), sem("late_weights")
        onehot_ready, decay_done, looked_up = sem("onehot_ready"), sem("decay_done"), sem("looked_up")
        decay_copied, scanned, pre_ready = sem("decay_copied"), sem("scanned"), sem("pre_ready")
        x_t, stats_ready, rstd_ready = sem("x_transposed"), sem("stats_ready"), sem("rstd_ready")
        rstd_bc, normed, x_ready = sem("rstd_broadcast"), sem("normed"), sem("x_ready")
        x0_ready, memory_looked_up = sem("x0_ready"), sem("memory_looked_up")
        late_folds_done = sem("late_folds_done")
        xhi_ready, xlo_ready = sem("xhi_ready"), sem("xlo_ready")
        mm1_done, gelu_done = sem("mm1_done"), sem("gelu_done")
        hhi_ready, hlo_ready, mm2_done = sem("hhi_ready"), sem("hlo_ready"), sem("mm2_done")
        w1_loaded = [sem(f"w1_loaded{f}") for f in range(F)]
        w2_loaded = sem("w2_loaded")
        head_done, h0_ready, mv0_ready = sem("head_done"), sem("h0_ready"), sem("mv0_ready")
        s0_ready = sem("s0_ready")
        z_ready, zhi_ready, zlo_ready = sem("z_ready"), sem("zhi_ready"), sem("zlo_ready")
        res_ready = sem("residual_ready")
        z_t, zt_ready = sem("z_transposed"), sem("zt_ready")
        k_done, qv_done = sem("k_done"), sem("qv_done")
        kmax_ready, kexp_ready, v_ready = sem("kmax_ready"), sem("kexp_ready"), sem("v_ready")
        qsub_ready, qexp_ready, qn_ready = sem("qsub_ready"), sem("qexp_ready"), sem("qn_ready")
        k_t, kt_ready, q_t, qt_ready = sem("k_t"), sem("kt_ready"), sem("q_t"), sem("qt_ready")
        ctx_done, ctm_ready, m_done, m_ready = (sem("ctx_done"), sem("ctm_ready"), sem("m_done"),
                                                sem("m_ready"))
        o_done, o_ready, mvo_ready, r2_ready = (sem("o_done"), sem("o_ready"), sem("mvo_ready"),
                                                sem("r2_ready"))
        h1_ready, mv1_ready, s1_ready = sem("h1_ready"), sem("mv1_ready"), sem("s1_ready")
        ez_ready, ezhi_ready, ezlo_ready = sem("ez_ready"), sem("ezhi_ready"), sem("ezlo_ready")
        ez_t, eza_ready = sem("ez_t"), sem("eza_ready")
        lt_done, lt_copied = sem("lt_done"), sem("lt_copied")
        router_done, gap_ready, gate_tanh = sem("router_done"), sem("gap_ready"), sem("gate_tanh")
        gates_ready, gates_t, gates_copied = sem("gates_ready"), sem("gates_t"), sem("gates_copied")
        e1_done, wb_done, eg_done = sem("e1_done"), sem("wb_done"), sem("eg_done")
        hw_ready, hwhi_ready, hwlo_ready = sem("hw_ready"), sem("hwhi_ready"), sem("hwlo_ready")
        e2_done, y_done, y_copied = sem("e2_done"), sem("y_done"), sem("y_copied")
        yt_done, out_ready = sem("yt_done"), sem("out_ready")
        stored = [sem("stored0"), sem("stored1")]

        def per_tile(ap, width):
            return ap.unsqueeze(2).broadcast_to([P, NT, width])

        def tiles(ap, width=D2):
            return ap.rearrange("p (t c) -> p t c", c=width)

        def at(buf, b):
            return buf[:, bass.ds(b, 1), :].rearrange("p o n -> p (o n)")

        def at_stat(buf, b, c):
            return buf[:, bass.ds(b, 1), :, c].rearrange("p o t -> p (o t)")

        def row64(first):
            return rows[:, first:first + D2].unsqueeze(1).broadcast_to([P, NT, D2])

        def qv_view(k):
            both = ps[:, 4 * k + 2:4 * k + 4, :].rearrange("p a n -> p (a n)")
            return both.rearrange("p (t w c) -> p t w c", t=NT, w=2)

        block = ctx.enter_context(nc.Block())

        @block.sync
        def _(sp):
            def load(name, dst, src):
                sp.dma_start(dst, src).then_inc(ld[name], 16)

            def load_tokens(c):
                piece = slice(c * (B * S // TOKC), (c + 1) * (B * S // TOKC))
                sp.dma_start(toks[:, piece], tok_in[piece].partition_broadcast(P)).then_inc(ld_tok[c], 16)

            load("cons", cons[:, :], cons_in)
            load("emb", emb2, emb_in)
            load("wupd", wupd, wupd_in)
            load("cols", cols[:, :], cols_in)
            load("rows", rows[:, :], rows_in.partition_broadcast(P))
            load("wf", wf, wf_in)
            for c in range(3):
                load_tokens(c)
            load("w1", w1_raw.rearrange("p l n -> p (l n)"), w1_in)
            for c in range(3, 5):
                load_tokens(c)
            load("w2", w2_raw.rearrange("p l n -> p (l n)"), w2_in)
            for c in range(5, TOKC):
                load_tokens(c)
            load("headw", headw[:, :], headw_in)
            load("wqkv", wqkv_raw[:, :], wqkv_in)
            load("wout", wout[:, :], wout_in)
            load("memv", memv[:, :], memv_in)
            load("wr", wr_raw[:, :], wr_in)
            load("ew1", ew1_raw[:, :], ew1_in)
            load("ew2", ew2_raw[:, :, :].rearrange("p e n -> p (e n)"), ew2_in)
            load("eb2", eb2_raw[:, :], eb2_in)

            for n in (1, L):
                sp.wait_ge(w1_hi_ready, n)
                sp.wait_ge(w1_lo_ready, n)
                sp.wait_ge(w2_hi_ready, n)
                sp.wait_ge(w2_lo_ready, n)
                if n == 1:
                    for f in range(F):
                        sp.dma_start(w_cur[:, 0, f, :, :].bitcast(fp32), w_all[:, 0, 0, f, :, :]).then_inc(w1_loaded[f], 16)
                    sp.dma_start(w_cur[:, 1, :, :, :].bitcast(fp32), w_all[:, 0, 1, :, :, :]).then_inc(w2_loaded, 16)
            with sp.Fori(1, L) as l:
                for f in range(F):
                    sp.wait_ge(mm1_done, l * (B * F) + (f + 1 - F))
                    sp.dma_start(w_cur[:, 0, f, :, :].bitcast(fp32),
                                 w_all[:, bass.ds(l, 1), 0, f, :, :]).then_inc(w1_loaded[f], 16)
                sp.wait_ge(mm2_done, l * B)
                sp.dma_start(w_cur[:, 1, :, :, :].bitcast(fp32),
                             w_all[:, bass.ds(l, 1), 1, :, :, :]).then_inc(w2_loaded, 16)

            with sp.Fori(0, B // 2) as g:
                for k in range(2):
                    sp.wait_ge(out_ready, g * 2 + (k + 1) + FREE)
                    dst = out_hbm[bass.ds(g * 2 + k, 1), :, :].rearrange("o (t p) c -> p (o t) c", p=P)
                    src = h1[:, bass.ds(g * 2 + k, 1), :].rearrange("p o n -> p (o n)")
                    sp.dma_start(dst, tiles(src)).then_inc(stored[k], 16)
            sp.wait_ge(stored[0], 16 * (B // 2))
            sp.wait_ge(stored[1], 16 * (B // 2))

        @block.gpsimd
        def _(pool):
            own = Own(pool, own_pool)
            pool.memset(two[:, :], 2.0)
            pool.memset(eps_row[:, :], EPS)
            pool.memset(mhalf[:, :], -0.5).then_inc(mhalf_set, 1)

            def w2_lo(l):
                pool.wait_ge(w2_hi_ready, l + 1)
                pool.tensor_tensor(w_all[:, l, 1, :, 1, :].bitcast(fp32r),
                                   w2_raw[:, l, :].rearrange("p (f n) -> p f n", f=F),
                                   w_all[:, l, 1, :, 0, :], ALU.subtract).then_inc(w2_lo_ready, 1)

            def inverse_root_of_pair(n):
                pool.wait_ge(stats_ready, n + 2 + FREE)
                st, vi = stats6[:, n % 4:n % 4 + 2, :, :], var_in[:, n % 4:n % 4 + 2, :, :]
                own.inc(pool.tensor_tensor(vi[:, :, 0, :], st[:, :, :, 1], st[:, :, :, 4], ALU.subtract))
                v = own.inc(pool.tensor_tensor(vi[:, :, 1, :], st[:, :, :, 2], st[:, :, :, 5], ALU.add))
                own.wait(v)
                v = own.inc(pool.tensor_scalar(vi[:, :, 1, :], vi[:, :, 1, :], 4.0 / D, 4.0 * EPS, ALU.mult, ALU.add))
                own.inc(pool.tensor_tensor(vi[:, :, 0, :], vi[:, :, 0, :], vi[:, :, 0, :], ALU.mult))
                own.wait(v + 1)
                v = own.inc(pool.tensor_tensor(vi[:, :, 2, :], vi[:, :, 0, :], vi[:, :, 1, :], ALU.add))
                own.wait(v)
                half = mhalf[:, :].rearrange("p (k t) -> p k t", t=NT)
                v = own.inc(pool.tensor_tensor(vi[:, :, 0, :], vi[:, :, 2, :], half, ALU.pow))
                own.wait(v)
                twos = two[:, :].unsqueeze(1).broadcast_to([P, 2, NT])
                pool.tensor_tensor(rstd[:, n % 4:n % 4 + 2, :], vi[:, :, 0, :], twos, ALU.mult).then_inc(rstd_ready, 2)

            def inverse_root_of_row(n, slot):
                pool.wait_ge(stats_ready, n + 1 + FREE)
                st, vi = stats6[:, slot, :, :], var_in[:, slot, :, :]
                own.inc(pool.tensor_tensor(vi[:, 0, :], st[:, :, 1], st[:, :, 4], ALU.subtract))
                v = own.inc(pool.tensor_tensor(vi[:, 1, :], st[:, :, 2], st[:, :, 5], ALU.add))
                own.wait(v)
                alone(pool, "pool")
                v = own.inc(pool.tensor_scalar(vi[:, 1, :], vi[:, 1, :], 4.0 / D, 4.0 * EPS, ALU.mult, ALU.add))
                own.inc(pool.tensor_tensor(vi[:, 0, :], vi[:, 0, :], vi[:, 0, :], ALU.mult))
                own.wait(v + 1)
                v = own.inc(pool.tensor_tensor(vi[:, 2, :], vi[:, 0, :], vi[:, 1, :], ALU.add))
                own.wait(v)
                v = own.inc(pool.tensor_tensor(vi[:, 0, :], vi[:, 2, :], mhalf[:, 0:NT], ALU.pow))
                own.wait(v)
                pool.tensor_tensor(rstd[:, slot, :], vi[:, 0, :], two[:, 0:NT], ALU.mult).then_inc(rstd_ready, 1)

            pool.wait_ge(mhalf_set, 1)
            inverse_root_of_pair(0)
            inverse_root_of_pair(2)
            pool.wait_ge(ld["w2"], 16)
            w2_lo(0)
            inverse_root_of_pair(4)
            w2_lo(1)
            w2_lo(2)
            inverse_root_of_pair(6)
            w2_lo(3)
            for n in range(2):
                inverse_root_of_row(B + n, n % 4)
            with pool.Fori(0, L) as l:
                own.enter(l, B * 6)
                for i in range(B):
                    inverse_root_of_row(l * B + (B + i + 2), (i + 2) % 4)
                own.leave(L)

            for b in range(B):
                pool.wait_ge(mv0_ready, b + 1)
                v = own.inc(pool.tensor_scalar(s0_in[:, b, :], mv0[:, b, :, 1], EPS / 64e24, None, ALU.max))
                own.wait(v)
                pool.tensor_tensor(s0[:, b, :], s0_in[:, b, :], mhalf[:, 0:NT], ALU.pow).then_inc(s0_ready, 1)

            def residual_base(b, k):
                v = own.inc(pool.tensor_tensor(r0_in[:, k, 0:NT], at_stat(mv0, b, 1), eps_row[:, 0:NT], ALU.add))
                own.wait(v)
                own.inc(pool.tensor_tensor(r0_in[:, k, NT:2 * NT], r0_in[:, k, 0:NT], mhalf[:, 0:NT], ALU.pow))
                v = own.inc(pool.tensor_tensor(tiles(xc[:, k, :]), tiles(at(h0, b)), per_tile(at_stat(mv0, b, 0), D2),
                                               ALU.subtract))
                own.wait(v)
                v = own.inc(pool.tensor_tensor(tiles(xc[:, k, :]), tiles(xc[:, k, :]),
                                               per_tile(r0_in[:, k, NT:2 * NT], D2), ALU.mult))
                pool.wait_ge(z_ready, b + 1)
                alone(pool, "pool")
                own.wait(v)
                alone(pool, "pool")
                pool.tensor_tensor(at(h0, b), at(h0, b), xc[:, k, :], ALU.add).then_inc(res_ready, 1)

            def output_norm(b, k):
                pool.wait_ge(mvo_ready, b + 1)
                v = own.inc(pool.tensor_tensor(e2o[:, k, 0, :], mvo[:, k, :, 0], mvo[:, k, :, 0], ALU.mult))
                own.wait(v)
                v = own.inc(pool.tensor_tensor(e2o[:, k, 1, :], e2o[:, k, 0, :], mvo[:, k, :, 1], ALU.add))
                own.wait(v)
                alone(pool, "pool")
                v = own.inc(pool.tensor_scalar(e2o[:, k, 0, :], e2o[:, k, 1, :], 1e-24 / D2, None, ALU.max))
                own.wait(v)
                pool.tensor_tensor(r2[:, k, :], e2o[:, k, 0, :], mhalf[:, 0:NT], ALU.pow).then_inc(r2_ready, 1)

            def expert_norm(b, k):
                pool.wait_ge(mv1_ready, b + 1)
                alone(pool, "pool")
                v = own.inc(pool.tensor_scalar(t1s[:, k, :], mv1[:, k, :, 1], 1.0 + EPS, EPS * EPS, ALU.mult, ALU.add))
                own.wait(v)
                pool.tensor_tensor(s1[:, k, :], t1s[:, k, :], mhalf[:, 0:NT], ALU.pow).then_inc(s1_ready, 1)

            def pool_turn(g, more):
                for k in range(2):
                    output_norm(g * 2 + k, k)
                for k in range(2):
                    expert_norm(g * 2 + k, k)
                if more:
                    for k in range(2):
                        residual_base(g * 2 + (k + 2), k)

            for k in range(2):
                residual_base(k, k)
            with pool.Fori(0, B // 2 - 1) as g:
                own.enter(g, 2 * 8)
                pool_turn(g, True)
                own.leave(B // 2 - 1)
            pool_turn(B // 2 - 1, False)

        @block.scalar
        def _(act):
            act.preload_act_table(ACT.Gelu)
            act.wait_ge(ld["rows"], 16)
            act.activation(small[:, 0:1], rows[:, R_DECAY:R_DECAY + 1], ACT.Tanh, scale=0.5).then_inc(tanh_done, 1)

            def decays(n):
                act.wait_ge(decay_done, n + 1)
                if n >= 2:
                    act.wait_ge(scanned, n - 1 + FREE)
                act.activation(scratch[:, 2 + n % 2, :], bank[n % 2], ACT.Copy).then_inc(decay_copied, 1)

            def affine(n):
                act.wait_ge(normed, n + 1 + FREE)
                act.activation(x[:, n, :], x[:, n, :], ACT.Identity, bias=cols[:, C_NB:C_NB + 1],
                               scale=cols[:, C_NG:C_NG + 1]).then_inc(x0_ready, 1)

            def w1_in(l):
                act.activation(scratch[:, 4 + l, :], w1_raw[:, l, :], ACT.Copy,
                               scale=cols[:, C_LNG + l:C_LNG + l + 1]).then_inc(w1_scaled, 1)

            def w2_hi(l):
                act.activation(w_all[:, l, 1, :, 0, :].bitcast(fp32r),
                               w2_raw[:, l, :].rearrange("p (f n) -> p f n", f=F), ACT.Copy).then_inc(w2_hi_ready, 1)

            def w1_hi(l):
                act.wait_ge(w1_centred, l + 1)
                act.activation(w_all[:, l, 0, :, 0, :].bitcast(fp32r),
                               bank[W1_BANK[l]].rearrange("p (f n) -> p f n", f=F),
                               ACT.Copy).then_inc(w1_hi_ready, 1)

            act.wait_ge(ld["cols"], 16)
            for n in range(B + 4):
                if n < B:
                    decays(n)
                if n == 4:
                    act.wait_ge(ld["w1"], 16)
                    act.wait_ge(ld["w2"], 16)
                if n >= 4:
                    affine(n - 4)
                if n >= W1_STEP + 1 and n - W1_STEP - 1 < L:
                    w1_hi(n - W1_STEP - 1)
                if n >= W1_STEP - 1 and n - W1_STEP + 1 < L:
                    w1_in(n - W1_STEP + 1)
                if n >= 4 and n - 4 < L:
                    w2_hi(n - 4)
            act.wait_ge(folds_ready, 1)

            def xhi(j, i):
                act.wait_ge(normed, j + (B + 1) + FREE)
                act.activation(xn_hi[:, i % 2, :], xn[:, i % 2, :], ACT.Copy).then_inc(xhi_ready, 1)

            xhi(0, 0)
            with act.Fori(0, L) as l:
                for i in range(B):
                    j = l * B + i
                    if i == 0:
                        xhi(j + 1, i + 1)
                    for f in range(F):
                        act.wait_ge(mm1_done, j * F + (f + 1))
                        alone(act, "act")
                        act.activation(hid[:, i % 2, f, :], bank[f], ACT.Gelu,
                                       bias=b1_fold[:, bass.ds(l * F + f, 1)]).then_inc(gelu_done, 1)
                        if f % 2:
                            act.wait_ge(gelu_done, j * F + (f + 1))
                            act.activation(hid_hi[:, i % 2, f - 1:f + 1, :], hid[:, i % 2, f - 1:f + 1, :],
                                           ACT.Copy).then_inc(hhi_ready, 1)
                        if f == 1 and 0 < i < B - 1:
                            xhi(j + 1, i + 1)
                xhi(l * B + B, 0)

            def z_hi(b, k):
                act.wait_ge(z_ready, b + 1)
                act.activation(tiles(zst[:, k, :], 2 * D2)[:, :, 0:D2].bitcast(fp32r), tiles(zf[:, k, :]),
                               ACT.Copy).then_inc(zhi_ready, 1)

            def z_turned(b, k):
                act.wait_ge(z_t, b + 1)
                act.activation(zt[:, k, :], bank[4 * k], ACT.Copy).then_inc(zt_ready, 1)

            def exp_k(b, k):
                act.wait_ge(kmax_ready, b + 1)
                act.activation(kexp[:, k, 0:S], bank[4 * k + 1], ACT.Exp, bias=kstat[:, k, 1:2],
                               accum_out=kstat[:, k, 2:3])
                act.activation(kexp[:, k, S:S + NMEM], cols[:, C_MK:C_MK + NMEM], ACT.Exp,
                               bias=kstat[:, k, 1:2], accum_out=kstat[:, k, 3:4]).then_inc(kexp_ready, 1)

            def exp_q(b, k):
                act.wait_ge(qsub_ready, b + 1)
                act.activation(q_sb[:, k, :], q_sb[:, k, :], ACT.Exp).then_inc(qexp_ready, 1)

            def copy_v(b, k):
                act.wait_ge(qsub_ready, b + 1)
                act.activation(tiles(v_sb[:, k, :], P), qv_view(k)[:, :, 1, :], ACT.Copy).then_inc(v_ready, 1)

            def k_turned(b, k):
                act.wait_ge(k_t, b + 1)
                act.activation(kT[:, k, :], bank[4 * k], ACT.Copy)
                act.activation(memT[0:NMEM, k, :], bank[4 * k + 1][0:NMEM, 0:P], ACT.Copy).then_inc(kt_ready, 1)

            def q_turned(b, k):
                act.wait_ge(q_t, b + 1)
                act.activation(qT[:, k, :], bank[4 * k], ACT.Copy).then_inc(qt_ready, 1)

            def attended(b, k):
                act.wait_ge(o_done, b + 1)
                alone(act, "act")
                act.activation(at(h1, b), bank[4 * k + 1][:, 2 * P:4 * P], ACT.Copy).then_inc(o_ready, 1)

            def ez_hi(b, k):
                act.wait_ge(ez_ready, b + 1)
                alone(act, "act")
                act.activation(tiles(zst1[:, bass.ds(b * S, S)], 2 * D2)[:, :, 0:D2].bitcast(fp32r),
                               tiles(zf[:, k, :]), ACT.Copy).then_inc(ezhi_ready, 1)

            def act_pair(steps, b):
                for step in steps:
                    for k in range(2):
                        step(b + k, k)

            def act_turn(g, more, before):
                now, nxt, prev = g * 2, g * 2 + 2, g * 2 - 2
                if more:
                    act_pair((z_hi,), nxt)
                act_pair((q_turned, attended), now)
                if before:
                    act_pair((ez_hi,), prev)
                if more:
                    act_pair((z_turned, exp_k, k_turned, exp_q, copy_v), nxt)

            act.preload_act_table(ACT.Exp)
            for n in ("wqkv", "wr", "ew1", "ew2", "eb2"):
                act.wait_ge(ld[n], 16)
            act.wait_ge(late_folds_done, 1)
            for dst, src, gain in ((wqkv_g[:, :], wqkv_raw[:, :], C_GPRE), (wr_g[:, :], wr_raw[:, :], C_GAMMA),
                                   (ew1_raw[:, :], ew1_raw[:, :], C_GAMMA)):
                act.activation(dst, src, ACT.Copy, scale=cols[:, gain:gain + 1]).then_inc(late_scaled, 1)
            act.activation(ew2[:, :, 0, :], ew2_raw[:, :, :], ACT.Copy)
            act.activation(eb2_hi[:, :], eb2_raw[:, :], ACT.Copy)
            act.wait_ge(late_scaled, 3)
            act.activation(wqkv[:, 0, :], wqkv_g[:, :], ACT.Copy).then_inc(late_hi_ready, 1)
            act.activation(wr[:, 0, :], wr_g[:, :], ACT.Copy)
            act.activation(ew1[:, 0, :], ew1_raw[:, :], ACT.Copy).then_inc(late_hi_ready, 1)
            act_pair((z_hi, z_turned, exp_k, k_turned, exp_q, copy_v), 0)
            act_turn(0, True, False)
            with act.Fori(1, B // 2 - 1) as g:
                act_turn(g, True, True)
            def expert_z_turned(b):
                act.wait_ge(ez_t, b + 1)
                act.activation(z_all[:, b * S:(b + 1) * S], bank[2 + b % 2], ACT.Copy).then_inc(eza_ready, 1)

            def logits_out(b):
                act.wait_ge(lt_done, b + 1)
                if b >= 2:
                    act.wait_ge(router_done, b - 1)
                act.activation(lt_sb[0:2 * E, b % 2, :], bank[6 + b % 2][0:2 * E, :], ACT.Copy).then_inc(lt_copied, 1)

            def gate(half):
                r = slice(half * R // 2, (half + 1) * R // 2)
                act.wait_ge(gap_ready, half + 1)
                act.activation(top[:, 5, r], top[:, 4, r], ACT.Tanh, scale=0.5).then_inc(gate_tanh, 1)

            act_pair((q_turned,), B - 2)
            for b in (0, 1):
                expert_z_turned(b)
            act_pair((attended,), B - 2)
            for b in (0, 1):
                logits_out(b)
            act_pair((ez_hi,), B - 4)
            for b in (2, 3):
                expert_z_turned(b)
            for b in (2, 3):
                logits_out(b)
            act.preload_act_table(ACT.Gelu)
            for step in (expert_z_turned, logits_out):
                for b in (HALF, HALF + 1):
                    step(b)
            gate(0)
            act_pair((ez_hi,), B - 2)
            for step in (expert_z_turned, logits_out):
                for b in (HALF + 2, HALF + 3):
                    step(b)

            def copy_gates(b):
                act.wait_ge(gates_t, b + 1)
                act.activation(wT_all[:, b * S:(b + 1) * S], bank[GATES_BANK[b]][0:4 * E, :],
                               ACT.Copy).then_inc(gates_copied, 1)

            def copy_sum(g, k):
                act.wait_ge(y_done, g * 2 + (k + 1))
                act.activation(y_sb[:, k, :], bank[6 + k], ACT.Copy).then_inc(y_copied, 1)

            def gelu(g, m):
                act.wait_ge(e1_done, g * (2 * E) + (m + 1))
                act.activation(hg[:, m % NSLOT, :], bank[m % 4], ACT.Gelu,
                               bias=eb1_fold[:, m % E:m % E + 1]).then_inc(eg_done, 1)

            def hidden_hi(g, m):
                slot = m % NSLOT
                act.wait_ge(hw_ready, g * (2 * E) + (m + 1))
                act.activation(hw_hi[:, slot * S:(slot + 1) * S], hw[:, slot, :], ACT.Copy).then_inc(hwhi_ready, 1)

            def act_job(g, m, more):
                if m < 2 * E or more:
                    gelu(g, m)
                if m <= 2 * E or more:
                    hidden_hi(g, m - 1)

            def act_experts(g, more):
                for m in range(AHEAD, 2 * E + AHEAD):
                    act_job(g, m, more)
                    if m == E + 4:
                        copy_sum(g, 0)
                    if m == 2 * E + 3:
                        copy_sum(g, 1)

            for b in range(HALF):
                copy_gates(b)
            gate(1)
            for m in range(4):
                gelu(0, m)
            hidden_hi(0, 0)
            gelu(0, 4)
            hidden_hi(0, 1)
            copy_gates(HALF)
            hidden_hi(0, 2)
            copy_gates(HALF + 1)
            hidden_hi(0, 3)
            copy_gates(HALF + 2)
            copy_gates(HALF + 3)
            with act.Fori(0, B // 2 - 1) as g:
                act_experts(g, True)
            act_experts(B // 2 - 1, False)

        @block.vector
        def _(dve):
            own = Own(dve, own_dve)
            for free in (stats_ready, normed, scanned, out_ready):
                dve.sem_inc(free, FREE)
            dve.wait_ge(embt_done, 1)
            dve.tensor_copy(embT, bank[6][:, 0:P]).then_inc(embt_copied, 1)
            dve.wait_ge(ld["cols"], 16)
            dve.wait_ge(u_done, 1)
            v = own.inc(dve.tensor_scalar(uT, bank[7][:, 0:P], cols[:, C_BUPD:C_BUPD + 1], None, ALU.add))
            own.wait(v)
            dve.memset(xn[:, 0, 2 * P:2 * P + 1], 0.0).then_inc(u_ready, 1)
            dve.memset(xn[:, 0, 2 * P + V:2 * P + V + 1], 0.0).then_inc(u_ready, 1)
            dve.wait_ge(tanh_done, 1)
            dve.wait_ge(ld["cons"], 16)
            own.inc(dve.tensor_scalar(small[:, 1:2], small[:, 0:1], 0.5, 0.5, ALU.mult, ALU.add))
            own.inc(dve.tensor_scalar(small[:, 2:3], small[:, 0:1], -0.5, 0.5, ALU.mult, ALU.add))
            v = own.inc(dve.tensor_scalar(small[:, 3:4], vocab_id, 0.0, None, ALU.is_equal))
            own.wait(v)
            v = own.inc(dve.scalar_tensor_tensor(small[:, 4:5], small[:, 2:3], small[:, 3:4], small[:, 1:2],
                                                 ALU.mult, ALU.add))
            own.wait(v)
            own.inc(dve.tensor_copy(tab_full[:, 0, :], small[:, 4:5].broadcast_to([P, P])))
            dve.wait_ge(ld["emb"], 16)
            own.inc(dve.reduce_sum(small[:, 5:6], emb2, AX.X))
            dve.wait_ge(tmem_done, 1)
            own.inc(dve.tensor_copy(small[:, 9:10], bank[4][:, 0:1]))
            v = own.inc(dve.reduce_sum(small[:, 6:7], bank[5][:, 0:P], AX.X))
            own.wait(v)
            v = own.inc(dve.tensor_scalar(small[:, 7:9], small[:, 5:7], -1.0 / D, None, ALU.mult))
            own.wait(v)
            own.inc(dve.tensor_scalar(tab_full[:, 2, :], emb2, small[:, 7:8], None, ALU.add))
            v = own.inc(dve.tensor_scalar(tab_full[:, 1, :], bank[5][:, 0:P], small[:, 8:9], None, ALU.add))
            own.wait(v)
            own.inc(dve.tensor_copy(tab[0:V], tab_full[0:V]))
            v = own.inc(dve.tensor_copy(tab_hi[V:P], tab_full[V:P]))
            own.wait(v)
            dve.tensor_tensor(tab[V:P], tab_full[V:P], tab_hi[V:P].bitcast(fp32), ALU.subtract).then_inc(tables_ready, 1)

            def row_stats(slot, waited):
                dve.wait_ge(x_t, waited)
                for t in range(NT):
                    last = dve.bn_stats(stats6[:, slot, t, :], bank[TB][:, t * P:(t + 1) * P])
                last.then_inc(stats_ready, 1)

            def one_hot(n):
                dve.wait_ge(ld_tok[n], 16)
                dve.tensor_scalar(onehot[:, n * S:(n + 1) * S], toks[:, n * S:(n + 1) * S], vocab_id, None,
                                  ALU.is_equal).then_inc(onehot_ready, 1)

            def scan(n):
                dve.wait_ge(decay_copied, n + 1)
                dve.wait_ge(memory_looked_up, n + 1)
                dve.tensor_tensor_scan(x[:, n, :], scratch[:, 2 + n % 2, :], bank[2 + n % 2], 0.0,
                                       ALU.mult, ALU.add).then_inc(scanned, 1)

            def pre(n):
                dve.wait_ge(scanned, n + 1 + FREE)
                dve.wait_ge(looked_up, n + 1)
                dve.scalar_tensor_tensor(x[:, n, :], x[:, n, :], small[:, 9:10],
                                         bank[4], ALU.add, ALU.add).then_inc(pre_ready, 1)

            def norm(n):
                dve.wait_ge(rstd_bc, n + 1)
                dve.tensor_tensor(x[:, n, :], x[:, n, :], bank[BB],
                                  ALU.mult).then_inc(normed, 1)

            def w1_lo(l):
                dve.wait_ge(w1_hi_ready, l + 1)
                dve.tensor_tensor(w_all[:, l, 0, :, 1, :].bitcast(fp32r),
                                  bank[W1_BANK[l]].rearrange("p (f n) -> p f n", f=F),
                                  w_all[:, l, 0, :, 0, :], ALU.subtract).then_inc(w1_lo_ready, 1)

            one_hot(0)
            one_hot(1)
            for n in range(B + 4):
                if n + 2 < B:
                    one_hot(n + 2)
                if n < B:
                    scan(n)
                if 1 <= n <= B:
                    row_stats((n - 1) % 4, n)
                if n < B:
                    pre(n)
                if n >= 4:
                    norm(n - 4)
                if n == B + 1:
                    row_stats(0, B + 1)
                    row_stats(1, B + 2)
                if n == W1_STEP:
                    dve.wait_ge(folds_done, 1)
                    dve.tensor_tensor(b1_fold[:, :], bank[5][:, 0:L * F], cols[:, C_B1:C_B1 + L * F],
                                      ALU.add).then_inc(folds_ready, 1)
                if n > W1_STEP and n - W1_STEP - 1 < L:
                    w1_lo(n - W1_STEP - 1)

            def norm_x(j, i):
                dve.wait_ge(rstd_bc, j + (B + 1))
                dve.tensor_tensor(xn[:, i % 2, :], x[:, i % B, :], bank[BB], ALU.mult).then_inc(normed, 1)

            def x_lo(j, i):
                dve.wait_ge(xhi_ready, j + 1)
                dve.tensor_tensor(xn_lo[:, i % 2, :], xn[:, i % 2, :], xn_hi[:, i % 2, :].bitcast(fp32),
                                  ALU.subtract).then_inc(xlo_ready, 1)

            def h_lo(j, i, p):
                dve.wait_ge(hhi_ready, j * 2 + (p + 1))
                dve.tensor_tensor(hid_lo[:, i % 2, 2 * p:2 * p + 2, :], hid[:, i % 2, 2 * p:2 * p + 2, :],
                                  hid_hi[:, i % 2, 2 * p:2 * p + 2, :].bitcast(fp32),
                                  ALU.subtract).then_inc(hlo_ready, 1)

            def residual(j, i, l):
                dve.wait_ge(mm2_done, j + 1)
                dve.scalar_tensor_tensor(x[:, i, :], bank[YB + i % 2], cols[:, bass.ds(l + C_B2, 1)],
                                         x[:, i, :], ALU.add, ALU.add).then_inc(x_ready, 1)

            norm_x(0, 0)
            x_lo(0, 0)
            dve.wait_ge(x0_ready, B)
            dve.sem_inc(x_ready, B)
            with dve.Fori(0, L) as l:
                for i in range(B):
                    j = l * B + i
                    if i < B - 1:
                        row_stats((i + 2) % 4, j + (B + 3))
                        if i == 1:
                            h_lo(j - 1, 0, 0)
                        norm_x(j + 1, i + 1)
                        if i == 1:
                            h_lo(j - 1, 0, 1)
                    if i >= 2:
                        residual(j - 2, i - 2, l)
                    if i == 0:
                        x_lo(j + 1, i + 1)
                    else:
                        h_lo(j, i, 0)
                        if i < B - 1:
                            x_lo(j + 1, i + 1)
                        h_lo(j, i, 1)
                j = l * B + B
                row_stats(1, j + (B + 2))
                norm_x(j, B)
                residual(j - 2, B - 2, l)
                x_lo(j, B)
                residual(j - 1, B - 1, l)

            dve.wait_ge(late_folds_done, 1)
            own.inc(dve.tensor_tensor(eb1_fold[:, :], bank[0][:, 0:E], cols[:, C_EB1:C_EB1 + E], ALU.add))
            own.inc(dve.tensor_tensor(br_fold[:, :], bank[0][:, E:2 * E], rows[:, R_BR:R_BR + E], ALU.add))
            own.inc(dve.tensor_copy(sel[:, :], cons[0:4 * E, K_SEL:K_SEL + E]))
            own.inc(dve.tensor_scalar(bout_share[:, :], rows[:, R_BOUT:R_BOUT + D2], 1.0 / HEADS, None, ALU.mult))
            own.inc(dve.reduce_max(mk_max[:, :], cols[:, C_MK:C_MK + NMEM], AX.X))
            own.inc(dve.memset(eb2[:, D2:P].bitcast(fp32), 0.0))

            def qkv_lo():
                dve.wait_ge(late_hi_ready, 1)
                dve.tensor_tensor(wqkv[:, 1, :], wqkv_g[:, :], wqkv[:, 0, :].bitcast(fp32),
                                  ALU.subtract).then_inc(wqkv_ready, 1)

            def expert_lo():
                dve.wait_ge(late_hi_ready, 2)
                own.inc(dve.tensor_tensor(wr[:, 1, :], wr_g[:, :], wr[:, 0, :].bitcast(fp32), ALU.subtract))
                v = own.inc(dve.tensor_tensor(eb2_lo[:, :], eb2_raw[:, :], eb2_hi[:, :].bitcast(fp32), ALU.subtract))
                own.inc(dve.tensor_tensor(ew2[:, :, 1, :], ew2_raw[:, :, :], ew2[:, :, 0, :].bitcast(fp32), ALU.subtract))
                half = cons[0:4 * E, K_HALF:K_HALF + 1]
                own.wait(v)
                v = own.inc(dve.tensor_tensor(eb2_mix[:, :], eb2_lo[:, :], eb2_hi[:, :].bitcast(fp32), ALU.subtract))
                own.wait(v)
                v = own.inc(dve.tensor_scalar(eb2_mix[:, :], eb2_mix[:, :], half, None, ALU.mult))
                own.wait(v)
                own.inc(dve.tensor_tensor(eb2[:, 0:D2], eb2_mix[:, :], eb2_hi[:, :].bitcast(fp32), ALU.add))
                dve.tensor_tensor(ew1[:, 1, :], ew1_raw[:, :], ew1[:, 0, :].bitcast(fp32),
                                  ALU.subtract).then_inc(late_weights, 1)

            def row_moments(src, st, out):
                for t in range(NT):
                    v = own.inc(dve.bn_stats(st[:, t, :], src[:, t, :]))
                own.wait(v)
                alone(dve, "dve")
                for t in range(NT):
                    last = dve.bn_aggr(out[:, t, :], st[:, t, :])
                return last

            def head_moments(b):
                dve.wait_ge(h0_ready, b + 1)
                row_moments(tiles(h0[:, b, :]), st0[:, b, :, :], mv0[:, b, :, :]).then_inc(mv0_ready, 1)


            def centred(b, k):
                own.inc(dve.tensor_tensor(tiles(t_sb[:, k, :]), tiles(at(h0, b)), per_tile(at_stat(mv0, b, 0), D2),
                                          ALU.subtract))

            def z_of(b, k, v):
                own.wait(v)
                dve.tensor_tensor(tiles(zf[:, k, :]), tiles(t_sb[:, k, :]), per_tile(at(s0, b), D2),
                                  ALU.mult).then_inc(z_ready, 1)

            def z_lo(b, k):
                dve.wait_ge(zhi_ready, b + 1)
                st = tiles(zst[:, k, :], 2 * D2)
                dve.tensor_tensor(st[:, :, D2:2 * D2].bitcast(fp32r), tiles(zf[:, k, :]), st[:, :, 0:D2],
                                  ALU.subtract).then_inc(zlo_ready, 1)

            def max_k(b, k):
                dve.wait_ge(k_done, b + 1)
                own.inc(dve.reduce_max(kstat[:, k, 0:1], bank[4 * k + 1], AX.X))

            def negated(b, k, v):
                own.wait(v)
                dve.tensor_scalar(kstat[:, k, 1:2], kstat[:, k, 0:1], mk_max[:, 0:1], -1.0, ALU.max,
                                  ALU.mult).then_inc(kmax_ready, 1)

            def q_heads(k):
                return qv_view(k)[:, :, 0, :].rearrange("p t (h d) -> p t h d", h=HEADS)

            def max_q(b, k):
                dve.wait_ge(qv_done, b + 1)
                own.inc(dve.reduce_max(qmax[:, k, :].rearrange("p (t h) -> p t h", h=HEADS), q_heads(k), AX.X))

            def sub_q(b, k, v):
                own.wait(v)
                dve.tensor_tensor(q_sb[:, k, :].rearrange("p (t h d) -> p t h d", t=NT, h=HEADS), q_heads(k),
                                  qmax[:, k, :].rearrange("p (t h) -> p t h", h=HEADS).unsqueeze(3)
                                  .broadcast_to([P, NT, HEADS, DH]), ALU.subtract).then_inc(qsub_ready, 1)

            def q_by_head(k):
                return q_sb[:, k, :].rearrange("p (a d) -> p a d", d=DH)

            def sum_q(b, k):
                dve.wait_ge(qexp_ready, b + 1)
                own.inc(dve.reduce_sum(qsum[:, k, :], q_by_head(k), AX.X))

            def one_over_sum(b, k, v):
                own.wait(v)
                own.inc(dve.reciprocal(qrec[:, k, :], qsum[:, k, :]))

            def normed_q(b, k, v):
                own.wait(v)
                dve.tensor_tensor(q_by_head(k), q_by_head(k), qrec[:, k, :].unsqueeze(2)
                                  .broadcast_to([P, NT * HEADS, DH]), ALU.mult).then_inc(qn_ready, 1)

            def k_total(b, k):
                own.inc(dve.tensor_scalar(kstat[:, k, 4:5], kstat[:, k, 2:3], kstat[:, k, 3:4], float(DH) ** 0.5,
                                          ALU.add, ALU.mult))

            def one_over_total(b, k, v):
                own.wait(v)
                own.inc(dve.reciprocal(kstat[:, k, 5:6], kstat[:, k, 4:5]))

            def masked_context(b, k):
                dve.wait_ge(ctx_done, b + 1)
                dve.tensor_tensor(ctm[:, k, :], bank[4 * k + 1][:, P:2 * P], blkmask, ALU.mult).then_inc(ctm_ready, 1)

            def scaled_m(b, k, v):
                own.wait(v)
                dve.wait_ge(m_done, b + 1)
                dve.scalar_tensor_tensor(mx_sb[:, k, :], bank[4 * k + 1][:, 2 * P:2 * P + D2], kstat[:, k, 5:6],
                                         bout_share[:, :], ALU.mult, ALU.add).then_inc(m_ready, 1)

            def moments(b, src_ready, st, mv, done):
                for k in range(2):
                    dve.wait_ge(src_ready, b + (k + 1))
                    alone(dve, "dve")
                    for t in range(NT):
                        v = own.inc(dve.bn_stats(st[:, k, t, :], tiles(at(h1, b + k))[:, t, :]))
                for k in range(2):
                    own.wait(v - NT * (1 - k))
                    alone(dve, "dve")
                    for t in range(NT):
                        last = dve.bn_aggr(mv[:, k, t, :], st[:, k, t, :])
                    last.then_inc(done, 1)

            def scaled_output(b, k):
                dve.wait_ge(r2_ready, b + 1)
                own.inc(dve.tensor_tensor(tiles(t_sb[:, k, :]), tiles(at(h1, b)), per_tile(r2[:, k, :], D2), ALU.mult))

            def gained_output(b, k, v):
                own.wait(v)
                own.inc(dve.tensor_tensor(tiles(t_sb[:, k, :]), tiles(t_sb[:, k, :]), row64(R_GOUT), ALU.mult))

            def add_base(b, k, v):
                dve.wait_ge(res_ready, b + 1)
                own.wait(v)
                dve.tensor_tensor(at(h1, b), t_sb[:, k, :], at(h0, b), ALU.add).then_inc(h1_ready, 1)

            def expert_centred(b, k):
                dve.wait_ge(mv1_ready, b + 1)
                own.inc(dve.tensor_tensor(tiles(t_sb[:, k, :]), tiles(at(h1, b)), per_tile(mv1[:, k, :, 0], D2),
                                          ALU.subtract))

            def expert_z(b, k, v):
                own.wait(v)
                dve.wait_ge(s1_ready, b + 1)
                dve.tensor_tensor(tiles(zf[:, k, :]), tiles(t_sb[:, k, :]), per_tile(s1[:, k, :], D2),
                                  ALU.mult).then_inc(ez_ready, 1)

            def expert_z_lo(b, k):
                dve.wait_ge(ezhi_ready, b + 1)
                alone(dve, "dve")
                st = tiles(zst1[:, bass.ds(b * S, S)], 2 * D2)
                dve.tensor_tensor(st[:, :, D2:2 * D2].bitcast(fp32r), tiles(zf[:, k, :]), st[:, :, 0:D2],
                                  ALU.subtract).then_inc(ezlo_ready, 1)

            def both(step, b):
                for k in range(2):
                    step(b + k, k)

            def both_own(step, b, each=1):
                v = own.base + own.n
                for k in range(2):
                    step(b + k, k, v - each * (1 - k))

            def dve_turn(g, more, before):
                now, nxt, prev = g * 2, g * 2 + 2, g * 2 - 2
                both(sum_q, now)
                both_own(one_over_sum, now)
                both_own(normed_q, now)
                both(k_total, now)
                both_own(one_over_total, now)
                v_total = own.base + own.n
                if more:
                    both(centred, nxt)
                    both_own(z_of, nxt)
                if before and not more:
                    both(expert_centred, prev)
                    both_own(expert_z, prev)
                both(masked_context, now)
                for k in range(2):
                    scaled_m(now + k, k, v_total)
                if more:
                    both(z_lo, nxt)
                if before and more:
                    both(expert_centred, prev)
                    both_own(expert_z, prev)
                moments(now, o_ready, sto, mvo, mvo_ready)
                if before:
                    both(expert_z_lo, prev)
                if more:
                    both(max_k, nxt)
                    both_own(negated, nxt)
                    both(max_q, nxt)
                    v_max = own.base + own.n
                both(scaled_output, now)
                both_own(gained_output, now)
                both_own(add_base, now)
                moments(now, h1_ready, st1, mv1, mv1_ready)
                if more:
                    for k in range(2):
                        sub_q(nxt + k, k, v_max)

            for b in range(B):
                dve.wait_ge(head_done, b + 1)
                dve.tensor_tensor(tiles(h0[:, b, :]), tiles(bank[HEAD_BANK[b % 4]][:, 0:NT * D2]), row64(R_HEADB),
                                  ALU.add).then_inc(h0_ready, 1)
                if b:
                    head_moments(b - 1)
                if b == Z_ROW - 1:
                    qkv_lo()
                if b == Z_ROW:
                    dve.wait_ge(s0_ready, 2)
                    both(centred, 0)
                    both_own(z_of, 0)
                if b == Z_ROW + 1:
                    both(z_lo, 0)
            head_moments(B - 1)
            expert_lo()
            both(max_k, 0)
            both_own(negated, 0)
            both(max_q, 0)
            both_own(sub_q, 0)
            dve.wait_ge(s0_ready, B)
            dve_turn(0, True, False)
            with dve.Fori(1, B // 2 - 1) as g:
                own.enter(g, TURN_OWN, 1)
                dve_turn(g, True, True)
                own.leave(B // 2 - 2)
            dve_turn(B // 2 - 1, False, True)

            def chain(instruction):
                own.wait(own.inc(instruction))

            def each(ap):
                return ap.unsqueeze(2).broadcast_to([P, R // 2, E])

            def top_two(half):
                r = slice(half * R // 2, (half + 1) * R // 2)
                l, e1, o1, e2, o2 = (a[:, r, :] for a in (lg, eq1, oh1, eq2, oh2))
                later = back8.unsqueeze(1).broadcast_to([P, R // 2, E])
                dve.wait_ge(router_done, (half + 1) * HALF)
                parts = bank[LOGITS_BANK[half]][:, 0:R * E].rearrange("p (r c e) -> p r c e", c=2, e=E)
                chain(dve.tensor_tensor(l, parts[:, :, 0, :], br_fold[:, :].unsqueeze(1).broadcast_to([P, R // 2, E]),
                                        ALU.add))
                chain(dve.tensor_tensor(l, l, parts[:, :, 1, :], ALU.add))
                chain(dve.reduce_max(top[:, 0, r], l, AX.X))
                chain(dve.tensor_tensor(e1, l, each(top[:, 0, r]), ALU.is_equal))
                chain(dve.tensor_tensor(e1, e1, later, ALU.mult))
                chain(dve.reduce_max(top[:, 1, r], e1, AX.X))
                chain(dve.tensor_tensor(o1, e1, each(top[:, 1, r]), ALU.is_equal))
                chain(dve.scalar_tensor_tensor(l, o1, -3e38, l, ALU.mult, ALU.add))
                chain(dve.reduce_max(top[:, 2, r], l, AX.X))
                dve.tensor_tensor(top[:, 4, r], top[:, 0, r], top[:, 2, r], ALU.subtract).then_inc(gap_ready, 1)
                chain(dve.tensor_tensor(e2, l, each(top[:, 2, r]), ALU.is_equal))
                chain(dve.tensor_tensor(e2, e2, later, ALU.mult))
                chain(dve.reduce_max(top[:, 3, r], e2, AX.X))
                own.inc(dve.tensor_tensor(o2, e2, each(top[:, 3, r]), ALU.is_equal))

            def weights(half):
                r = slice(half * R // 2, (half + 1) * R // 2)
                o1, o2, w = (a[:, r, :] for a in (oh1, oh2, wgt))
                dve.wait_ge(gate_tanh, half + 1)
                own.inc(dve.tensor_scalar(top[:, 6, r], top[:, 5, r], 0.5, 0.5, ALU.mult, ALU.add))
                chain(dve.tensor_scalar(top[:, 7, r], top[:, 5, r], -0.5, 0.5, ALU.mult, ALU.add))
                own.inc(dve.tensor_tensor(o1, o1, each(top[:, 6, r]), ALU.mult))
                chain(dve.tensor_tensor(o2, o2, each(top[:, 7, r]), ALU.mult))
                chain(dve.tensor_tensor(w, o1, o2, ALU.add))
                for c in range(2):
                    w5 = w32[:, r, c * 2 * E:(c + 1) * 2 * E]
                    v = own.inc(dve.tensor_copy(w5[:, :, 0:E].bitcast(fp32r), w))
                for c in range(2):
                    w5 = w32[:, r, c * 2 * E:(c + 1) * 2 * E]
                    own.wait(v - 1 + c)
                    dve.tensor_tensor(w5[:, :, E:2 * E].bitcast(fp32r), w, w5[:, :, 0:E],
                                      ALU.subtract).then_inc(gates_ready, 1)

            both(expert_centred, B - 2)
            top_two(0)
            both_own(expert_z, B - 2)
            both(expert_z_lo, B - 2)
            weights(0)
            top_two(1)
            weights(1)

            def dve_job(g, m, more):
                n = g * (2 * E) + m
                if m < 2 * E or more:
                    dve.wait_ge(eg_done, n + 1)
                    dve.wait_ge(wb_done, n + 1)
                    dve.tensor_tensor(hw[:, m % NSLOT, :], hg[:, m % NSLOT, :], bank[4 + m % 2],
                                      ALU.mult).then_inc(hw_ready, 1)
                if m >= 1 and (m <= 2 * E or more):
                    slot = (m - 1) % NSLOT
                    dve.wait_ge(hwhi_ready, n)
                    dve.tensor_tensor(hw_lo(slot), hw[:, slot, :], hw_hi[:, slot * S:(slot + 1) * S].bitcast(fp32),
                                      ALU.subtract).then_inc(hwlo_ready, 1)

            def output(g, k):
                b = g * 2 + k
                dve.wait_ge(yt_done, b + 1)
                dve.tensor_tensor(at(h1, b), bank[6 + k][:, 0:NT * D2], at(h1, b), ALU.add).then_inc(out_ready, 1)

            def dve_experts(g, more):
                for m in range(AHEAD, 2 * E + AHEAD):
                    dve_job(g, m, more)
                    if m == E + 4:
                        output(g, 0)
                output(g, 1)

            for m in range(AHEAD):
                dve_job(0, m, True)
            with dve.Fori(0, B // 2 - 1) as g:
                dve_experts(g, True)
            dve_experts(B // 2 - 1, False)

        @block.tensor
        def _(pe):
            def mm(out, lhsT, rhs, start=True, stop=True):
                return pe.matmul(out, lhsT, rhs, start=start, stop=stop)

            pe.wait_ge(ld["cons"], 16)
            pe.wait_ge(ld["emb"], 16)
            pe.transpose(bank[6][:, 0:P], emb2, ident).then_inc(embt_done, 1)
            pe.wait_ge(ld["wupd"], 16)
            pe.wait_ge(embt_copied, 1)
            mm(bank[7][:, 0:P], wupd, embT).then_inc(u_done, 1)
            pe.wait_ge(ld["wf"], 16)
            pe.wait_ge(ld["cols"], 16)
            pe.wait_ge(u_ready, 2)
            mm(bank[4][:, 0:1], centre, cols[:, C_BF:C_BF + 1])
            mm(bank[5][:, 0:P], uT, wf).then_inc(tmem_done, 1)

            def turn(src, ready, count, n):
                pe.wait_ge(ready, count)
                pe.wait_ge(stats_ready, n + FREE)
                for t in range(NT):
                    last = pe.transpose(bank[TB][:, t * P:(t + 1) * P], src[:, t * P:(t + 1) * P], ident)
                last.then_inc(x_t, 1)

            def broadcast(slot, n):
                pe.wait_ge(rstd_ready, n + 1)
                pe.wait_ge(normed, n + FREE)
                for t in range(NT):
                    last = pe.transpose(bank[BB][:, t * P:(t + 1) * P], rstd[:, slot, t:t + 1].broadcast_to([P, P]), ident)
                last.then_inc(rstd_bc, 1)

            def look_up(n):
                row = onehot[:, n * S:(n + 1) * S]
                pe.wait_ge(onehot_ready, n + 1)
                if n >= 2:
                    pe.wait_ge(decay_copied, n - 1)
                mm(bank[n % 2], tab[:, 0, :], row).then_inc(decay_done, 1)
                if n >= 2:
                    pe.wait_ge(scanned, n - 1 + FREE)
                mm(bank[2 + n % 2], tab[:, 1, :], row).then_inc(memory_looked_up, 1)

            def look_up_embedding(n):
                if n >= 1:
                    pe.wait_ge(pre_ready, n)
                mm(bank[4], tab[:, 2, :], onehot[:, n * S:(n + 1) * S]).then_inc(looked_up, 1)

            def bias_fold(l):
                for f in range(F):
                    last = mm(bank[5][:, l * F + f:l * F + f + 1], w1_raw[:, l, f * P:(f + 1) * P],
                              cols[:, C_LNB + l:C_LNB + l + 1])
                if l == L - 1:
                    last.then_inc(folds_done, 1)

            def centre_w1(l):
                pe.wait_ge(w1_scaled, l + 1)
                if l == 0:
                    pe.wait_ge(folds_ready, 1)
                elif l == 3:
                    pe.wait_ge(scanned, B - 1 + FREE)
                else:
                    pe.wait_ge(decay_copied, B - 2 + l)
                mm(bank[W1_BANK[l]], centre, scratch[:, 4 + l, :]).then_inc(w1_centred, 1)

            pe.wait_ge(tables_ready, 1)
            look_up(0)
            look_up_embedding(0)
            for n in range(B + 4):
                if n + 1 < B:
                    look_up(n + 1)
                if n >= 4:
                    broadcast((n - 4) % 4, n - 4)
                if n == B + 1:
                    for i in range(2):
                        turn(x[:, i, :], x0_ready, i + 1, B + i)
                if n >= W1_STEP - L and n < W1_STEP:
                    if n == W1_STEP - L:
                        pe.wait_ge(ld["w1"], 16)
                    bias_fold(n - (W1_STEP - L))
                if n < B:
                    turn(x[:, n, :], pre_ready, n + 1, n)
                if n + 1 < B:
                    look_up_embedding(n + 1)
                if n >= W1_STEP and n - W1_STEP < L:
                    centre_w1(n - W1_STEP)
            broadcast(0, B)
            pe.wait_ge(w1_lo_ready, L)

            def up(j, i):
                pe.wait_ge(xlo_ready, j + 1)
                for f in range(F):
                    if i == 0:
                        pe.wait_ge(w1_loaded[f], l * 16 + 16)
                    else:
                        pe.wait_ge(gelu_done, j * F + (f + 1 - F))
                    hi, lo = w_cur[:, 0, f, 0, :], w_cur[:, 0, f, 1, :]
                    mm(bank[f], hi, xn_hi[:, i % 2, :], stop=False)
                    mm(bank[f], hi, xn_lo[:, i % 2, :], start=False, stop=False)
                    mm(bank[f], lo, xn_hi[:, i % 2, :], start=False).then_inc(mm1_done, 1)

            def down(j, i):
                if i == 0:
                    pe.wait_ge(w2_loaded, l * 16 + 16)
                pe.wait_ge(x_ready, j + (B - 1))
                for f in range(F):
                    if f % 2 == 0:
                        pe.wait_ge(hlo_ready, j * 2 + (f // 2 + 1))
                    hi, lo = w_cur[:, 1, f, 0, :], w_cur[:, 1, f, 1, :]
                    mm(bank[YB + i % 2], hi, hid_hi[:, i % 2, f, :], start=f == 0, stop=False)
                    mm(bank[YB + i % 2], hi, hid_lo[:, i % 2, f, :], start=False, stop=False)
                    last = mm(bank[YB + i % 2], lo, hid_hi[:, i % 2, f, :], start=False, stop=f == F - 1)
                last.then_inc(mm2_done, 1)

            with pe.Fori(0, L) as l:
                for i in range(B):
                    j = l * B + i
                    if i < B - 1:
                        turn(x[:, (i + 2) % B, :], x_ready, j + 3, j + (B + 2))
                        broadcast((i + 1) % 4, j + (B + 1))
                    up(j, i)
                    if i:
                        down(j - 1, i - 1)
                j = l * B + B
                turn(x[:, 1, :], x_ready, j + 2, j + (B + 1))
                broadcast(0, j + B)
                down(j - 1, B - 1)

            for n in ("ew1", "wr"):
                pe.wait_ge(ld[n], 16)
            pe.wait_ge(gelu_done, L * B * F)
            beta = cols[0:D2, C_BETA:C_BETA + 1]
            for e in range(E):
                mm(bank[0][:, e:e + 1], ew1_raw[0:D2, e * P:(e + 1) * P], beta)
            mm(bank[0][:, E:2 * E], beta.broadcast_to([D2, P]), wr_raw[0:D2, :]).then_inc(late_folds_done, 1)

            pe.wait_ge(ld["headw"], 16)
            pe.wait_ge(stats_ready, B * (L + 1) + 2 + FREE)
            pe.wait_ge(normed, B * (L + 1) + 1 + FREE)

            def head(b):
                pe.wait_ge(x_ready, B * L + b + 1)
                if b >= 4:
                    pe.wait_ge(h0_ready, b - 3)
                for t in range(NT):
                    last = mm(bank[HEAD_BANK[b % 4]][:, t * D2:(t + 1) * D2], x[:, b, t * P:(t + 1) * P], headw[:, :])
                last.then_inc(head_done, 1)

            for n in ("wout", "memv"):
                pe.wait_ge(ld[n], 16)

            def turn_z(src, dst):
                for t in range(NT):
                    last = pe.transpose(dst[:, t * P:(t + 1) * P], src[:, t * P:(t + 1) * P], ident)
                return last

            def z_transposes(b, k):
                pe.wait_ge(zlo_ready, b + 1)
                turn_z(zst[:, k, :], bank[4 * k]).then_inc(z_t, 1)

            def qkv(b, k):
                kb = bank[4 * k + 1]
                pe.wait_ge(zt_ready, b + 1)
                mm(kb, wqkv[:, 0, P:2 * P], zt[:, k, :], stop=False)
                mm(kb, wqkv[:, 1, P:2 * P], zt[:, k, :], start=False).then_inc(k_done, 1)
                qv = qv_view(k)
                for t in range(NT):
                    for h in range(2):
                        w = wqkv[:, h, :].rearrange("p (c n) -> p c n", c=3)[:, 0:3:2, :]
                        last = mm(qv[:, t, :, :], zt[:, k, t * P:(t + 1) * P], w, start=h == 0, stop=h == 1)
                last.then_inc(qv_done, 1)

            def k_transposes(b, k):
                pe.wait_ge(kexp_ready, b + 1)
                for t in range(NT):
                    pe.transpose(bank[4 * k][:, t * P:(t + 1) * P], kexp[:, k, t * P:(t + 1) * P], ident)
                pe.transpose(bank[4 * k + 1][0:NMEM, 0:P], kexp[:, k, S:S + NMEM], ident).then_inc(k_t, 1)

            def context(b, k):
                pe.wait_ge(kt_ready, b + 1)
                pe.wait_ge(v_ready, b + 1)
                cb = bank[4 * k + 1][:, P:2 * P]
                for t in range(NT):
                    mm(cb, v_sb[:, k, t * P:(t + 1) * P], kT[:, k, t * P:(t + 1) * P], start=t == 0, stop=False)
                mm(cb, memv[:, :], memT[0:NMEM, k, :], start=False).then_inc(ctx_done, 1)

            def q_transposes(b, k):
                pe.wait_ge(qn_ready, b + 1)
                for t in range(NT):
                    last = pe.transpose(bank[4 * k][:, t * P:(t + 1) * P], q_sb[:, k, t * P:(t + 1) * P], ident)
                last.then_inc(q_t, 1)

            def projected_context(b, k):
                pe.wait_ge(ctm_ready, b + 1)
                mm(bank[4 * k + 1][:, 2 * P:2 * P + D2], ctm[:, k, :], wout[:, :]).then_inc(m_done, 1)

            def attend(b, k):
                pe.wait_ge(m_ready, b + 1)
                pe.wait_ge(qt_ready, b + 1)
                for t in range(NT):
                    last = mm(bank[4 * k + 1][:, 2 * P + t * D2:2 * P + (t + 1) * D2], qT[:, k, t * P:(t + 1) * P],
                              mx_sb[:, k, :])
                last.then_inc(o_done, 1)

            def pe_turn(g):
                for step in (context, q_transposes, projected_context, attend):
                    for k in range(2):
                        step(g * 2 + k, k)
                for k in range(2):
                    z_transposes(g * 2 + (k + 2), k)
                for k in range(2):
                    pe.wait_ge(o_ready, g * 2 + (k + 1))
                    qkv(g * 2 + (k + 2), k)
                for k in range(2):
                    k_transposes(g * 2 + (k + 2), k)

            def expert_z_transposes(b):
                pe.wait_ge(ezlo_ready, b + 1)
                if b >= 2:
                    pe.wait_ge(eza_ready, b - 1)
                turn_z(zst1[:, b * S:(b + 1) * S], bank[2 + b % 2]).then_inc(ez_t, 1)

            def route(b):
                pe.wait_ge(eza_ready, b + 1)
                if b >= 2:
                    pe.wait_ge(lt_copied, b - 1)
                mm(bank[6 + b % 2][0:2 * E, :], wr[:, :, :].rearrange("p h e -> p (h e)"),
                   z_all[:, b * S:(b + 1) * S]).then_inc(lt_done, 1)

            def logits(b):
                pe.wait_ge(lt_copied, b + 1)
                for t in range(NT):
                    r = (b % HALF) * NT + t
                    last = pe.transpose(bank[LOGITS_BANK[b // HALF]][:, r * 2 * E:(r + 1) * 2 * E],
                                        lt_sb[0:2 * E, b % 2, t * P:(t + 1) * P], ident[0:2 * E, 0:2 * E])
                last.then_inc(router_done, 1)

            def router(first, end):
                for b in range(first, end, 2):
                    for step in (expert_z_transposes, route, logits):
                        step(b)
                        step(b + 1)

            def last_turn():
                def pair(step):
                    for k in range(2):
                        step(B - 2 + k, k)
                pair(context)
                pair(q_transposes)
                pair(projected_context)
                expert_z_transposes(0)
                expert_z_transposes(1)
                pair(attend)
                pe.wait_ge(late_weights, 1)
                route(0)
                route(1)
                expert_z_transposes(2)
                expert_z_transposes(3)
                logits(0)
                logits(1)
                for b in (2, 3):
                    route(b)
                for b in (2, 3):
                    logits(b)
                pe.wait_ge(o_ready, B)

            for b in range(B):
                head(b)
            z_transposes(0, 0)
            z_transposes(1, 1)
            pe.wait_ge(wqkv_ready, 1)
            pe.wait_ge(h0_ready, B)
            for k in range(2):
                qkv(k, k)
            for k in range(2):
                k_transposes(k, k)
            with pe.Fori(0, B // 2 - 1) as g:
                pe_turn(g)
            last_turn()
            router(HALF, B)

            def turn_gates(b):
                pe.wait_ge(gates_ready, 2 * (b // HALF) + 2)
                before = [r for r in range(b) if GATES_BANK[r] == GATES_BANK[b]]
                if before:
                    pe.wait_ge(gates_copied, before[-1] + 1)
                for t in range(NT):
                    last = pe.transpose(bank[GATES_BANK[b]][0:4 * E, t * P:(t + 1) * P], w32[:, b * NT + t, :], ident)
                last.then_inc(gates_t, 1)

            def first_products(g, m):
                hidden(g, m)
                spread_gates(g, m)
                if m % E == 0:
                    bias_sum(g, m)

            def hidden(g, m):
                n, e = g * (2 * E) + m, m % E
                z_b = z_all[:, bass.ds(g * (2 * S) + m // E * S, S)]
                if m >= 4:
                    pe.wait_ge(eg_done, n - 3)
                mm(bank[m % 4], ew1[:, 0, e * P:(e + 1) * P], z_b, stop=False)
                mm(bank[m % 4], ew1[:, 1, e * P:(e + 1) * P], z_b, start=False).then_inc(e1_done, 1)

            def spread_gates(g, m):
                n, e = g * (2 * E) + m, m % E
                if m >= 2:
                    pe.wait_ge(hw_ready, n - 1)
                    alone(pe, "pe")
                mm(bank[4 + m % 2], sel[:, e:e + 1].broadcast_to([4 * E, P]),
                   wT_all[:, bass.ds(g * (2 * S) + m // E * S, S)]).then_inc(wb_done, 1)

            def bias_sum(g, m):
                if m:
                    pe.wait_ge(out_ready, g * 2 + (m // E - 1 + FREE))
                    alone(pe, "pe")
                mm(bank[6 + m // E % 2], eb2[:, :], wT_all[:, bass.ds(g * (2 * S) + m // E * S, S)], stop=False)

            def second_products(g, m):
                n = g * (2 * E) + m
                k, e, slot = m // E % 2, m % E, m % NSLOT
                w = ew2[:, e, :, :].rearrange("p h n -> p (h n)")
                pe.wait_ge(hwlo_ready, n + 1)
                mm(bank[6 + k], w, hw_hi[:, slot * S:(slot + 1) * S], start=False, stop=False)
                last = mm(bank[6 + k], w, hw_lo(slot), start=False, stop=e == E - 1)
                if e == E - 1:
                    last.then_inc(y_done, 1)

            def turn_sum(g, k):
                pe.wait_ge(y_copied, g * 2 + (k + 1))
                for t in range(NT):
                    last = mm(bank[6 + k][:, t * D2:(t + 1) * D2], y_sb[:, k, t * P:(t + 1) * P], stack2)
                last.then_inc(yt_done, 1)

            def pe_experts(g, more):
                for m in range(AHEAD, 2 * E + AHEAD):
                    if m == E:
                        pe.wait_ge(gates_copied, B)
                    if m < 2 * E or more:
                        first_products(g, m)
                    if m - SKEW < 2 * E or more:
                        second_products(g, m - SKEW)
                    if m == E + 4:
                        turn_sum(g, 0)
                    if m == 2 * E + 4:
                        turn_sum(g, 1)

            for b in range(HALF):
                turn_gates(b)
            for m in range(4):
                hidden(0, m)
            pe.wait_ge(gates_copied, HALF)
            spread_gates(0, 0)
            bias_sum(0, 0)
            pe.wait_ge(gates_ready, 4)
            spread_gates(0, 1)
            hidden(0, 4)
            spread_gates(0, 2)
            turn_gates(HALF)
            spread_gates(0, 3)
            second_products(0, 0)
            turn_gates(HALF + 1)
            spread_gates(0, 4)
            second_products(0, 1)
            turn_gates(HALF + 2)
            turn_gates(HALF + 3)
            with pe.Fori(0, B // 2 - 1) as g:
                pe_experts(g, True)
            pe_experts(B // 2 - 1, False)


def kernel(**inputs):
    import numpy as np
    import concourse.bacc as bacc
    from concourse.bass_utils import run_bass_kernel_spmd

    a = {n: np.asarray(t) for n, t in inputs.items()}
    tok = {n[7:]: t for n, t in a.items() if n.startswith("L0_tok_")}
    att = {n[8:]: t for n, t in a.items() if n.startswith("L0_attn_")}
    ffn = {n[7:]: t for n, t in a.items() if n.startswith("L0_ffn_")}

    def twice(t):
        return np.concatenate([t, t], axis=0)

    cols = np.concatenate([
        tok["b_upd"][:, None], tok["b_f"][:, None], tok["norm_g"][:, None], tok["norm_b"][:, None],
        tok["cms_ln_g"].T, tok["cms_ln_b"].T, tok["cms_b2"].T,
        tok["cms_b1"].reshape(L * F, P).T,
        twice(att["g_pre"][:, None]), twice(ffn["gamma"][:, None]), twice(ffn["beta"][:, None]),
        ffn["b1"].T, att["mem_kv"][0].reshape(P, NMEM)], axis=1)
    rows = np.concatenate([tok["head_b"], att["b_out"], att["g_out"], ffn["br"], tok["decay_param"]])

    cons = np.zeros((P, NCON), np.float32)
    lane = np.arange(P)
    cons[:, K_ID:K_ID + P] = np.eye(P)
    cons[:, K_CEN:K_CEN + P] = np.eye(P) - 1.0 / P
    cons[:, K_BLK:K_BLK + P] = lane[:, None] // DH == lane[None, :] // DH
    cons[:, K_II:K_II + D2] = lane[:, None] % D2 == np.arange(D2)
    cons[:, K_BACK8:K_BACK8 + E] = E - np.arange(E)
    cons[:, K_VOC] = lane % V
    cons[:2 * E, K_SEL:K_SEL + E] = lane[:2 * E, None] % E == np.arange(E)
    cons[2 * E:4 * E, K_HALF] = 1.0

    arrays = {
        "tokens": a["x"].reshape(B * S),
        "emb": twice(tok["emb"]),
        "w_upd": tok["W_upd"],
        "w_f": tok["W_f"],
        "w1": tok["cms_W1"].transpose(1, 0, 2).reshape(P, L * F * P),
        "w2": tok["cms_W2"].reshape(L, F, P, D).transpose(2, 0, 1, 3).reshape(P, L * F * D),
        "head_w": tok["head_W"],
        "cols": cols,
        "rows": rows,
        "constants": cons,
        "w_qkv": twice(att["w_qkv"]),
        "w_out": att["w_out"],
        "mem_v": att["mem_kv"][1].reshape(P, NMEM).T,
        "w_r": twice(ffn["Wr"]),
        "expert_w1": twice(ffn["W1"].transpose(1, 0, 2).reshape(D2, E * P)),
        "expert_w2": ffn["W2"].transpose(1, 0, 2).reshape(P, E * D2),
        "expert_b2": np.concatenate([ffn["b2"]] * 4, axis=0),
    }
    arrays = {n: np.ascontiguousarray(t) for n, t in arrays.items()}
    nc = bacc.Bacc("TRN2", target_bir_lowering=False, num_devices=1)
    args = [nc.dram_tensor("in_" + n, t.shape, mybir.dt.from_np(t.dtype), kind="ExternalInput").ap()
            for n, t in arrays.items()]
    out = nc.dram_tensor("out", (B, S, D2), fp32, kind="ExternalOutput").ap()
    build(nc, *args, out)
    r = run_bass_kernel_spmd(nc, [{"in_" + n: t for n, t in arrays.items()}], core_ids=[0])
    return r.results[0]["out"]
```
